# Optimizing a Trainium2 kernel written in Bass

```python
import numpy as np
import jax
import jax.numpy as jnp

def _softmax(x, axis=-1):
    return jax.nn.softmax(x, axis=axis)

def _gelu(x):
    return jax.nn.gelu(x, approximate=True)

def _silu(x):
    return jax.nn.silu(x)

def _sigmoid(x):
    return jax.nn.sigmoid(x)

def _layernorm(x, axis=-1, eps=1e-05):
    m = jnp.mean(x, axis=axis, keepdims=True)
    v = jnp.var(x, axis=axis, keepdims=True)
    return (x - m) / jnp.sqrt(v + eps)

def _scatter_add(tgt, idx, src, axis=0):
    return tgt.at[idx].add(src)

def _segment_sum(src, seg, n):
    return jax.ops.segment_sum(src, seg, n)
kernel_name = 'mk_xattn_ffn_d2_seqx_r8_ea6d0d'

def setup_inputs(seed: int=0):
    np.random.seed(seed)
    _w = jnp.asarray

    def _rec_inputs():
        import jax
        import jax.numpy as jnp
        _rk = jax.random.key(seed)
        x = 7.22e-05 + 1 * jax.random.normal(jax.random.fold_in(_rk, 1), (128, 64, 128), jnp.float32)
        _lenS = 64 - jax.random.randint(jax.random.fold_in(_rk, 7), (128,), 0, max(1, 64 // 4) + 1, jnp.int32)
        _lenS2 = 64 - jax.random.randint(jax.random.fold_in(_rk, 8), (128,), 0, max(1, 64 // 4) + 1, jnp.int32)
        _ctx_1024P = jax.random.normal(jax.random.fold_in(_rk, 11), (128, 16, 128), jnp.float32)
        _ctx_1024c = jax.random.dirichlet(jax.random.fold_in(_rk, 511), 0.3 * jnp.ones((16,), jnp.float32), (128, 64))
        _ctx_1024t = jnp.einsum('bsk,bkd->bsd', _ctx_1024c, _ctx_1024P)
        _ctx_1024t = _ctx_1024t * jax.lax.rsqrt(jnp.mean(jnp.square(_ctx_1024t)) + 1e-12) * 0.953939
        ctx_1024 = 4.13588e-05 + 0.999923 * (_ctx_1024t + 0.3 * jax.random.normal(jax.random.fold_in(_rk, 611), (128, 64, 128), jnp.float32))
        return (x, ctx_1024)
    x, ctx_1024 = _rec_inputs()

    def _L0_xattn_setup():
        import math
        import jax, jax.numpy as jnp
        import numpy as np
        NUM_BUCKETS = 32
        MAX_DISTANCE = 128
        NUM_HEADS = 16

        def _relative_position_bucket_bidirectional(relative_position):
            nb = NUM_BUCKETS // 2
            buckets = (relative_position > 0).astype(jnp.int32) * nb
            rp = jnp.abs(relative_position)
            max_exact = nb // 2
            is_small = rp < max_exact
            rp_safe = jnp.maximum(rp, 1)
            large = max_exact + (jnp.log(rp_safe.astype(jnp.float32) / max_exact) / math.log(MAX_DISTANCE / max_exact) * (nb - max_exact)).astype(jnp.int32)
            large = jnp.minimum(large, nb - 1)
            return buckets + jnp.where(is_small, rp, large)

        def compute_bias(rel_bias, tgt_len, src_len):
            ctx = jnp.arange(tgt_len)[:, None]
            mem = jnp.arange(src_len)[None, :]
            buckets = _relative_position_bucket_bidirectional(mem - ctx)
            values = rel_bias[buckets]
            return jnp.transpose(values, (2, 0, 1))[None]
        key = jax.random.key(seed)
        ks = jax.random.split(key, 7)
        B, S, D = (4, 256, 128)
        s = 1.0 / math.sqrt(D)
        return {'query_states': jax.random.normal(ks[0], (B, S, D), jnp.float32), 'key_value_states': jax.random.normal(ks[1], (B, S, D), jnp.float32), 'wq': jax.random.normal(ks[2], (D, D), jnp.float32) * s, 'wk': jax.random.normal(ks[3], (D, D), jnp.float32) * s, 'wv': jax.random.normal(ks[4], (D, D), jnp.float32) * s, 'wo': jax.random.normal(ks[5], (D, D), jnp.float32) * s, 'rel_bias': jax.random.normal(ks[6], (NUM_BUCKETS, NUM_HEADS), jnp.float32)}
    _L0_xattn_all = _L0_xattn_setup()
    _L0_xattn_in = {k: v for k, v in _L0_xattn_all.items() if k in ('wq', 'wk', 'wv', 'wo', 'rel_bias')}
    del _L0_xattn_all

    def _L0_ffn_setup():
        import jax, jax.numpy as jnp
        import numpy as np
        S, B, D = (128, 2, 128)
        E, TOPK = (15, 3)
        F = 128
        FS = 256

        def _uinit(k, shape, out_dim):
            std = out_dim ** (-0.5)
            return jax.random.uniform(k, shape, jnp.float32, -std, std)
        key = jax.random.key(seed)
        ks = jax.random.split(key, 10)
        return {'x': jax.random.normal(ks[0], (S, B, D), jnp.float32), 'gate_w': jax.random.normal(ks[1], (E, D), jnp.float32) * D ** (-0.5), 'fc1_w': _uinit(ks[2], (E, 2 * F, D), 2 * F), 'fc1_b': _uinit(ks[3], (E, 2 * F), 2 * F), 'geglu_mult': jnp.ones((E, F), jnp.float32), 'fc2_w': _uinit(ks[4], (E, D, F), D), 'fc2_b': _uinit(ks[5], (E, D), D), 's_fc1_w': _uinit(ks[6], (2 * FS, D), 2 * FS), 's_fc1_b': _uinit(ks[7], (2 * FS,), 2 * FS), 's_geglu_mult': jnp.ones((FS,), jnp.float32), 's_fc2_w': _uinit(ks[8], (D, FS), D), 's_fc2_b': _uinit(ks[9], (D,), D)}
    _L0_ffn_all = _L0_ffn_setup()
    _L0_ffn_in = {k: v for k, v in _L0_ffn_all.items() if k in ('gate_w', 'fc1_w', 'fc1_b', 'geglu_mult', 'fc2_w', 'fc2_b', 's_fc1_w', 's_fc1_b', 's_geglu_mult', 's_fc2_w', 's_fc2_b')}
    del _L0_ffn_all

    def _L1_xattn_setup():
        import jax, jax.numpy as jnp
        import numpy as np
        EMBED = 128
        HEADS = 16
        HEAD_DIM = EMBED // HEADS
        key = jax.random.key(seed)
        ks = jax.random.split(key, 10)
        B, SQ, SK = (2, 256, 256)
        s = 0.02
        return {'decoder_hidden_state': jax.random.normal(ks[0], (B, SQ, EMBED), jnp.float32), 'encoder_hidden_state': jax.random.normal(ks[1], (B, SK, EMBED), jnp.float32), 'wq': jax.random.normal(ks[2], (HEADS, EMBED, HEAD_DIM), jnp.float32) * s, 'bq': jax.random.normal(ks[3], (HEADS, HEAD_DIM), jnp.float32) * s, 'wk': jax.random.normal(ks[4], (HEADS, EMBED, HEAD_DIM), jnp.float32) * s, 'bk': jax.random.normal(ks[5], (HEADS, HEAD_DIM), jnp.float32) * s, 'wv': jax.random.normal(ks[6], (HEADS, EMBED, HEAD_DIM), jnp.float32) * s, 'bv': jax.random.normal(ks[7], (HEADS, HEAD_DIM), jnp.float32) * s, 'wo': jax.random.normal(ks[8], (EMBED, EMBED), jnp.float32) * s, 'bo': jax.random.normal(ks[9], (EMBED,), jnp.float32) * s}
    _L1_xattn_all = _L1_xattn_setup()
    _L1_xattn_in = {k: v for k, v in _L1_xattn_all.items() if k in ('wq', 'bq', 'wk', 'bk', 'wv', 'bv', 'wo', 'bo')}
    del _L1_xattn_all

    def _L1_ffn_setup():
        import jax, jax.numpy as jnp
        import numpy as np
        HIDDEN = 128
        MOE_FF = 64
        SHARED_FF = 352
        NUM_EXPERTS = 16
        TOP_K = 2
        NORM_TOPK = True
        key = jax.random.key(seed)
        ks = jax.random.split(key, 8)
        s = 0.02
        return {'layer_input': jax.random.normal(ks[0], (1, 256, HIDDEN), dtype=jnp.float32), 'gate_w': jax.random.normal(ks[1], (NUM_EXPERTS, HIDDEN), dtype=jnp.float32) * s, 'w_gate_up': jax.random.normal(ks[2], (NUM_EXPERTS, HIDDEN, 2 * MOE_FF), dtype=jnp.float32) * s, 'w_down': jax.random.normal(ks[3], (NUM_EXPERTS, MOE_FF, HIDDEN), dtype=jnp.float32) * s, 'shared_w_gate': jax.random.normal(ks[4], (SHARED_FF, HIDDEN), dtype=jnp.float32) * s, 'shared_w_up': jax.random.normal(ks[5], (SHARED_FF, HIDDEN), dtype=jnp.float32) * s, 'shared_w_down': jax.random.normal(ks[6], (HIDDEN, SHARED_FF), dtype=jnp.float32) * s, 'shared_gate_w': jax.random.normal(ks[7], (1, HIDDEN), dtype=jnp.float32) * s}
    _L1_ffn_all = _L1_ffn_setup()
    _L1_ffn_in = {k: v for k, v in _L1_ffn_all.items() if k in ('gate_w', 'w_gate_up', 'w_down', 'shared_w_gate', 'shared_w_up', 'shared_w_down', 'shared_gate_w')}
    del _L1_ffn_all
    return {'x': x, 'ctx_1024': ctx_1024, 'L0_xattn_wq': _L0_xattn_in['wq'], 'L0_xattn_wk': _L0_xattn_in['wk'], 'L0_xattn_wv': _L0_xattn_in['wv'], 'L0_xattn_wo': _L0_xattn_in['wo'], 'L0_xattn_rel_bias': _L0_xattn_in['rel_bias'], 'L0_ffn_gate_w': _L0_ffn_in['gate_w'], 'L0_ffn_fc1_w': _L0_ffn_in['fc1_w'], 'L0_ffn_fc1_b': _L0_ffn_in['fc1_b'], 'L0_ffn_geglu_mult': _L0_ffn_in['geglu_mult'], 'L0_ffn_fc2_w': _L0_ffn_in['fc2_w'], 'L0_ffn_fc2_b': _L0_ffn_in['fc2_b'], 'L0_ffn_s_fc1_w': _L0_ffn_in['s_fc1_w'], 'L0_ffn_s_fc1_b': _L0_ffn_in['s_fc1_b'], 'L0_ffn_s_geglu_mult': _L0_ffn_in['s_geglu_mult'], 'L0_ffn_s_fc2_w': _L0_ffn_in['s_fc2_w'], 'L0_ffn_s_fc2_b': _L0_ffn_in['s_fc2_b'], 'L1_xattn_wq': _L1_xattn_in['wq'], 'L1_xattn_bq': _L1_xattn_in['bq'], 'L1_xattn_wk': _L1_xattn_in['wk'], 'L1_xattn_bk': _L1_xattn_in['bk'], 'L1_xattn_wv': _L1_xattn_in['wv'], 'L1_xattn_bv': _L1_xattn_in['bv'], 'L1_xattn_wo': _L1_xattn_in['wo'], 'L1_xattn_bo': _L1_xattn_in['bo'], 'L1_ffn_gate_w': _L1_ffn_in['gate_w'], 'L1_ffn_w_gate_up': _L1_ffn_in['w_gate_up'], 'L1_ffn_w_down': _L1_ffn_in['w_down'], 'L1_ffn_shared_w_gate': _L1_ffn_in['shared_w_gate'], 'L1_ffn_shared_w_up': _L1_ffn_in['shared_w_up'], 'L1_ffn_shared_w_down': _L1_ffn_in['shared_w_down'], 'L1_ffn_shared_gate_w': _L1_ffn_in['shared_gate_w']}

def reference(x, ctx_1024, L0_xattn_wq, L0_xattn_wk, L0_xattn_wv, L0_xattn_wo, L0_xattn_rel_bias, L0_ffn_gate_w, L0_ffn_fc1_w, L0_ffn_fc1_b, L0_ffn_geglu_mult, L0_ffn_fc2_w, L0_ffn_fc2_b, L0_ffn_s_fc1_w, L0_ffn_s_fc1_b, L0_ffn_s_geglu_mult, L0_ffn_s_fc2_w, L0_ffn_s_fc2_b, L1_xattn_wq, L1_xattn_bq, L1_xattn_wk, L1_xattn_bk, L1_xattn_wv, L1_xattn_bv, L1_xattn_wo, L1_xattn_bo, L1_ffn_gate_w, L1_ffn_w_gate_up, L1_ffn_w_down, L1_ffn_shared_w_gate, L1_ffn_shared_w_up, L1_ffn_shared_w_down, L1_ffn_shared_gate_w):
    import jax
    import jax.numpy as jnp

    def _L0_xattn_ref(query_states, key_value_states, wq, wk, wv, wo, rel_bias):
        import math
        import jax, jax.numpy as jnp
        import numpy as np
        NUM_BUCKETS = 32
        MAX_DISTANCE = 128
        NUM_HEADS = 16

        def _relative_position_bucket_bidirectional(relative_position):
            nb = NUM_BUCKETS // 2
            buckets = (relative_position > 0).astype(jnp.int32) * nb
            rp = jnp.abs(relative_position)
            max_exact = nb // 2
            is_small = rp < max_exact
            rp_safe = jnp.maximum(rp, 1)
            large = max_exact + (jnp.log(rp_safe.astype(jnp.float32) / max_exact) / math.log(MAX_DISTANCE / max_exact) * (nb - max_exact)).astype(jnp.int32)
            large = jnp.minimum(large, nb - 1)
            return buckets + jnp.where(is_small, rp, large)

        def compute_bias(rel_bias, tgt_len, src_len):
            ctx = jnp.arange(tgt_len)[:, None]
            mem = jnp.arange(src_len)[None, :]
            buckets = _relative_position_bucket_bidirectional(mem - ctx)
            values = rel_bias[buckets]
            return jnp.transpose(values, (2, 0, 1))[None]
        B, T, D = query_states.shape
        S = key_value_states.shape[1]
        H = NUM_HEADS
        dh = D // H

        def shape(x, L):
            return jnp.transpose(x.reshape(B, L, H, dh), (0, 2, 1, 3))
        q = shape(query_states @ wq, T)
        k = shape(key_value_states @ wk, S)
        v = shape(key_value_states @ wv, S)
        bias = compute_bias(rel_bias, T, S)
        scores = jnp.einsum('bhtd,bhsd->bhts', q, k) + bias
        weights = jax.nn.softmax(scores, axis=-1)
        attn = jnp.einsum('bhts,bhsd->bhtd', weights, v)
        attn = jnp.transpose(attn, (0, 2, 1, 3)).reshape(B, T, D)
        return attn @ wo

    def _L0_ffn_ref(x, gate_w, fc1_w, fc1_b, geglu_mult, fc2_w, fc2_b, s_fc1_w, s_fc1_b, s_geglu_mult, s_fc2_w, s_fc2_b):
        import jax, jax.numpy as jnp
        import numpy as np
        S, B, D = (128, 2, 128)
        E, TOPK = (15, 3)
        F = 128
        FS = 256

        def _uinit(k, shape, out_dim):
            std = out_dim ** (-0.5)
            return jax.random.uniform(k, shape, jnp.float32, -std, std)
        s, b, d = x.shape
        xt = x.reshape(-1, d)
        T = xt.shape[0]
        logits = xt @ gate_w.T
        scores = jax.nn.softmax(logits, axis=-1)
        topk_w, topk_idx = jax.lax.top_k(scores, TOPK)
        topk_w = topk_w / (jnp.sum(topk_w, axis=-1, keepdims=True) + 1e-20)
        comb = jnp.zeros((T, E), xt.dtype).at[jnp.arange(T)[:, None], topk_idx].add(topk_w)
        h = jnp.einsum('td,efd->etf', xt, fc1_w) + fc1_b[:, None, :]
        xh, g = (h[..., :F], h[..., F:])
        a = jax.nn.gelu(g, approximate=False) * xh * geglu_mult[:, None, :]
        yexp = jnp.einsum('etf,edf->etd', a, fc2_w) + fc2_b[:, None, :]
        y = jnp.einsum('etd,te->td', yexp, comb)
        hs = xt @ s_fc1_w.T + s_fc1_b
        xs, gs = (hs[..., :FS], hs[..., FS:])
        as_ = jax.nn.gelu(gs, approximate=False) * xs * s_geglu_mult
        ys = as_ @ s_fc2_w.T + s_fc2_b
        return (y + ys).reshape(s, b, d)

    def _L1_xattn_ref(decoder_hidden_state, encoder_hidden_state, wq, bq, wk, bk, wv, bv, wo, bo):
        import jax, jax.numpy as jnp
        import numpy as np
        EMBED = 128
        HEADS = 16
        HEAD_DIM = EMBED // HEADS
        q = jnp.einsum('bqe,hed->bhqd', decoder_hidden_state, wq) + bq[None, :, None, :]
        k = jnp.einsum('bke,hed->bhkd', encoder_hidden_state, wk) + bk[None, :, None, :]
        v = jnp.einsum('bke,hed->bhkd', encoder_hidden_state, wv) + bv[None, :, None, :]
        scale = 1.0 / jnp.sqrt(jnp.asarray(HEAD_DIM, q.dtype))
        scores = jnp.einsum('bhqd,bhkd->bhqk', q, k) * scale
        attn = jax.nn.softmax(scores, axis=-1)
        ctx = jnp.einsum('bhqk,bhkd->bhqd', attn, v)
        B, H, SQ, D = ctx.shape
        ctx = jnp.transpose(ctx, (0, 2, 1, 3)).reshape(B, SQ, H * D)
        return ctx @ wo + bo

    def _L1_ffn_ref(layer_input, gate_w, w_gate_up, w_down, shared_w_gate, shared_w_up, shared_w_down, shared_gate_w):
        import jax, jax.numpy as jnp
        import numpy as np
        HIDDEN = 128
        MOE_FF = 64
        SHARED_FF = 352
        NUM_EXPERTS = 16
        TOP_K = 2
        NORM_TOPK = True
        B, S, D = layer_input.shape
        x = layer_input.reshape(-1, D)
        N = x.shape[0]
        shared = jax.nn.silu(x @ shared_w_gate.T) * (x @ shared_w_up.T) @ shared_w_down.T
        shared = shared * jax.nn.sigmoid(x @ shared_gate_w.T)
        logits = x @ gate_w.T
        probs = jax.nn.softmax(logits.astype(jnp.float32), axis=-1)
        rw, sel = jax.lax.top_k(probs, TOP_K)
        if NORM_TOPK:
            rw = rw / rw.sum(axis=-1, keepdims=True)
        rw = rw.astype(x.dtype)
        combine = jnp.zeros((N, NUM_EXPERTS), x.dtype).at[jnp.arange(N)[:, None], sel].set(rw)
        gu = jnp.einsum('nd,edf->nef', x, w_gate_up)
        g, h = jnp.split(gu, 2, axis=-1)
        h = jax.nn.silu(g) * h
        expert_out = jnp.einsum('nef,efd,ne->nd', h, w_down, combine)
        out = expert_out + shared
        return out.reshape(B, S, D)
    x = x + _L0_xattn_ref(_layernorm(x, axis=-1), ctx_1024, L0_xattn_wq, L0_xattn_wk, L0_xattn_wv, L0_xattn_wo, L0_xattn_rel_bias)
    x = x + _L0_ffn_ref(_layernorm(x, axis=-1), L0_ffn_gate_w, L0_ffn_fc1_w, L0_ffn_fc1_b, L0_ffn_geglu_mult, L0_ffn_fc2_w, L0_ffn_fc2_b, L0_ffn_s_fc1_w, L0_ffn_s_fc1_b, L0_ffn_s_geglu_mult, L0_ffn_s_fc2_w, L0_ffn_s_fc2_b)
    x = x + _L1_xattn_ref(_layernorm(x, axis=-1), ctx_1024, L1_xattn_wq, L1_xattn_bq, L1_xattn_wk, L1_xattn_bk, L1_xattn_wv, L1_xattn_bv, L1_xattn_wo, L1_xattn_bo)
    x = x + _L1_ffn_ref(_layernorm(x, axis=-1), L1_ffn_gate_w, L1_ffn_w_gate_up, L1_ffn_w_down, L1_ffn_shared_w_gate, L1_ffn_shared_w_up, L1_ffn_shared_w_down, L1_ffn_shared_gate_w)
    return x

_drawn_inputs = setup_inputs


def setup_inputs(seed=0):
    import zlib

    import numpy as np

    out = dict(_drawn_inputs(seed))
    spreads = {'L0_ffn_geglu_mult': (1.0, 0.6), 'L0_ffn_s_geglu_mult': (1.0, 0.6)}
    factors = {'L0_ffn_fc1_b': 8.0,
     'L0_ffn_s_fc1_b': 8.0,
     'L1_xattn_wq': 8.0,
     'L1_xattn_bq': 8.0,
     'L1_xattn_wk': 8.0,
     'L1_xattn_bk': 8.0,
     'L1_xattn_wv': 2.769,
     'L1_xattn_bv': 8.0,
     'L1_xattn_wo': 2.774,
     'L1_xattn_bo': 3.253,
     'L1_ffn_gate_w': 8.0,
     'L1_ffn_w_gate_up': 8.0,
     'L1_ffn_w_down': 8.0,
     'L1_ffn_shared_w_gate': 8.0,
     'L1_ffn_shared_w_up': 8.0,
     'L1_ffn_shared_w_down': 8.0,
     'L1_ffn_shared_gate_w': 8.0}
    for name, (base, spread) in spreads.items():
        noise = np.random.default_rng([zlib.crc32(name.encode()), seed]).standard_normal(out[name].shape)
        drawn = base * np.exp(spread * noise) if base else spread * noise
        out[name] = jnp.asarray(drawn.astype(out[name].dtype))
    for name, factor in factors.items():
        out[name] = (out[name] * factor).astype(out[name].dtype)
    return out
```

```python
import math
from contextlib import ExitStack

import numpy as np

import concourse.bass as bass
from concourse import mybir

ALU = mybir.AluOpType
ACT = mybir.ActivationFunctionType
AX = mybir.AxisListType
F32 = mybir.dt.float32
F32R = mybir.dt.float32r
U32 = mybir.dt.uint32

P = 128
B, S, D = 128, 64, 128
H, DH = 16, 8
HQ, HJ = 4, 4
NC = 4
TOK = B * S
TILES = TOK // P
HP = H // 2
AT = 2
AN = AT * P
AG = TILES // AT
FT = 4
FN = FT * P
FG = TILES // FT
NE = 16
ROWS = 64
EPS = 1e-5
NB = (17, 11)
NCOMB = (15, 11)
TOPK = (3, 2)
LOGITS = (15, 17)
EXPERTS = (15, 16)
NBUCKET = 32


def add(k, n):
    return k + n if n else k


def at_least(engine, sem, value):
    if isinstance(value, int) and value <= 0:
        return
    engine.wait_ge(sem, value)


def stand_alone(engine, mem):
    engine.sem_inc(mem.tick, 1)


class Turn:

    def __init__(self, k, u):
        self.k, self.u = k, u

    def __add__(self, n):
        v = self.u + n
        return Turn(add(self.k, v // 2), v % 2)

    def times(self, per, extra=0):
        return add(self.k * (2 * per), per * self.u + extra)

    def loads(self, per):
        return add(self.k * (16 * per), 16 * per)


def run_groups(engine, groups, emit, start=0):
    emit(Turn(start, 0), True, False)
    emit(Turn(start, 1), False, False)
    with engine.Fori(start + 1, start + groups // 2 - 1) as k:
        emit(Turn(k, 0), False, False)
        emit(Turn(k, 1), False, False)
    k = start + groups // 2 - 1
    emit(Turn(k, 0), False, False)
    emit(Turn(k, 1), False, True)


class Memory:

    def __init__(self, nc, ctx):
        def sb(name, shape, dt=F32):
            return ctx.enter_context(nc.sbuf_tensor(name, shape, dt))

        self.ident = sb("ident", [P, P])
        self.iota = sb("iota", [P, NE])
        self.minus_half = sb("minus_half", [P, FT])
        self.bias = sb("bias", [P, H * S])
        self.stage = sb("stage", [P, max(NB) * P])
        self.wq, self.wk, self.wv, self.wo = (sb(n, [P, D]) for n in ("wq", "wk", "wv", "wo"))
        self.bqk = sb("bqk", [P, 2])
        self.bv, self.bo = sb("bv", [P, D]), sb("bo", [P, D])
        self.x = sb("x", [P, 2, AT, D])
        self.ctx = sb("ctx", [P, 2, AT, D])
        self.xn = sb("xn", [P, 2, AT, D])
        self.xres = sb("xres", [P, 2, AT, D])
        self.xnew = sb("xnew", [P, 2, AT, D])
        self.st = sb("st", [P, FT, 6])
        self.mv = sb("mv", [P, FT, 2])
        self.veps = sb("veps", [P, FT])
        self.rstd = sb("rstd", [P, FT])
        self.xcT = sb("xcT", [P, 2 * AN])
        self.qk = sb("qk", [P, 2, 2 * AN], F32R)
        self.kstage = sb("kstage", [P, HJ, AN], F32R)
        self.qst = sb("qst", [P, 2, HJ * AT, 2, P], F32R)
        self.kst = sb("kst", [P, 2, HQ, HJ, AN], F32R)
        self.vst = sb("vst", [P, 2, 2 * AT * HP, 32])
        self.probs = sb("probs", [P, 2, H * S])
        self.rowmax = sb("rowmax", [P, 2, H])
        self.probsT = sb("probsT", [P, 2, 4 * P])
        self.o_sb = sb("o_sb", [P, 2 * AN])
        self.rden = sb("rden", [P, AT * HP, 2])
        self.onorm = sb("onorm", [P, AN])
        self.oT = sb("oT", [P, AN])
        nb = max(NB)
        self.wg = [sb(f"wg{i}", [P, nb, P], F32R) for i in range(2)]
        self.wu = [sb(f"wu{i}", [P, nb, P], F32R) for i in range(2)]
        self.wd = [sb(f"wd{i}", [P, nb, P], F32R) for i in range(2)]
        self.b2 = [sb(f"b2{i}", [ROWS, D], F32R) for i in range(2)]
        self.stack = self.wd[1][:, 0:4 * HJ, :].rearrange("p (i c j) m -> p i c j m", i=2, c=2)
        self.sel = sb("sel", [ROWS, max(NCOMB), P], F32R)
        self.bgu = sb("bgu", [P, 2, nb])
        self.mult = sb("mult", [P, nb])
        self.gateT = sb("gateT", [P, max(LOGITS)])

        def ps(name, banks):
            return ctx.enter_context(nc.psum_tensor(name, [P, banks * 512], F32))

        self.banks = [ps(f"bank{i}", n) for i, n in enumerate((2, 2, 1, 1, 1, 1))]


def constants(nc, ctx, mem, dram, block_sems):
    loaded, memset, rows_ps, rows_sb, rows_stored, bias_loaded = (
        ctx.enter_context(nc.semaphore(n)) for n in
        ("const_loaded", "memset_done", "bias_rows_ps", "bias_rows_sb", "bias_rows_stored", "bias_loaded"))
    PIECES = S * S // 512
    HALF = S * S // 2
    rel = mem.wq[0:NBUCKET, 0:H]
    ready = block_sems["ready"]

    def sync(sp):
        sp.dma_start(mem.ident[:], dram["ident"]).then_inc(loaded, 16)
        sp.dma_start(mem.iota[:], dram["iota"]).then_inc(loaded, 16)
        sp.dma_start(rel, dram["rel_bias"]).then_inc(loaded, 16)
        sp.dma_start(mem.stage[0:NBUCKET, 0:HALF], dram["buckets"][:, 0:HALF]).then_inc(loaded, 16)
        for i in range(PIECES):
            if i == PIECES // 2:
                sp.wait_ge(rows_sb, i)
                sp.dma_start(mem.stage[0:NBUCKET, 0:HALF], dram["buckets"][:, HALF:2 * HALF]).then_inc(loaded, 16)
            sp.wait_ge(rows_sb, i + 1)
            sp.dma_start(dram["bias_rows"][:, i * 512:(i + 1) * 512],
                         mem.probs[0:H, i % 2, 0:512]).then_inc(rows_stored, 16)
            sp.wait_ge(rows_stored, 16 * (i + 1))
        src = dram["bias_rows"].rearrange("h (t s) -> t h s", t=S)
        for b in range(2):
            sp.dma_start(mem.bias[b * S:(b + 1) * S, :].rearrange("t (h s) -> t h s", h=H), src)\
                .then_inc(bias_loaded, 16)
        sp.wait_ge(bias_loaded, 32)
        sp.sem_inc(ready, 1)

    def tensor(pe):
        pe.wait_ge(loaded, 64)
        for i in range(PIECES):
            if i == PIECES // 2:
                pe.wait_ge(loaded, 80)
            at = (i % (PIECES // 2)) * 512
            at_least(pe, rows_sb, i - 1)
            nc.tensor.matmul(mem.banks[0][0:H, (i % 2) * 512:(i % 2 + 1) * 512],
                             rel, mem.stage[0:NBUCKET, at:at + 512], start=True, stop=True)\
                .then_inc(rows_ps, 1)

    def scalar(act):
        for i in range(PIECES):
            act.wait_ge(rows_ps, i + 1)
            if i >= 2:
                act.wait_ge(rows_stored, 16 * (i - 1))
            nc.scalar.copy(mem.probs[0:H, i % 2, 0:512],
                           mem.banks[0][0:H, (i % 2) * 512:(i % 2 + 1) * 512]).then_inc(rows_sb, 1)

    def gpsimd(pool):
        nc.gpsimd.memset(mem.minus_half[:], -0.5).then_inc(memset, 1)
        nc.gpsimd.memset(mem.kst[:].bitcast(F32), 0.0).then_inc(memset, 1)
        nc.gpsimd.memset(mem.qst[:].bitcast(F32), 0.0).then_inc(memset, 1)
        pool.wait_ge(memset, 3)
        pool.sem_inc(ready, 1)

    def vector(dve):
        nc.vector.memset(mem.vst[:], 0.0).then_inc(block_sems["vzero"], 1)
        dve.wait_ge(block_sems["vzero"], 1)
        for h2 in range(2):
            nc.vector.memset(mem.vst[h2 * S:(h2 + 1) * S, :, :, 16 + 8 * h2:24 + 8 * h2], 1.0)\
                .then_inc(block_sems["vzero"], 1)
        dve.wait_ge(block_sems["vzero"], 3)
        dve.sem_inc(ready, 1)

    return dict(sync=sync, tensor=tensor, scalar=scalar, gpsimd=gpsimd, vector=vector)


def attention(nc, sem, mem, dram, layer, x_dram, out_dram, x_ready):
    BASE = layer * (AG // 2)
    w_loaded, w_scaled = sem("w_loaded"), sem("w_scaled")
    x_loaded, ctx_loaded, res_loaded, stored = ([sem(f"{n}{u}") for u in range(2)] for n in
                                                ("x_loaded", "ctx_loaded", "res_loaded", "stored"))
    k_spread = [sem(f"k_spread{u}") for u in range(2)]
    stack_ready, stacked, k_staged, q_placed = sem("stack_ready"), sem("stacked"), sem("k_staged"), sem("q_placed")
    stats, ln_scale, ln_chain, xn_ready = sem("stats"), sem("ln_scale"), sem("ln_chain"), sem("xn_ready")
    tr_done, xcT_ready = sem("tr_done"), sem("xcT_ready")
    qk_done, qk_hi, qk_lo = sem("qk_done"), sem("qk_hi"), sem("qk_lo")
    v_done, v_ready = sem("v_done"), sem("v_ready")
    scores_done, scores_read, max_ready, shifted = sem("scores_done"), sem("scores_read"), sem("max_ready"), sem("shifted")
    exp_done = sem("exp_done")
    pT_done, pT_ready, pv_done, o_ready = sem("pT_done"), sem("pT_ready"), sem("pv_done"), sem("o_ready")
    oT_back, rden_ready, normed, oT_done, oT_ready = sem("o_back"), sem("rden"), sem("normed"), sem("oT_done"), sem("oT_ready")
    y_done, res_biased, added = sem("y_done"), sem("res_biased"), sem("added")

    scores, pT_ps, o_ps, tp_v, qk_ps, tail = mem.banks
    WEIGHTS = (5, 5 + 8)[layer]
    xt = x_dram.rearrange("(g t p) d -> p g t d", t=AT, p=P)
    ct = dram["ctx"].rearrange("(g t p) d -> p g t d", t=AT, p=P)
    ot = out_dram.rearrange("(g t p) d -> p g t d", t=AT, p=P)

    def group_of(ap, turn):
        g = turn.times(1, -layer * AG)
        if isinstance(g, int):
            return ap[:, g, :, :]
        return ap[:, bass.ds(g, 1), :, :].rearrange("p a t d -> p (a t) d")

    def sync(sp):
        def load_x(h):
            at_least(sp, xn_ready, h.times(1, -1))
            stand_alone(sp, mem)
            sp.dma_start(mem.x[:, h.u], group_of(xt, h)).then_inc(x_loaded[h.u], 16)

        def load_ctx(h):
            at_least(sp, tr_done, h.times(1, -1))
            stand_alone(sp, mem)
            sp.dma_start(mem.ctx[:, h.u], group_of(ct, h)).then_inc(ctx_loaded[h.u], 16)

        def load_res(h):
            at_least(sp, added, h.times(1, -1))
            stand_alone(sp, mem)
            sp.dma_start(mem.xres[:, h.u], group_of(xt, h)).then_inc(res_loaded[h.u], 16)

        def spread_keys(h):
            at_least(sp, k_staged, h.times(2, 2))
            stand_alone(sp, mem)
            at_least(sp, scores_done, h.times(AT, -AT))
            stand_alone(sp, mem)
            for h4 in range(HQ):
                rows = slice(32 * h4, 32 * h4 + 32)
                sp.dma_start(mem.kst[rows, h.u, h4, :, :].bitcast(F32), mem.kstage[rows, :, :].bitcast(F32))\
                    .then_inc(k_spread[h.u], 16)

        def store(h):
            at_least(sp, added, h.times(1, 1))
            stand_alone(sp, mem)
            sp.dma_start(group_of(ot, h), mem.xnew[:, h.u]).then_inc(stored[h.u], 16)

        if x_ready is not None:
            for s, v in x_ready:
                sp.wait_ge(s, v)
        for n, t in (("wq", mem.wq), ("wk", mem.wk), ("wv", mem.wv), ("wo", mem.wo)):
            sp.dma_start(t[:], dram[f"{n}{layer}"]).then_inc(w_loaded, 16)
        if layer:
            sp.dma_start(mem.bqk[:], dram["bqk"]).then_inc(w_loaded, 16)
            sp.dma_start(mem.bv[:], dram["bv"].to_broadcast([P, D])).then_inc(w_loaded, 16)
            sp.dma_start(mem.bo[:], dram["bo"].to_broadcast([P, D])).then_inc(w_loaded, 16)
        sp.dma_start(mem.stage[:, 0:4 * HJ * P], dram["stack"]).then_inc(w_loaded, 16)
        z = Turn(BASE, 0)
        for n in range(2):
            load_x(z + n)
            load_ctx(z + n)
        spread_keys(z)

        def step(g, first, last):
            if not last:
                if not (isinstance(g.k, int) and 2 * g.k + g.u + 2 >= 2 * BASE + AG):
                    load_x(g + 2)
                    load_ctx(g + 2)
            load_res(g)
            if not last:
                spread_keys(g + 1)
            if not first:
                store(g + -1)
        run_groups(sp, AG, step, BASE)
        store(Turn(BASE + AG // 2 - 1, 1))

    def tensor(pe):
        def transposes(h):
            at_least(pe, xn_ready, h.times(1, 1))
            at_least(pe, ctx_loaded[h.u], h.loads(1))
            at_least(pe, v_ready, h.times(1))
            for t in range(AT):
                nc.tensor.transpose(tp_v[:, t * P:(t + 1) * P], mem.xn[:, h.u, t, :], mem.ident[:])
            for t in range(AT):
                last = nc.tensor.transpose(tp_v[:, AN + t * P:AN + (t + 1) * P], mem.ctx[:, h.u, t, :], mem.ident[:])
            last.then_inc(tr_done, 1)

        def project_qk(h):
            at_least(pe, xcT_ready, h.times(1, 1))
            at_least(pe, q_placed, h.times(2))
            nc.tensor.matmul(qk_ps[:, 0:AN], mem.wq[:], mem.xcT[:, 0:AN], start=True, stop=True)
            nc.tensor.matmul(qk_ps[:, AN:2 * AN], mem.wk[:], mem.xcT[:, AN:2 * AN], start=True, stop=True)\
                .then_inc(qk_done, 1)

        def stack(h, n):
            if n == 0:
                at_least(pe, qk_hi, h.times(1, 1))
                at_least(pe, qk_lo, h.times(1, 1))
            elif n < 3:
                at_least(pe, k_staged, h.times(2, n))
            else:
                at_least(pe, q_placed, h.times(2, 1))
            i = 1 - n // 2
            for jj in range(2):
                out = qk_ps[:, jj * AN:(jj + 1) * AN]
                for part in range(2):
                    last = nc.tensor.matmul(out, mem.stack[:, i, part, 2 * (n % 2) + jj, :],
                                            mem.qk[:, part, i * AN:(i + 1) * AN], start=(part == 0), stop=(part == 1))
            last.then_inc(stacked, 1)

        def project_v(h):
            at_least(pe, xcT_ready, h.times(1, 1))
            for b in range(2 * AT):
                for h2 in range(2):
                    last = nc.tensor.matmul(tp_v[h2 * S:(h2 + 1) * S, b * 64:(b + 1) * 64],
                                            mem.xcT[:, AN + b * S:AN + (b + 1) * S],
                                            mem.wv[:, h2 * 64:(h2 + 1) * 64], start=True, stop=True)
            last.then_inc(v_done, 1)

        def score(g, t):
            at_least(pe, q_placed, g.times(2, 2))
            at_least(pe, k_spread[g.u], g.loads(HQ))
            at_least(pe, shifted if layer else scores_read, g.times(AT, t))
            for j in range(HJ):
                for b in range(2):
                    last = nc.tensor.matmul(scores[:, j * 256:(j + 1) * 256], mem.qst[:, g.u, j * AT + t, b, :],
                                            mem.kst[:, g.u, :, j, t * P + b * S:t * P + (b + 1) * S],
                                            start=(b == 0), stop=(b == 1))
            last.then_inc(scores_done, 1)

        def transpose_probs(g, t):
            at_least(pe, exp_done, g.times(AT, t + 1))
            for half in range(2):
                at_least(pe, pT_ready, g.times(2 * AT, 2 * t - 1 + half))
                for i in range(4):
                    hp = 4 * half + i
                    last = nc.tensor.transpose(pT_ps[:, hp * P:(hp + 1) * P],
                                               mem.probs[:, t, hp * P:(hp + 1) * P], mem.ident[:])
                last.then_inc(pT_done, 1)

        def values(g, t):
            at_least(pe, pT_ready, g.times(2 * AT, 2 * t + 2))
            at_least(pe, v_ready, g.times(1, 1))
            if t == 0:
                at_least(pe, o_ready, g.times(1))
            for hp in range(HP):
                col = t * 256 + (hp // 4) * P
                for b in range(2):
                    last = nc.tensor.matmul(o_ps[32 * (hp % 4):32 * (hp % 4) + 32, col + b * S:col + (b + 1) * S],
                                            mem.vst[:, g.u, (2 * t + b) * HP + hp, :],
                                            mem.probsT[:, hp // 4, (hp % 4) * P + b * S:(hp % 4) * P + (b + 1) * S],
                                            start=True, stop=True)
            last.then_inc(pv_done, 1)

        def back_o(g):
            at_least(pe, o_ready, g.times(1, 1))
            at_least(pe, added, g.times(1))
            for i in range(2 * AT):
                last = nc.tensor.transpose(tail[:, i * P:(i + 1) * P], mem.o_sb[:, i * P:(i + 1) * P], mem.ident[:])
            last.then_inc(oT_back, 1)

        def transpose_o(g):
            at_least(pe, normed, g.times(1, 1))
            for t in range(AT):
                last = nc.tensor.transpose(tail[:, t * P:(t + 1) * P], mem.onorm[:, t * P:(t + 1) * P], mem.ident[:])
            last.then_inc(oT_done, 1)

        def project_o(g):
            at_least(pe, oT_ready, g.times(1, 1))
            for t in range(AT):
                last = nc.tensor.matmul(tail[:, AN + t * P:AN + (t + 1) * P], mem.oT[:, t * P:(t + 1) * P],
                                        mem.wo[:], start=True, stop=True)
            last.then_inc(y_done, 1)

        pe.wait_ge(w_loaded, 16 * WEIGHTS)
        pe.wait_ge(stack_ready, layer + 1)
        if layer:
            pe.wait_ge(w_scaled, 2)
        z = Turn(BASE, 0)
        transposes(z)
        project_qk(z)
        for n in range(4):
            stack(z, n)
        project_v(z)

        def step(g, first, last):
            if not last:
                transposes(g + 1)
            score(g, 0)
            if not first:
                transpose_probs(g + -1, 1)
            if not last:
                project_qk(g + 1)
            if not first:
                values(g + -1, 1)
            if not last:
                stack(g + 1, 0)
            score(g, 1)
            if not last:
                stack(g + 1, 1)
                project_v(g + 1)
            if not first:
                back_o(g + -1)
            if not last:
                stack(g + 1, 2)
            transpose_probs(g, 0)
            if not last:
                stack(g + 1, 3)
            values(g, 0)
            if not first:
                transpose_o(g + -1)
                project_o(g + -1)
        run_groups(pe, AG, step, BASE)
        g = Turn(BASE + AG // 2 - 1, 1)
        transpose_probs(g, 1)
        values(g, 1)
        back_o(g)
        transpose_o(g)
        project_o(g)

    def scalar(act):
        def copy_xcT(h):
            at_least(act, tr_done, h.times(1, 1))
            at_least(act, v_done, h.times(1))
            nc.scalar.copy(mem.xcT[:], tp_v[:]).then_inc(xcT_ready, 1)

        def split_high(h):
            at_least(act, qk_done, h.times(1, 1))
            at_least(act, stacked, h.times(4))
            if layer:
                nc.scalar.activation(mem.qk[:, 0, 0:AN], qk_ps[:, 0:AN], ACT.Identity, bias=mem.bqk[:, 0:1])
                nc.scalar.activation(mem.qk[:, 0, AN:2 * AN], qk_ps[:, AN:2 * AN], ACT.Identity,
                                     bias=mem.bqk[:, 1:2]).then_inc(qk_hi, 1)
            else:
                nc.scalar.copy(mem.qk[:, 0, :], qk_ps[:]).then_inc(qk_hi, 1)

        def stage_keys(h, n):
            at_least(act, stacked, h.times(4, n + 1))
            p = h + -1
            if n == 0 and not (isinstance(p.k, int) and p.k < 0):
                at_least(act, k_spread[p.u], p.loads(HQ))
            nc.scalar.copy(mem.kstage[:, 2 * n:2 * n + 2, :].rearrange("p j t -> p (j t)"), qk_ps[:]).then_inc(k_staged, 1)

        def exponentials(g, t):
            at_least(act, shifted, g.times(AT, t + 1))
            nc.scalar.activation(mem.probs[:, t, :], mem.probs[:, t, :], ACT.Exp).then_inc(exp_done, 1)

        def copy_pT(g, t):
            at_least(act, pv_done, g.times(AT, t))
            for half in range(2):
                at_least(act, pT_done, g.times(2 * AT, 2 * t + half + 1))
                nc.scalar.copy(mem.probsT[:, half, :], pT_ps[:, half * 512:(half + 1) * 512]).then_inc(pT_ready, 1)

        def copy_o(g):
            at_least(act, pv_done, g.times(AT, AT))
            at_least(act, oT_back, g.times(1))
            nc.scalar.copy(mem.o_sb[:], o_ps[:]).then_inc(o_ready, 1)

        def copy_oT(g):
            at_least(act, oT_done, g.times(1, 1))
            at_least(act, y_done, g.times(1))
            nc.scalar.copy(mem.oT[:], tail[:, 0:AN]).then_inc(oT_ready, 1)

        act.wait_ge(w_loaded, 16 * WEIGHTS)
        nc.scalar.copy(mem.stack.rearrange("p i c j m -> p (i c j m)"), mem.stage[:, 0:4 * HJ * P]).then_inc(stack_ready, 1)
        z = Turn(BASE, 0)
        copy_xcT(z)
        split_high(z)
        stage_keys(z, 0)
        stage_keys(z, 1)

        def step(g, first, last):
            if not last:
                copy_xcT(g + 1)
            if not first:
                copy_pT(g + -1, 1)
            if not last:
                split_high(g + 1)
            exponentials(g, 0)
            if not last:
                stage_keys(g + 1, 0)
            if not first:
                copy_o(g + -1)
            if not last:
                stage_keys(g + 1, 1)
            copy_pT(g, 0)
            exponentials(g, 1)
            if not first:
                copy_oT(g + -1)
        run_groups(act, AG, step, BASE)
        g = Turn(BASE + AG // 2 - 1, 1)
        copy_pT(g, 1)
        copy_o(g)
        copy_oT(g)

    def vector(dve):
        def layer_norm_stats(h):
            at_least(dve, x_loaded[h.u], h.loads(1))
            at_least(dve, ln_scale, h.times(1))
            for t in range(AT):
                last = nc.vector.bn_stats(mem.st[:, t, :], mem.x[:, h.u, t, :])
            last.then_inc(ln_chain, 1)
            dve.wait_ge(ln_chain, h.times(1, 1))
            stand_alone(dve, mem)
            for t in range(AT):
                last = nc.vector.bn_aggr(mem.mv[:, t, :], mem.st[:, t, :])
            last.then_inc(stats, 1)

        def normalise(h):
            at_least(dve, ln_scale, h.times(1, 1))
            at_least(dve, tr_done, h.times(1, -1))
            for t in range(AT):
                last = nc.vector.tensor_scalar(mem.xn[:, h.u, t, :], mem.x[:, h.u, t, :], mem.mv[:, t, 0:1],
                                               mem.rstd[:, t:t + 1], ALU.subtract, ALU.mult)
            last.then_inc(xn_ready, 1)

        def split_low(h):
            at_least(dve, qk_hi, h.times(1, 1))
            hi = mem.qk[:, 0, :].bitcast(F32)
            if layer:
                for i in range(2):
                    part = slice(i * AN, (i + 1) * AN)
                    last = nc.vector.scalar_tensor_tensor(mem.qk[:, 1, part], qk_ps[:, part], mem.bqk[:, i:i + 1],
                                                          hi[:, part], ALU.add, ALU.subtract)
            else:
                last = nc.vector.tensor_tensor(mem.qk[:, 1, :], qk_ps[:], hi, ALU.subtract)
            last.then_inc(qk_lo, 1)

        def place_queries(h, n):
            at_least(dve, stacked, h.times(4, 3 + n))
            at_least(dve, scores_done, h.times(AT, -AT))
            src = qk_ps[:].rearrange("p (m b s) -> p m b s", b=2, s=S)
            for b in range(2):
                last = nc.vector.tensor_copy(mem.qst[:, h.u, 2 * AT * n:2 * AT * (n + 1), b, b * S:(b + 1) * S],
                                             src[:, :, b, :])
            last.then_inc(q_placed, 1)

        def softmax_shift(g, t):
            at_least(dve, scores_done, g.times(AT, t + 1))
            at_least(dve, pT_done, g.times(2 * AT, 2 * t - 2))
            probs = mem.probs[:, t, :].rearrange("p (h s) -> p h s", h=H)
            raw = scores[:, :].rearrange("p (h s) -> p h s", h=H)
            if layer == 0:
                nc.vector.tensor_tensor(mem.probs[:, t, :], scores[:, :], mem.bias[:], ALU.add)\
                    .then_inc(scores_read, 1)
                raw = probs
                dve.wait_ge(scores_read, g.times(AT, t + 1))
            nc.vector.tensor_reduce(mem.rowmax[:, t, :], raw, AX.X, ALU.max).then_inc(max_ready, 1)
            if layer:
                dve.wait_ge(max_ready, g.times(AT, t + 1))
                nc.vector.tensor_tensor(probs, raw, mem.rowmax[:, t, :].unsqueeze(2).to_broadcast([P, H, S]),
                                        ALU.subtract).then_inc(shifted, 1)

        def place_values(h):
            at_least(dve, v_done, h.times(1, 1))
            at_least(dve, pv_done, h.times(AT, -AT))
            for h2 in range(2):
                part = slice(h2 * S, (h2 + 1) * S)
                src = tp_v[part, 0:AN].rearrange("p (b n d) -> p b n d", b=2 * AT, n=HP)
                to = mem.vst[part, h.u, :, h2 * DH:(h2 + 1) * DH].rearrange("p (b n) d -> p b n d", b=2 * AT)
                if layer:
                    bias = mem.bv[part, h2 * 64:(h2 + 1) * 64].rearrange("p (n d) -> p n d", n=HP)
                    last = nc.vector.tensor_tensor(to, src, bias.unsqueeze(1).to_broadcast([S, 2 * AT, HP, DH]), ALU.add)
                else:
                    last = nc.vector.tensor_copy(to, src)
            last.then_inc(v_ready, 1)

        def divide(g):
            at_least(dve, oT_back, g.times(1, 1))
            back = tail[:, :].rearrange("p (n k h d) -> p n k h d", n=AT * HP, k=2, h=2)
            nc.vector.reciprocal(mem.rden[:], back[:, :, 1, :, 0]).then_inc(rden_ready, 1)
            dve.wait_ge(rden_ready, g.times(1, 1))
            at_least(dve, oT_done, g.times(1))
            nc.vector.tensor_tensor(mem.onorm[:].rearrange("p (n h d) -> p n h d", n=AT * HP, h=2),
                                    back[:, :, 0, :, :], mem.rden[:].unsqueeze(3).to_broadcast([P, AT * HP, 2, DH]),
                                    ALU.mult).then_inc(normed, 1)

        def add_residual(g):
            at_least(dve, y_done, g.times(1, 1))
            if layer:
                at_least(dve, res_biased, g.times(1, 1 - AG))
            else:
                at_least(dve, res_loaded[g.u], g.loads(1))
            p = g + -2
            if not (isinstance(p.k, int) and p.k < 0):
                at_least(dve, stored[p.u], p.loads(1))
            nc.vector.tensor_tensor(mem.xnew[:, g.u].rearrange("p t d -> p (t d)"), tail[:, AN:2 * AN],
                                    mem.xres[:, g.u].rearrange("p t d -> p (t d)"), ALU.add).then_inc(added, 1)

        if layer:
            dve.wait_ge(w_loaded, 16 * WEIGHTS)
            nc.vector.tensor_scalar(mem.wq[:], mem.wq[:], float(DH) ** -0.5, None, ALU.mult).then_inc(w_scaled, 1)
            nc.vector.tensor_scalar(mem.bqk[:, 0:1], mem.bqk[:, 0:1], float(DH) ** -0.5, None, ALU.mult)\
                .then_inc(w_scaled, 1)
            dve.wait_ge(w_scaled, 2)
        z = Turn(BASE, 0)
        layer_norm_stats(z)
        normalise(z)
        layer_norm_stats(z + 1)
        normalise(z + 1)
        split_low(z)
        place_queries(z, 0)
        place_queries(z, 1)
        place_values(z)

        def step(g, first, last):
            ahead = not (isinstance(g.k, int) and 2 * g.k + g.u + 2 >= 2 * BASE + AG)
            softmax_shift(g, 0)
            if not last:
                split_low(g + 1)
            if ahead:
                layer_norm_stats(g + 2)
            softmax_shift(g, 1)
            if not first:
                divide(g + -1)
            if not last:
                place_queries(g + 1, 0)
                place_values(g + 1)
                place_queries(g + 1, 1)
            if ahead:
                normalise(g + 2)
            if not first:
                add_residual(g + -1)
        run_groups(dve, AG, step, BASE)
        g = Turn(BASE + AG // 2 - 1, 1)
        divide(g)
        add_residual(g)

    def gpsimd(pool):
        def ln_scales(h):
            at_least(pool, stats, h.times(1, 1))
            at_least(pool, xn_ready, h.times(1))
            stand_alone(pool, mem)
            nc.gpsimd.tensor_scalar(mem.veps[:, 0:AT], mem.mv[:, 0:AT, 1], EPS, None, ALU.add).then_inc(pool_chain, 1)
            pool.wait_ge(pool_chain, h.times(1, 1))
            nc.gpsimd.tensor_tensor(mem.rstd[:, 0:AT], mem.veps[:, 0:AT], mem.minus_half[:, 0:AT], ALU.pow)\
                .then_inc(ln_scale, 1)

        def shift(g, t):
            at_least(pool, max_ready, g.times(AT, t + 1))
            probs = mem.probs[:, t, :].rearrange("p (h s) -> p h s", h=H)
            nc.gpsimd.tensor_tensor(probs, probs, mem.rowmax[:, t, :].unsqueeze(2).to_broadcast([P, H, S]),
                                    ALU.subtract).then_inc(shifted, 1)

        def bias_residual(g):
            at_least(pool, res_loaded[g.u], g.loads(1))
            nc.gpsimd.tensor_tensor(mem.xres[:, g.u], mem.xres[:, g.u],
                                    mem.bo[:].unsqueeze(1).to_broadcast([P, AT, D]), ALU.add).then_inc(res_biased, 1)

        pool_chain = gp_chain
        if layer:
            pool.wait_ge(w_loaded, 16 * WEIGHTS)
        z = Turn(BASE, 0)
        ln_scales(z)
        ln_scales(z + 1)

        def step(g, first, last):
            if not (isinstance(g.k, int) and 2 * g.k + g.u + 2 >= 2 * BASE + AG):
                ln_scales(g + 2)
            if layer == 0:
                shift(g, 0)
            if layer:
                bias_residual(g)
            if layer == 0:
                shift(g, 1)
        run_groups(pool, AG, step, BASE)

    gp_chain = sem("pool_chain")
    done = [(stored[u], 16 * (BASE + AG // 2)) for u in range(2)]
    return dict(sync=sync, tensor=tensor, scalar=scalar, vector=vector, gpsimd=gpsimd), done


def feed_forward(nc, ctx, mem, dram, layer, x_dram, out_dram, x_ready):
    L = f"f{layer}_"

    def sem(name):
        return ctx.enter_context(nc.semaphore(L + name))

    def sb(name, shape, dt=F32):
        return mem_ff(name, shape, dt)

    def mem_ff(name, shape, dt):
        if name not in mem.ff:
            mem.ff[name] = mem.ctx_stack.enter_context(nc.sbuf_tensor("ff_" + name, shape, dt))
        return mem.ff[name]

    nb, ncomb, topk, nlog, nexp = NB[layer], NCOMB[layer], TOPK[layer], LOGITS[layer], EXPERTS[layer]
    act_fn = ACT.Silu if layer else ACT.Gelu
    biased = layer == 0

    w_staged, w_hi, w_lo, w_misc, w_mult, stage_scaled = (sem(n) for n in ("w_staged", "w_hi", "w_lo", "w_misc", "w_mult", "stage_scaled"))
    x_loaded, res_loaded, stored = ([sem(f"{n}{u}") for u in range(2)] for n in ("x_loaded", "res_loaded", "stored"))
    stats, ln_scale, ln_chain, pool_chain, xn_ready = (sem(n) for n in ("stats", "ln_scale", "ln_chain", "pool_chain", "xn_ready"))
    xT_done, xT_ready, x_hi, x_lo = (sem(n) for n in ("xT_done", "xT_ready", "x_hi", "x_lo"))
    logits_done, route, route_exp, route_gate = (sem(n) for n in ("logits_done", "route", "route_exp", "route_gate"))
    comb_ready, combT_done, combT_ready = (sem(n) for n in ("comb_ready", "combT_done", "combT_ready"))
    gate_done, up_done, comb_done, act_done = (sem(n) for n in ("gate_done", "up_done", "comb_done", "act_done"))
    hidden, hidden_scaled, h_hi, h_lo, down_done = (sem(n) for n in ("hidden", "hidden_scaled", "h_hi", "h_lo", "down_done"))
    y_ready, y_back, added = (sem(n) for n in ("y_ready", "y_back", "added"))

    x = sb("x", [P, 2, FT, D])
    xres = sb("xres", [P, 2, FT, D])
    xnew = sb("xnew", [P, 2, FT, D])
    xn = sb("xn", [P, FT, D])
    xT = mem.o_sb
    xTh = sb("xTh", [P, 2, FN], F32R)
    xTl = sb("xTl", [P, 2, FN], F32R)
    combT = sb("combT", [ROWS, 2, FN], F32R)
    activated = mem.probs[:, 0, :].rearrange("p (n t) -> p n t", n=2)
    hid = mem.probs[:, 1, :].rearrange("p (n t) -> p n t", n=2)
    product, yT = (mem.probsT[:, 0, :], mem.xcT[:]), mem.probsT[:, 1, :]
    hh_hl = [sb("hh", [P, 2, FN], F32R), sb("hl", [P, 2, FN], F32R)]
    hh, hl = ([hh_hl[i][:, 0], hh_hl[i][:, 1], mem.kstage[:, 2 * i:2 * i + 2, :].rearrange("p j t -> p (j t)")]
              for i in range(2))
    z17 = sb("z", [P, FT, 32])
    zmax = sb("zmax", [P, FT])
    pexp = sb("pexp", [P, FT, NE])
    psum = sb("psum_z", [P, FT])
    top = sb("top", [P, FT, 8])
    idx = sb("idx", [P, FT, 8], U32)
    idxf = sb("idxf", [P, FT, 8])
    wsum = sb("wsum", [P, FT])
    onehot = sb("onehot", [P, FT, 4, NE])
    comb = sb("comb", [P, FT, 32])
    comb_h = sb("comb_h", [P, FT, 32], F32R)
    comb2 = sb("comb2", [P, FT, ROWS])

    gu01, gu23, misc0, y0, y1, tail = mem.banks
    gate_ps = [gu01[:, 0:512], gu01[:, 512:1024]]
    up_ps = [gu23[:, 0:512], gu23[:, 512:1024]]
    comb_ps = misc0
    y_ps = [y0, y1]

    xt = x_dram.rearrange("(g t p) d -> p g t d", t=FT, p=P)
    ot = out_dram.rearrange("(g t p) d -> p g t d", t=FT, p=P)

    def group_of(ap, turn):
        g = turn.times(1)
        if isinstance(g, int):
            return ap[:, g, :, :]
        return ap[:, bass.ds(g, 1), :, :].rearrange("p a t d -> p (a t) d")

    def has_comb(b):
        return b < ncomb

    def two_ahead(g):
        return not (isinstance(g.k, int) and 2 * g.k + g.u + 2 >= FG)

    def slots(engine, per_slot):
        def step(g, first, last):
            for b in range(nb):
                per_slot(g, b, first, last)
        run_groups(engine, FG, step)

    def before(g, b, n):
        return (g, b - n) if b >= n else (g + -1, b - n + nb)

    def count(g, b, extra=0):
        return g.times(nb, b + extra)

    LAG = 3

    def buffer_free(engine, g, b):
        at_least(engine, down_done, count(g, b, 1 - (LAG if b >= nb % LAG else nb % LAG)))

    last_turn = Turn(FG // 2 - 1, 1)
    SLOT_X, SLOT_LOGITS, SLOT_SHIFT, SLOT_EXP, SLOT_Y, SLOT_WEIGHTS, SLOT_COMB = 0, 1, 2, 3, 6, 5, min(nb - 1, 12)
    SLOT_STATS, SLOT_NORMALISE = ((3, 8), (12, 14))[nb > 12]
    ROUTE = ["largest", "shift", "sum_and_top", "inverse_and_places", "scale", "sum_of_top", "guard", "inverse_of_top",
             "weights", "put_weights", "gather", "gather_third", "high", "parts"]
    if topk == 2:
        ROUTE.remove("guard")
        ROUTE.remove("gather_third")
    STEPS = len(ROUTE) - 1
    SHIFTED = ROUTE.index("shift") + 1

    def sync(sp):
        def load(h):
            at_least(sp, xn_ready, h.times(1, -1))
            stand_alone(sp, mem)
            sp.dma_start(x[:, h.u], group_of(xt, h)).then_inc(x_loaded[h.u], 16)

        def load_res(h):
            at_least(sp, added, h.times(1, -1))
            stand_alone(sp, mem)
            sp.dma_start(xres[:, h.u], group_of(xt, h)).then_inc(res_loaded[h.u], 16)

        def store(h):
            at_least(sp, added, h.times(1, 1))
            stand_alone(sp, mem)
            sp.dma_start(group_of(ot, h), xnew[:, h.u]).then_inc(stored[h.u], 16)

        for s, v in x_ready:
            sp.wait_ge(s, v)
        sp.dma_start(mem.gateT[:, 0:nlog], dram[f"gateT{layer}"]).then_inc(w_misc, 16)
        if biased:
            sp.dma_start(mem.bgu[:], dram["bgu"]).then_inc(w_misc, 16)
            sp.dma_start(mem.mult[:], dram["mult"]).then_inc(w_misc, 16)
        z = Turn(0, 0)
        load(z)
        load(z + 1)
        for i, name in enumerate(("wg", "wu", "wd", "b2")[:4 if biased else 3]):
            at_least(sp, w_hi, i)
            stand_alone(sp, mem)
            at_least(sp, w_lo, i)
            stand_alone(sp, mem)
            if name == "b2":
                sp.dma_start(mem.stage[0:ROWS, 0:D], dram["b2"]).then_inc(w_staged, 16)
            else:
                sp.dma_start(mem.stage[:, 0:nb * P], dram[f"{name}{layer}"]).then_inc(w_staged, 16)
        sp.wait_ge(w_hi, arrays)
        sp.wait_ge(w_lo, arrays)
        sp.dma_start(mem.stage[0:ROWS, 0:ncomb * P], dram[f"sel{layer}"]).then_inc(w_staged, 16)

        def step(g, first, last):
            if two_ahead(g):
                load(g + 2)
            load_res(g)
            if not first:
                store(g + -1)
        run_groups(sp, FG, step)
        store(last_turn)

    arrays = 4 if biased else 3

    def tensor(pe):
        def three(out, w, cols, hi, lo, start, stop):
            nc.tensor.matmul(out, w[0][:, cols, :], hi, start=start, stop=False)
            nc.tensor.matmul(out, w[0][:, cols, :], lo, start=False, stop=False)
            return nc.tensor.matmul(out, w[1][:, cols, :], hi, start=False, stop=stop)

        def gate_up(g, b):
            if b == 0:
                at_least(pe, x_hi, g.times(1, 1))
                at_least(pe, x_lo, g.times(1, 1))
            n = b % 2 if nb % 2 == 0 else (b + g.u) % 2
            at_least(pe, act_done, count(g, b, -1))
            three(gate_ps[n], mem.wg, b, xTh[:, g.u], xTl[:, g.u], True, True).then_inc(gate_done, 1)
            at_least(pe, hidden, count(g, b, -1))
            three(up_ps[n], mem.wu, b, xTh[:, g.u], xTl[:, g.u], True, True).then_inc(up_done, 1)

        def router_weights(g, b):
            if b == 0:
                at_least(pe, combT_ready, g.times(1, 1))
            at_least(pe, hidden, count(g, b))
            nc.tensor.matmul(comb_ps[:, :], mem.sel[:, b, :], combT[:, g.u], start=True, stop=True)\
                .then_inc(comb_done, 1)

        def down(g, b):
            n = b % LAG
            at_least(pe, h_hi, count(g, b, 1))
            at_least(pe, h_lo, count(g, b, 1))
            if b == 0:
                at_least(pe, y_ready, g.times(1, -1))
                if biased:
                    nc.tensor.matmul(y_ps[g.u][:, :], mem.b2[0][:], combT[:, g.u], start=True, stop=False)
                    nc.tensor.matmul(y_ps[g.u][:, :], mem.b2[1][:], combT[:, g.u], start=False, stop=False)
            three(y_ps[g.u][:, :], mem.wd, b, hh[n], hl[n], b == 0 and not biased, b == nb - 1)\
                .then_inc(down_done, 1)

        def back_y(g):
            at_least(pe, y_ready, g.times(1, 1))
            at_least(pe, route, g.times(STEPS, 2 * STEPS + SHIFTED))
            for t in range(FT):
                last = nc.tensor.transpose(tail[:, t * P:(t + 1) * P], yT[:, t * P:(t + 1) * P], mem.ident[:])
            last.then_inc(y_back, 1)

        def back_last_but_one(g):
            at_least(pe, y_ready, g.times(1, 1))
            for t in range(FT):
                last = nc.tensor.transpose(tail[:, t * P:(t + 1) * P], yT[:, t * P:(t + 1) * P], mem.ident[:])
            last.then_inc(y_back, 1)

        def transpose_x(h):
            at_least(pe, xn_ready, h.times(1, 1))
            at_least(pe, combT_ready, h.times(1))
            for t in range(FT):
                last = nc.tensor.transpose(tail[:, t * P:(t + 1) * P], xn[:, t, :], mem.ident[:])
            last.then_inc(xT_done, 1)

        def logits(h):
            at_least(pe, xT_ready, h.times(1, 1))
            for t in range(FT):
                last = nc.tensor.matmul(tail[:, t * 32:t * 32 + nlog], xT[:, t * P:(t + 1) * P],
                                        mem.gateT[:, 0:nlog], start=True, stop=True)
            last.then_inc(logits_done, 1)

        def transpose_comb(h):
            at_least(pe, added, h.times(1, -1))
            at_least(pe, comb_ready, h.times(1, 1))
            stand_alone(pe, mem)
            for t in range(FT):
                last = nc.tensor.transpose(tail[0:ROWS, t * P:(t + 1) * P], comb2[:, t, :], mem.ident[:])
            last.then_inc(combT_done, 1)

        pe.wait_ge(w_misc, 16 * (3 if biased else 1))
        z = Turn(0, 0)
        transpose_x(z)
        logits(z)
        transpose_comb(z)
        pe.wait_ge(w_hi, arrays + 1)
        pe.wait_ge(w_lo, arrays)

        def slot(g, b, first, last):
            gate_up(g, b)
            if not (first and b < LAG):
                down(*before(g, b, LAG))
            if has_comb(b):
                router_weights(g, b)
            if b == SLOT_Y and not first:
                if last:
                    back_last_but_one(g + -1)
                else:
                    back_y(g + -1)
            if not last:
                if b == SLOT_X:
                    transpose_x(g + 1)
                if b == SLOT_LOGITS:
                    logits(g + 1)
                if b == SLOT_COMB:
                    transpose_comb(g + 1)
        slots(pe, slot)
        for n in range(LAG, 0, -1):
            down(last_turn, nb - n)
        at_least(pe, y_ready, last_turn.times(1, 1))
        at_least(pe, added, last_turn.times(1))
        for t in range(FT):
            last = nc.tensor.transpose(tail[:, t * P:(t + 1) * P], yT[:, t * P:(t + 1) * P], mem.ident[:])
        last.then_inc(y_back, 1)

    def scalar(act):
        def activate(g, b):
            n = (b + g.u) % 2
            at_least(act, gate_done, count(g, b, 1))
            at_least(act, hidden, count(g, b, -1))
            if biased:
                nc.scalar.activation(activated[:, n], gate_ps[n], act_fn, bias=mem.bgu[:, 0, b:b + 1])\
                    .then_inc(act_done, 1)
            else:
                nc.scalar.activation(activated[:, n], gate_ps[n], act_fn).then_inc(act_done, 1)

        def high(g, b):
            n = (b + g.u) % 2
            at_least(act, hidden, count(g, b, 1))
            buffer_free(act, g, b)
            nc.scalar.copy(hh[b % LAG], hid[:, n]).then_inc(h_hi, 1)

        def copy_y(g):
            at_least(act, down_done, g.times(nb, nb))
            at_least(act, y_back, g.times(1))
            nc.scalar.copy(yT, y_ps[g.u][:, :]).then_inc(y_ready, 1)

        def copy_xT(h):
            at_least(act, xT_done, h.times(1, 1))
            at_least(act, logits_done, h.times(1))
            at_least(act, x_lo, h.times(1))
            nc.scalar.copy(xT[:], tail[:, :]).then_inc(xT_ready, 1)

        def high_x(h):
            act.wait_ge(xT_ready, h.times(1, 1))
            at_least(act, up_done, h.times(nb, -nb))
            nc.scalar.copy(xTh[:, h.u], xT[:]).then_inc(x_hi, 1)

        def route_exponentials(h):
            at_least(act, route, h.times(STEPS, SHIFTED))
            nc.scalar.activation(pexp[:, :, 0:nexp], z17[:, :, 0:nexp], ACT.Exp).then_inc(route_exp, 1)

        def shared_gate(h):
            at_least(act, route, h.times(STEPS, SHIFTED))
            nc.scalar.activation(comb[:, :, NE:NE + 1], z17[:, :, NE:NE + 1], ACT.Tanh, scale=0.5)\
                .then_inc(route_gate, 1)

        def copy_combT(h):
            at_least(act, combT_done, h.times(1, 1))
            at_least(act, down_done, h.times(nb, 1 - 2 * nb))
            at_least(act, comb_done, h.times(ncomb, -ncomb))
            nc.scalar.copy(combT[:, h.u], tail[0:ROWS, :]).then_inc(combT_ready, 1)

        z = Turn(0, 0)
        copy_xT(z)
        high_x(z)
        route_exponentials(z)
        if layer:
            shared_gate(z)
        copy_combT(z)
        for i in range(arrays):
            act.wait_ge(w_staged, 16 * (i + 1))
            if i == 2 and biased:
                act.wait_ge(stage_scaled, 1)
            if i == 3:
                nc.scalar.copy(mem.b2[0][:], mem.stage[0:ROWS, 0:D]).then_inc(w_hi, 1)
            else:
                w = (mem.wg, mem.wu, mem.wd)[i]
                nc.scalar.copy(w[0][:, 0:nb, :].rearrange("p b f -> p (b f)"), mem.stage[:, 0:nb * P]).then_inc(w_hi, 1)
        act.wait_ge(w_staged, 16 * (arrays + 1))
        nc.scalar.copy(mem.sel[:, 0:ncomb, :].rearrange("r b f -> r (b f)"), mem.stage[0:ROWS, 0:ncomb * P])\
            .then_inc(w_hi, 1)

        def slot(g, b, first, last):
            activate(g, b)
            if not (first and b == 0):
                high(*before(g, b, 1))
            if b == SLOT_Y - 1 and not first:
                copy_y(g + -1)
            if not last:
                if b == SLOT_X:
                    copy_xT(g + 1)
                if b == SLOT_X + 1:
                    high_x(g + 1)
                if b == SLOT_EXP:
                    route_exponentials(g + 1)
                if b == SLOT_EXP + 1 and layer:
                    shared_gate(g + 1)
                if b == SLOT_COMB:
                    copy_combT(g + 1)
        slots(act, slot)
        high(last_turn, nb - 1)
        copy_y(last_turn)

    def vector(dve):
        def layer_norm_stats(h):
            at_least(dve, x_loaded[h.u], h.loads(1))
            at_least(dve, ln_scale, h.times(1))
            for t in range(FT):
                last = nc.vector.bn_stats(mem.st[:, t, :], x[:, h.u, t, :])
            last.then_inc(ln_chain, 1)
            dve.wait_ge(ln_chain, h.times(1, 1))
            stand_alone(dve, mem)
            for t in range(FT):
                last = nc.vector.bn_aggr(mem.mv[:, t, :], mem.st[:, t, :])
            last.then_inc(stats, 1)

        def normalise(h):
            at_least(dve, ln_scale, h.times(1, 1))
            at_least(dve, xT_done, h.times(1))
            for t in range(FT):
                last = nc.vector.tensor_scalar(xn[:, t, :], x[:, h.u, t, :], mem.mv[:, t, 0:1],
                                               mem.rstd[:, t:t + 1], ALU.subtract, ALU.mult)
            last.then_inc(xn_ready, 1)

        def route_step(h, n):
            name = ROUTE[n]

            def rows(column, width):
                return column.to_broadcast([P, FT, width])

            if name == "largest":
                at_least(dve, logits_done, h.times(1, 1))
            if name == "shift":
                at_least(dve, route_exp, h.times(1))
            if name == "sum_and_top":
                at_least(dve, route_exp, h.times(1, 1))
            if name == "gather" and layer:
                at_least(dve, route_gate, h.times(1, 1))
            if name == "parts":
                at_least(dve, combT_done, h.times(1))
            at_least(dve, route, h.times(STEPS, n))
            stand_alone(dve, mem)

            raw = tail[:, 0:FT * 32].rearrange("p (t e) -> p t e", t=FT)
            if name == "largest":
                last = nc.vector.tensor_reduce(zmax[:], raw[:, :, 0:nexp], AX.X, ALU.max)
            elif name == "shift":
                if layer:
                    nc.vector.tensor_copy(z17[:, :, NE:NE + 1], raw[:, :, NE:NE + 1])
                last = nc.vector.tensor_tensor(z17[:, :, 0:nexp], raw[:, :, 0:nexp], rows(zmax[:].unsqueeze(2), nexp),
                                               ALU.subtract)
            elif name == "sum_and_top":
                for t in range(FT):
                    nc.vector.max(top[:, t, :], pexp[:, t, :])
                last = nc.vector.tensor_reduce(psum[:], pexp[:, :, 0:nexp], AX.X, ALU.add)
            elif name == "inverse_and_places":
                for t in range(FT):
                    nc.vector.max_index(idx[:, t, :], top[:, t, :], pexp[:, t, :])
                last = nc.vector.reciprocal(psum[:], psum[:])
            elif name == "scale":
                nc.vector.tensor_copy(idxf[:], idx[:])
                last = nc.vector.tensor_tensor(top[:, :, 0:topk], top[:, :, 0:topk], rows(psum[:].unsqueeze(2), topk), ALU.mult)
            elif name == "sum_of_top":
                for k in range(topk):
                    nc.vector.tensor_tensor(onehot[:, :, k, :], mem.iota[:].unsqueeze(1).to_broadcast([P, FT, NE]),
                                            rows(idxf[:, :, k:k + 1], NE), ALU.is_equal)
                last = nc.vector.tensor_reduce(wsum[:], top[:, :, 0:topk], AX.X, ALU.add)
            elif name == "guard":
                last = nc.vector.tensor_scalar(wsum[:], wsum[:], 1e-20, None, ALU.add)
            elif name == "inverse_of_top":
                last = nc.vector.reciprocal(wsum[:], wsum[:])
            elif name == "weights":
                last = nc.vector.tensor_tensor(top[:, :, 0:topk], top[:, :, 0:topk], rows(wsum[:].unsqueeze(2), topk), ALU.mult)
            elif name == "put_weights":
                for k in range(topk):
                    last = nc.vector.tensor_tensor(onehot[:, :, k, :], onehot[:, :, k, :], rows(top[:, :, k:k + 1], NE),
                                                   ALU.mult)
            elif name == "gather":
                if layer:
                    nc.vector.tensor_scalar(comb[:, :, NE:NE + 1], comb[:, :, NE:NE + 1], 1.0, 0.5, ALU.add, ALU.mult)
                last = nc.vector.tensor_tensor(comb[:, :, 0:nexp], onehot[:, :, 0, 0:nexp], onehot[:, :, 1, 0:nexp], ALU.add)
            elif name == "gather_third":
                last = nc.vector.tensor_tensor(comb[:, :, 0:nexp], comb[:, :, 0:nexp], onehot[:, :, 2, 0:nexp], ALU.add)
            elif name == "high":
                last = nc.vector.tensor_copy(comb_h[:], comb[:])
            elif name == "parts":
                nc.vector.tensor_copy(comb2[:, :, 0:32], comb_h[:].bitcast(F32))
                nc.vector.tensor_tensor(comb2[:, :, 32:64], comb[:], comb_h[:].bitcast(F32), ALU.subtract)\
                    .then_inc(comb_ready, 1)
                return
            last.then_inc(route, 1)

        def multiply(g, b, last):
            n = (b + g.u) % 2
            at_least(dve, up_done, count(g, b, 1))
            at_least(dve, act_done, count(g, b, 1))
            at_least(dve, h_lo, count(g, b, -1))
            if has_comb(b):
                if biased:
                    nc.vector.scalar_tensor_tensor(product[n], up_ps[n], mem.bgu[:, 1, b:b + 1], activated[:, n],
                                                   ALU.add, ALU.mult).then_inc(hidden_scaled, 1)
                else:
                    nc.vector.tensor_tensor(product[n], up_ps[n], activated[:, n], ALU.mult)\
                        .then_inc(hidden_scaled, 1)
                if not last:
                    beside(g, b, 0)
                dve.wait_ge(hidden_scaled, g.times(ncomb, b + 1))
                at_least(dve, comb_done, g.times(ncomb, b + 1))
                nc.vector.tensor_tensor(hid[:, n], product[n], comb_ps[:, :], ALU.mult).then_inc(hidden, 1)
            else:
                nc.vector.scalar_tensor_tensor(hid[:, n], up_ps[n], mem.bgu[:, 1, b:b + 1], activated[:, n],
                                               ALU.add, ALU.mult).then_inc(hidden, 1)

        def beside(g, b, place):
            if b == SLOT_SHIFT:
                route_step(g + 1, place)
            n = 2 * (b - SLOT_WEIGHTS) + place
            if 0 <= n < len(ROUTE) - SHIFTED:
                route_step(g + 1, SHIFTED + n)

        def add_residual(g):
            at_least(dve, y_back, g.times(1, 1))
            at_least(dve, res_loaded[g.u], g.loads(1))
            p = g + -2
            if not (isinstance(p.k, int) and p.k < 0):
                at_least(dve, stored[p.u], p.loads(1))
            nc.vector.tensor_tensor(xnew[:, g.u].rearrange("p t d -> p (t d)"), tail[:, :],
                                    xres[:, g.u].rearrange("p t d -> p (t d)"), ALU.add).then_inc(added, 1)

        nc.vector.memset(comb[:], 0.0).then_inc(w_mult, 1)
        nc.vector.memset(pexp[:], -1.0).then_inc(w_mult, 1)
        dve.wait_ge(w_mult, 2)
        if layer == 0:
            nc.vector.memset(comb[:, :, NE - 1:NE], 1.0).then_inc(w_mult, 1)
            dve.wait_ge(w_mult, 3)
        dve.wait_ge(w_misc, 16 * (3 if biased else 1))
        z = Turn(0, 0)
        layer_norm_stats(z)
        normalise(z)
        layer_norm_stats(z + 1)
        for n in range(len(ROUTE)):
            route_step(z, n)
        normalise(z + 1)
        for i in range(arrays):
            dve.wait_ge(w_staged, 16 * (i + 1))
            if i == 2 and biased:
                staged = mem.stage[:, 0:nb * P].rearrange("p (b f) -> p b f", b=nb)
                nc.vector.tensor_tensor(staged, staged, mem.mult[:].unsqueeze(2).to_broadcast([P, nb, P]), ALU.mult)\
                    .then_inc(stage_scaled, 1)
            dve.wait_ge(w_hi, i + 1)
            if i == 3:
                nc.vector.tensor_tensor(mem.b2[1][:], mem.stage[0:ROWS, 0:D], mem.b2[0].bitcast(F32)[:], ALU.subtract)\
                    .then_inc(w_lo, 1)
            else:
                w = (mem.wg, mem.wu, mem.wd)[i]
                nc.vector.tensor_tensor(w[1][:, 0:nb, :].rearrange("p b f -> p (b f)"), mem.stage[:, 0:nb * P],
                                        w[0].bitcast(F32)[:, 0:nb, :].rearrange("p b f -> p (b f)"), ALU.subtract)\
                    .then_inc(w_lo, 1)

        def slot(g, b, first, last):
            multiply(g, b, last)
            if not last:
                beside(g, b, 1)
            if b == SLOT_Y and not first:
                add_residual(g + -1)
            if two_ahead(g):
                if b == SLOT_STATS:
                    layer_norm_stats(g + 2)
                if b == SLOT_NORMALISE:
                    normalise(g + 2)
        slots(dve, slot)
        add_residual(last_turn)

    def gpsimd(pool):
        def ln_scales(h):
            at_least(pool, stats, h.times(1, 1))
            at_least(pool, xn_ready, h.times(1))
            stand_alone(pool, mem)
            nc.gpsimd.tensor_scalar(mem.veps[:], mem.mv[:, :, 1], EPS, None, ALU.add).then_inc(pool_chain, 1)
            pool.wait_ge(pool_chain, h.times(1, 1))
            nc.gpsimd.tensor_tensor(mem.rstd[:], mem.veps[:], mem.minus_half[:], ALU.pow).then_inc(ln_scale, 1)

        def low_x(h):
            at_least(pool, x_hi, h.times(1, 1))
            nc.gpsimd.tensor_tensor(xTl[:, h.u], xT[:], xTh.bitcast(F32)[:, h.u], ALU.subtract).then_inc(x_lo, 1)

        def low(g, b):
            n = (b + g.u) % 2
            at_least(pool, h_hi, count(g, b, 1))
            buffer_free(pool, g, b)
            nc.gpsimd.tensor_tensor(hl[b % LAG], hid[:, n], hh[b % LAG].bitcast(F32), ALU.subtract).then_inc(h_lo, 1)

        z = Turn(0, 0)
        ln_scales(z)
        ln_scales(z + 1)
        low_x(z)

        def slot(g, b, first, last):
            low(g, b)
            if not last:
                if b == SLOT_X + 1:
                    low_x(g + 1)
            if b == SLOT_STATS and two_ahead(g):
                ln_scales(g + 2)
        slots(pool, slot)

    done = [(stored[u], 16 * (FG // 2)) for u in range(2)]
    return dict(sync=sync, tensor=tensor, scalar=scalar, vector=vector, gpsimd=gpsimd), done


def decoder_kernel(nc, dram, out):
    with ExitStack() as ctx:
        mem = Memory(nc, ctx)
        mem.ff, mem.ctx_stack = {}, ctx
        mem.tick = ctx.enter_context(nc.semaphore("tick"))
        ready = ctx.enter_context(nc.semaphore("ready"))
        vzero = ctx.enter_context(nc.semaphore("vzero"))
        x1, x2, x3 = (dram[n] for n in ("x1", "x2", "x3"))
        setup = constants(nc, ctx, mem, dram, {"ready": ready, "vzero": vzero})
        named = {}

        def shared(name):
            if name not in named:
                named[name] = ctx.enter_context(nc.semaphore("attn_" + name))
            return named[name]

        a0, x1_ready = attention(nc, shared, mem, dram, 0, dram["x"], x1, None)
        f0, x2_ready = feed_forward(nc, ctx, mem, dram, 0, x1, x2, x1_ready)
        a1, x3_ready = attention(nc, shared, mem, dram, 1, x2, x3, x2_ready)
        f1, out_ready = feed_forward(nc, ctx, mem, dram, 1, x3, out, x3_ready)
        block = ctx.enter_context(nc.Block())

        def phases(engine, name):
            setup[name](engine)
            engine.wait_ge(ready, 3)
            for part in (a0, f0, a1, f1):
                part[name](engine)

        @block.sync
        def _(sp):
            phases(sp, "sync")
            for s, v in out_ready:
                sp.wait_ge(s, v)

        @block.tensor
        def _(pe):
            phases(pe, "tensor")

        @block.scalar
        def _(act):
            phases(act, "scalar")

        @block.vector
        def _(dve):
            phases(dve, "vector")

        @block.gpsimd
        def _(pool):
            phases(pool, "gpsimd")


def bucket_table():
    rel = np.arange(S)[None, :] - np.arange(S)[:, None]
    half, exact, far = NBUCKET // 2, NBUCKET // 4, 128
    dist = np.abs(rel)
    log = np.log((np.maximum(dist, 1) / exact).astype(np.float32)) / np.float32(math.log(far / exact))
    large = np.minimum(exact + (log * (half - exact)).astype(np.int32), half - 1)
    bucket = (rel > 0) * half + np.where(dist < exact, dist, large)
    return (np.arange(NBUCKET)[:, None] == bucket.reshape(1, -1)).astype(np.float32)


def stacking():
    m = np.zeros((P, 2, 2, HJ, P), np.float32)
    for h4 in range(HQ):
        for c in range(NC):
            for d in range(DH):
                for j in range(HJ):
                    row, col = h4 * 32 + d * HJ + j, h4 * 32 + c * DH + d
                    m[row, 0, c % 2, j, col] = 1.0
                    m[row, 1, c // 2, j, col] = 1.0
    return m.reshape(P, -1)


def selection(layer):
    sel = np.zeros((ROWS, NCOMB[layer], P), np.float32)
    for b in range(NCOMB[layer]):
        for f in range(P):
            e = b if layer == 0 else (2 * b + f // 64 if b < 8 else NE)
            sel[e, b, f] = sel[32 + e, b, f] = 1.0
    return sel


def layout(inp):
    a = {k: np.asarray(v) for k, v in inp.items()}
    c = np.ascontiguousarray

    def qk_order(w):
        return c(w.reshape(-1, HJ, HQ, DH).transpose(0, 2, 3, 1).reshape(-1, D))

    def heads_last(w):
        return w.transpose(1, 0, 2).reshape(D, H * DH)

    def pairs_apart(w):
        return c(w.reshape(-1, HP, 2, DH).transpose(0, 2, 1, 3).reshape(-1, D))

    t = {"x": a["x"].reshape(TOK, D), "ctx": a["ctx_1024"].reshape(TOK, D)}
    t["wq0"], t["wk0"] = qk_order(a["L0_xattn_wq"]), qk_order(a["L0_xattn_wk"])
    t["wv0"], t["wo0"] = pairs_apart(a["L0_xattn_wv"]), a["L0_xattn_wo"]
    t["rel_bias"] = a["L0_xattn_rel_bias"]
    t["wq1"], t["wk1"] = qk_order(heads_last(a["L1_xattn_wq"])), qk_order(heads_last(a["L1_xattn_wk"]))
    t["wv1"], t["wo1"] = pairs_apart(heads_last(a["L1_xattn_wv"])), a["L1_xattn_wo"]
    t["bqk"] = np.stack([qk_order(a[n].reshape(1, D))[0] for n in ("L1_xattn_bq", "L1_xattn_bk")], 1)
    t["bv"], t["bo"] = pairs_apart(a["L1_xattn_bv"].reshape(1, D)), a["L1_xattn_bo"].reshape(1, D)
    F = 128
    fc1, sfc1 = a["L0_ffn_fc1_w"], a["L0_ffn_s_fc1_w"].reshape(2, 2, F, D)
    up = np.concatenate([fc1[:, :F], sfc1[0]])
    gate = np.concatenate([fc1[:, F:], sfc1[1]])
    t["wu0"], t["wg0"] = (w.transpose(2, 0, 1).reshape(D, -1) for w in (up, gate))
    down = np.concatenate([a["L0_ffn_fc2_w"], a["L0_ffn_s_fc2_w"].reshape(D, 2, F).transpose(1, 0, 2)])
    t["wd0"] = down.transpose(2, 0, 1).reshape(F, -1)
    b1, sb1 = a["L0_ffn_fc1_b"], a["L0_ffn_s_fc1_b"].reshape(2, 2, F)
    bias_gate, bias_up = np.concatenate([b1[:, F:], sb1[1]]), np.concatenate([b1[:, :F], sb1[0]])
    t["bgu"] = np.stack([bias_gate.T, bias_up.T], 1)
    t["mult"] = np.concatenate([a["L0_ffn_geglu_mult"], a["L0_ffn_s_geglu_mult"].reshape(2, F)]).T
    b2 = np.zeros((2, 32, D), np.float32)
    b2[:, :15], b2[:, 15] = a["L0_ffn_fc2_b"], a["L0_ffn_s_fc2_b"]
    t["b2"] = b2.reshape(ROWS, D)
    t["gateT0"] = a["L0_ffn_gate_w"].T
    gu = a["L1_ffn_w_gate_up"].reshape(8, 2, D, 2, 64).transpose(3, 2, 0, 1, 4).reshape(2, D, 8 * P)
    def filled(w):
        return np.concatenate([w, np.zeros((3 * P - w.shape[0], D), np.float32)])
    t["wg1"] = np.concatenate([gu[0], filled(a["L1_ffn_shared_w_gate"]).T], 1)
    t["wu1"] = np.concatenate([gu[1], filled(a["L1_ffn_shared_w_up"]).T], 1)
    d1 = a["L1_ffn_w_down"].reshape(8, P, D).transpose(1, 0, 2).reshape(P, -1)
    sd = filled(a["L1_ffn_shared_w_down"].T).reshape(3, P, D).transpose(1, 0, 2).reshape(P, -1)
    t["wd1"] = np.concatenate([d1, sd], 1)
    t["gateT1"] = np.concatenate([a["L1_ffn_gate_w"], a["L1_ffn_shared_gate_w"]]).T
    t["ident"] = np.eye(P, dtype=np.float32)
    t["iota"] = np.tile(np.arange(NE, dtype=np.float32), (P, 1))
    t["buckets"] = bucket_table()
    t["stack"] = stacking()
    t["sel0"], t["sel1"] = selection(0).reshape(ROWS, -1), selection(1).reshape(ROWS, -1)
    return {k: c(v) for k, v in t.items()}


def kernel(**inputs):
    import concourse.bacc as bacc
    from concourse.bass_utils import run_bass_kernel_spmd

    nc = bacc.Bacc("TRN2", target_bir_lowering=False, num_devices=1)
    arrays, dram = {}, {}
    for name, a in layout(inputs).items():
        arrays[f"in_{name}"] = a
        dram[name] = nc.dram_tensor(f"in_{name}", a.shape, mybir.dt.from_np(a.dtype), kind="ExternalInput").ap()
    for name, shape in (("x1", (TOK, D)), ("x2", (TOK, D)), ("x3", (TOK, D)), ("bias_rows", (H, S * S))):
        dram[name] = nc.dram_tensor(name, shape, F32, kind="Internal").ap()
    out = nc.dram_tensor("out", (TOK, D), F32, kind="ExternalOutput").ap()
    decoder_kernel(nc, dram, out)
    result = run_bass_kernel_spmd(nc, [arrays], core_ids=[0])
    return result.results[0]["out"].reshape(B, S, D)
```

```python
import math
from contextlib import ExitStack

import numpy as np

import concourse.bass as bass
from concourse import mybir

ALU = mybir.AluOpType
ACT = mybir.ActivationFunctionType
AX = mybir.AxisListType
F32 = mybir.dt.float32
F32R = mybir.dt.float32r
U32 = mybir.dt.uint32

P = 128
B, S, D = 128, 64, 128
H, DH = 16, 8
HQ, HJ = 4, 4
NC = 4
TOK = B * S
TILES = TOK // P
HP = H // 2
AT = 2
AN = AT * P
AG = TILES // AT
FT = 4
FN = FT * P
FG = TILES // FT
NE = 16
ROWS = 64
EPS = 1e-5
NB = (17, 11)
NCOMB = (15, 11)
TOPK = (3, 2)
LOGITS = (15, 17)
EXPERTS = (15, 16)
NBUCKET = 32


def add(k, n):
    return k + n if n else k


def at_least(engine, sem, value):
    if isinstance(value, int) and value <= 0:
        return
    engine.wait_ge(sem, value)


def stand_alone(engine, mem):
    engine.sem_inc(mem.tick, 1)


class Turn:

    def __init__(self, k, u):
        self.k, self.u = k, u

    def __add__(self, n):
        v = self.u + n
        return Turn(add(self.k, v // 2), v % 2)

    def times(self, per, extra=0):
        return add(self.k * (2 * per), per * self.u + extra)

    def loads(self, per):
        return add(self.k * (16 * per), 16 * per)


def run_groups(engine, groups, emit, start=0):
    emit(Turn(start, 0), True, False)
    emit(Turn(start, 1), False, False)
    with engine.Fori(start + 1, start + groups // 2 - 1) as k:
        emit(Turn(k, 0), False, False)
        emit(Turn(k, 1), False, False)
    k = start + groups // 2 - 1
    emit(Turn(k, 0), False, False)
    emit(Turn(k, 1), False, True)


class Memory:

    def __init__(self, nc, ctx):
        def sb(name, shape, dt=F32):
            return ctx.enter_context(nc.sbuf_tensor(name, shape, dt))

        self.ident = sb("ident", [P, P])
        self.iota = sb("iota", [P, NE])
        self.minus_half = sb("minus_half", [P, FT])
        self.bias = sb("bias", [P, H * S])
        self.stage = sb("stage", [P, max(NB) * P])
        self.wq, self.wk, self.wv, self.wo = (sb(n, [P, D]) for n in ("wq", "wk", "wv", "wo"))
        self.bqk = sb("bqk", [P, 2])
        self.bv, self.bo = sb("bv", [P, D]), sb("bo", [P, D])
        self.x = sb("x", [P, 2, AT, D])
        self.ctx = sb("ctx", [P, 2, AT, D])
        self.xn = sb("xn", [P, 2, AT, D])
        self.xres = sb("xres", [P, 2, AT, D])
        self.xnew = sb("xnew", [P, 2, AT, D])
        self.st = sb("st", [P, FT, 6])
        self.mv = sb("mv", [P, FT, 2])
        self.veps = sb("veps", [P, FT])
        self.rstd = sb("rstd", [P, FT])
        self.xcT = sb("xcT", [P, 2 * AN])
        self.qk = sb("qk", [P, 2, 2 * AN], F32R)
        self.kstage = sb("kstage", [P, HJ, AN], F32R)
        self.qst = sb("qst", [P, 2, HJ * AT, 2, P], F32R)
        self.kst = sb("kst", [P, 2, HQ, HJ, AN], F32R)
        self.vst = sb("vst", [P, 2, 2 * AT * HP, 32])
        self.probs = sb("probs", [P, 2, H * S])
        self.rowmax = sb("rowmax", [P, 2, H])
        self.probsT = sb("probsT", [P, 2, 4 * P])
        self.o_sb = sb("o_sb", [P, 2 * AN])
        self.rden = sb("rden", [P, AT * HP, 2])
        self.onorm = sb("onorm", [P, AN])
        self.oT = sb("oT", [P, AN])
        nb = max(NB)
        self.wg = [sb(f"wg{i}", [P, nb, P], F32R) for i in range(2)]
        self.wu = [sb(f"wu{i}", [P, nb, P], F32R) for i in range(2)]
        self.wd = [sb(f"wd{i}", [P, nb, P], F32R) for i in range(2)]
        self.b2 = [sb(f"b2{i}", [ROWS, D], F32R) for i in range(2)]
        self.stack = self.wd[1][:, 0:4 * HJ, :].rearrange("p (i c j) m -> p i c j m", i=2, c=2)
        self.sel = sb("sel", [ROWS, max(NCOMB), P], F32R)
        self.bgu = sb("bgu", [P, 2, nb])
        self.mult = sb("mult", [P, nb])
        self.gateT = sb("gateT", [P, max(LOGITS)])

        def ps(name, banks):
            return ctx.enter_context(nc.psum_tensor(name, [P, banks * 512], F32))

        self.banks = [ps(f"bank{i}", n) for i, n in enumerate((2, 2, 1, 1, 1, 1))]


def constants(nc, ctx, mem, dram, block_sems):
    loaded, memset, rows_ps, rows_sb, rows_stored, bias_loaded = (
        ctx.enter_context(nc.semaphore(n)) for n in
        ("const_loaded", "memset_done", "bias_rows_ps", "bias_rows_sb", "bias_rows_stored", "bias_loaded"))
    PIECES = S * S // 512
    HALF = S * S // 2
    rel = mem.wq[0:NBUCKET, 0:H]
    ready = block_sems["ready"]

    def sync(sp):
        sp.dma_start(mem.ident[:], dram["ident"]).then_inc(loaded, 16)
        sp.dma_start(mem.iota[:], dram["iota"]).then_inc(loaded, 16)
        sp.dma_start(rel, dram["rel_bias"]).then_inc(loaded, 16)
        sp.dma_start(mem.stage[0:NBUCKET, 0:HALF], dram["buckets"][:, 0:HALF]).then_inc(loaded, 16)
        for i in range(PIECES):
            if i == PIECES // 2:
                sp.wait_ge(rows_sb, i)
                sp.dma_start(mem.stage[0:NBUCKET, 0:HALF], dram["buckets"][:, HALF:2 * HALF]).then_inc(loaded, 16)
            sp.wait_ge(rows_sb, i + 1)
            sp.dma_start(dram["bias_rows"][:, i * 512:(i + 1) * 512],
                         mem.probs[0:H, i % 2, 0:512]).then_inc(rows_stored, 16)
            sp.wait_ge(rows_stored, 16 * (i + 1))
        src = dram["bias_rows"].rearrange("h (t s) -> t h s", t=S)
        for b in range(2):
            sp.dma_start(mem.bias[b * S:(b + 1) * S, :].rearrange("t (h s) -> t h s", h=H), src)\
                .then_inc(bias_loaded, 16)
        sp.wait_ge(bias_loaded, 32)
        sp.sem_inc(ready, 1)

    def tensor(pe):
        pe.wait_ge(loaded, 64)
        for i in range(PIECES):
            if i == PIECES // 2:
                pe.wait_ge(loaded, 80)
            at = (i % (PIECES // 2)) * 512
            at_least(pe, rows_sb, i - 1)
            nc.tensor.matmul(mem.banks[0][0:H, (i % 2) * 512:(i % 2 + 1) * 512],
                             rel, mem.stage[0:NBUCKET, at:at + 512], start=True, stop=True)\
                .then_inc(rows_ps, 1)

    def scalar(act):
        for i in range(PIECES):
            act.wait_ge(rows_ps, i + 1)
            if i >= 2:
                act.wait_ge(rows_stored, 16 * (i - 1))
            nc.scalar.copy(mem.probs[0:H, i % 2, 0:512],
                           mem.banks[0][0:H, (i % 2) * 512:(i % 2 + 1) * 512]).then_inc(rows_sb, 1)

    def gpsimd(pool):
        nc.gpsimd.memset(mem.minus_half[:], -0.5).then_inc(memset, 1)
        nc.gpsimd.memset(mem.kst[:].bitcast(F32), 0.0).then_inc(memset, 1)
        nc.gpsimd.memset(mem.qst[:].bitcast(F32), 0.0).then_inc(memset, 1)
        pool.wait_ge(memset, 3)
        pool.sem_inc(ready, 1)

    def vector(dve):
        nc.vector.memset(mem.vst[:], 0.0).then_inc(block_sems["vzero"], 1)
        dve.wait_ge(block_sems["vzero"], 1)
        for h2 in range(2):
            nc.vector.memset(mem.vst[h2 * S:(h2 + 1) * S, :, :, 16 + 8 * h2:24 + 8 * h2], 1.0)\
                .then_inc(block_sems["vzero"], 1)
        dve.wait_ge(block_sems["vzero"], 3)
        dve.sem_inc(ready, 1)

    return dict(sync=sync, tensor=tensor, scalar=scalar, gpsimd=gpsimd, vector=vector)


def attention(nc, sem, mem, dram, layer, x_dram, out_dram, x_ready):
    BASE = layer * (AG // 2)
    w_loaded, w_scaled = sem("w_loaded"), sem("w_scaled")
    x_loaded, ctx_loaded, res_loaded, stored = ([sem(f"{n}{u}") for u in range(2)] for n in
                                                ("x_loaded", "ctx_loaded", "res_loaded", "stored"))
    k_spread = [sem(f"k_spread{u}") for u in range(2)]
    stack_ready, stacked, k_staged, q_placed = sem("stack_ready"), sem("stacked"), sem("k_staged"), sem("q_placed")
    stats, ln_scale, ln_chain, xn_ready = sem("stats"), sem("ln_scale"), sem("ln_chain"), sem("xn_ready")
    tr_done, xcT_ready = sem("tr_done"), sem("xcT_ready")
    qk_done, qk_hi, qk_lo = sem("qk_done"), sem("qk_hi"), sem("qk_lo")
    v_done, v_ready = sem("v_done"), sem("v_ready")
    scores_done, scores_read, max_ready, shifted = sem("scores_done"), sem("scores_read"), sem("max_ready"), sem("shifted")
    exp_done = sem("exp_done")
    pT_done, pT_ready, pv_done, o_ready = sem("pT_done"), sem("pT_ready"), sem("pv_done"), sem("o_ready")
    oT_back, rden_ready, normed, oT_done, oT_ready = sem("o_back"), sem("rden"), sem("normed"), sem("oT_done"), sem("oT_ready")
    y_done, res_biased, added = sem("y_done"), sem("res_biased"), sem("added")

    scores, pT_ps, o_ps, tp_v, qk_ps, tail = mem.banks
    WEIGHTS = (5, 5 + 8)[layer]
    xt = x_dram.rearrange("(g t p) d -> p g t d", t=AT, p=P)
    ct = dram["ctx"].rearrange("(g t p) d -> p g t d", t=AT, p=P)
    ot = out_dram.rearrange("(g t p) d -> p g t d", t=AT, p=P)

    def group_of(ap, turn):
        g = turn.times(1, -layer * AG)
        if isinstance(g, int):
            return ap[:, g, :, :]
        return ap[:, bass.ds(g, 1), :, :].rearrange("p a t d -> p (a t) d")

    def exists(turn):
        return not isinstance(turn.k, int) or 0 <= turn.times(1, -2 * BASE) < AG

    def run_steps(engine, step):
        for n in range(-3, 2):
            step(Turn(BASE, 0) + n)
        with engine.Fori(BASE + 1, BASE + AG // 2 - 2) as k:
            step(Turn(k, 0))
            step(Turn(k, 1))
        for n in range(AG - 4, AG + 2):
            step(Turn(BASE, 0) + n)

    def sync(sp):
        def load_x(h):
            at_least(sp, xn_ready, h.times(1, -1))
            stand_alone(sp, mem)
            sp.dma_start(mem.x[:, h.u], group_of(xt, h)).then_inc(x_loaded[h.u], 16)

        def load_ctx(h):
            at_least(sp, tr_done, h.times(1, -1))
            stand_alone(sp, mem)
            sp.dma_start(mem.ctx[:, h.u], group_of(ct, h)).then_inc(ctx_loaded[h.u], 16)

        def load_res(h):
            at_least(sp, added, h.times(1, -1))
            stand_alone(sp, mem)
            sp.dma_start(mem.xres[:, h.u], group_of(xt, h)).then_inc(res_loaded[h.u], 16)

        def spread_keys(h):
            at_least(sp, k_staged, h.times(2, 2))
            stand_alone(sp, mem)
            at_least(sp, scores_done, h.times(2 * AT, -2 * AT))
            stand_alone(sp, mem)
            for h4 in range(HQ):
                rows = slice(32 * h4, 32 * h4 + 32)
                sp.dma_start(mem.kst[rows, h.u, h4, :, :].bitcast(F32), mem.kstage[rows, :, :].bitcast(F32))\
                    .then_inc(k_spread[h.u], 16)

        def store(h):
            at_least(sp, added, h.times(1, 1))
            stand_alone(sp, mem)
            sp.dma_start(group_of(ot, h), mem.xnew[:, h.u]).then_inc(stored[h.u], 16)

        if x_ready is not None:
            for s, v in x_ready:
                sp.wait_ge(s, v)
        for n, t in (("wq", mem.wq), ("wk", mem.wk), ("wv", mem.wv), ("wo", mem.wo)):
            sp.dma_start(t[:], dram[f"{n}{layer}"]).then_inc(w_loaded, 16)
        if layer:
            sp.dma_start(mem.bqk[:], dram["bqk"]).then_inc(w_loaded, 16)
            sp.dma_start(mem.bv[:], dram["bv"].to_broadcast([P, D])).then_inc(w_loaded, 16)
            sp.dma_start(mem.bo[:], dram["bo"].to_broadcast([P, D])).then_inc(w_loaded, 16)
        sp.dma_start(mem.stage[:, 0:4 * HJ * P], dram["stack"]).then_inc(w_loaded, 16)
        def step(g):
            if exists(g + 3):
                load_x(g + 3)
                load_ctx(g + 3)
            if exists(g + 1):
                spread_keys(g + 1)
            if exists(g + -2):
                store(g + -2)
            if exists(g):
                load_res(g)
        run_steps(sp, step)

    def tensor(pe):
        def transposes(h):
            at_least(pe, xn_ready, h.times(1, 1))
            at_least(pe, ctx_loaded[h.u], h.loads(1))
            at_least(pe, v_ready, h.times(1))
            for t in range(AT):
                nc.tensor.transpose(tp_v[:, t * P:(t + 1) * P], mem.xn[:, h.u, t, :], mem.ident[:])
            for t in range(AT):
                last = nc.tensor.transpose(tp_v[:, AN + t * P:AN + (t + 1) * P], mem.ctx[:, h.u, t, :], mem.ident[:])
            last.then_inc(tr_done, 1)

        def project_qk(h):
            at_least(pe, xcT_ready, h.times(1, 1))
            at_least(pe, q_placed, h.times(2))
            nc.tensor.matmul(qk_ps[:, 0:AN], mem.wq[:], mem.xcT[:, 0:AN], start=True, stop=True)
            nc.tensor.matmul(qk_ps[:, AN:2 * AN], mem.wk[:], mem.xcT[:, AN:2 * AN], start=True, stop=True)\
                .then_inc(qk_done, 1)

        def stack(h, n):
            if n == 0:
                at_least(pe, qk_hi, h.times(1, 1))
                at_least(pe, qk_lo, h.times(1, 1))
            elif n < 3:
                at_least(pe, k_staged, h.times(2, n))
            else:
                at_least(pe, q_placed, h.times(2, 1))
            i = 1 - n // 2
            for jj in range(2):
                out = qk_ps[:, jj * AN:(jj + 1) * AN]
                for part in range(2):
                    last = nc.tensor.matmul(out, mem.stack[:, i, part, 2 * (n % 2) + jj, :],
                                            mem.qk[:, part, i * AN:(i + 1) * AN], start=(part == 0), stop=(part == 1))
            last.then_inc(stacked, 1)

        def project_v(h):
            at_least(pe, xcT_ready, h.times(1, 1))
            for b in range(2 * AT):
                for h2 in range(2):
                    last = nc.tensor.matmul(tp_v[h2 * S:(h2 + 1) * S, b * 64:(b + 1) * 64],
                                            mem.xcT[:, AN + b * S:AN + (b + 1) * S],
                                            mem.wv[:, h2 * 64:(h2 + 1) * 64], start=True, stop=True)
            last.then_inc(v_done, 1)

        def score(g, t):
            at_least(pe, q_placed, g.times(2, 2))
            at_least(pe, k_spread[g.u], g.loads(HQ))
            for half in range(2):
                at_least(pe, shifted if layer else scores_read, g.times(2 * AT, 2 * t - 1 + half))
                for j in range(half * HJ // 2, (half + 1) * HJ // 2):
                    for b in range(2):
                        last = nc.tensor.matmul(scores[:, j * 256:(j + 1) * 256], mem.qst[:, g.u, j * AT + t, b, :],
                                                mem.kst[:, g.u, :, j, t * P + b * S:t * P + (b + 1) * S],
                                                start=(b == 0), stop=(b == 1))
                last.then_inc(scores_done, 1)

        def transpose_probs(g, t):
            at_least(pe, exp_done, g.times(AT, t + 1))
            for half in range(2):
                at_least(pe, pT_ready, g.times(2 * AT, 2 * t - 1 + half))
                for i in range(4):
                    hp = 4 * half + i
                    last = nc.tensor.transpose(pT_ps[:, hp * P:(hp + 1) * P],
                                               mem.probs[:, t, hp * P:(hp + 1) * P], mem.ident[:])
                last.then_inc(pT_done, 1)

        def values(g, t):
            at_least(pe, pT_ready, g.times(2 * AT, 2 * t + 2))
            at_least(pe, v_ready, g.times(1, 1))
            if t == 0:
                at_least(pe, o_ready, g.times(1))
            for hp in range(HP):
                col = t * 256 + (hp // 4) * P
                for b in range(2):
                    last = nc.tensor.matmul(o_ps[32 * (hp % 4):32 * (hp % 4) + 32, col + b * S:col + (b + 1) * S],
                                            mem.vst[:, g.u, (2 * t + b) * HP + hp, :],
                                            mem.probsT[:, hp // 4, (hp % 4) * P + b * S:(hp % 4) * P + (b + 1) * S],
                                            start=True, stop=True)
            last.then_inc(pv_done, 1)

        def back_o(g):
            at_least(pe, o_ready, g.times(1, 1))
            at_least(pe, added, g.times(1))
            for i in range(2 * AT):
                last = nc.tensor.transpose(tail[:, i * P:(i + 1) * P], mem.o_sb[:, i * P:(i + 1) * P], mem.ident[:])
            last.then_inc(oT_back, 1)

        def transpose_o(g):
            at_least(pe, normed, g.times(1, 1))
            for t in range(AT):
                last = nc.tensor.transpose(tail[:, t * P:(t + 1) * P], mem.onorm[:, t * P:(t + 1) * P], mem.ident[:])
            last.then_inc(oT_done, 1)

        def project_o(g):
            at_least(pe, oT_ready, g.times(1, 1))
            for t in range(AT):
                last = nc.tensor.matmul(tail[:, AN + t * P:AN + (t + 1) * P], mem.oT[:, t * P:(t + 1) * P],
                                        mem.wo[:], start=True, stop=True)
            last.then_inc(y_done, 1)

        pe.wait_ge(w_loaded, 16 * WEIGHTS)
        pe.wait_ge(stack_ready, layer + 1)
        if layer:
            pe.wait_ge(w_scaled, 2)
        def step(g):
            if exists(g + 1):
                project_qk(g + 1)
            if exists(g):
                score(g, 0)
            if exists(g + -2):
                transpose_o(g + -2)
            if exists(g + -1):
                transpose_probs(g + -1, 1)
            if exists(g + -2):
                project_o(g + -2)
            if exists(g + 1):
                stack(g + 1, 0)
                project_v(g + 1)
                stack(g + 1, 1)
            if exists(g + -1):
                values(g + -1, 1)
            if exists(g + 1):
                stack(g + 1, 2)
            if exists(g):
                score(g, 1)
            if exists(g + 1):
                stack(g + 1, 3)
            if exists(g):
                transpose_probs(g, 0)
            if exists(g + 2):
                transposes(g + 2)
            if exists(g + -1):
                back_o(g + -1)
            if exists(g):
                values(g, 0)
        run_steps(pe, step)

    def scalar(act):
        def copy_xcT(h):
            at_least(act, tr_done, h.times(1, 1))
            at_least(act, v_done, h.times(1))
            nc.scalar.copy(mem.xcT[:], tp_v[:]).then_inc(xcT_ready, 1)

        def split_high(h):
            at_least(act, qk_done, h.times(1, 1))
            at_least(act, stacked, h.times(4))
            if layer:
                nc.scalar.activation(mem.qk[:, 0, 0:AN], qk_ps[:, 0:AN], ACT.Identity, bias=mem.bqk[:, 0:1])
                nc.scalar.activation(mem.qk[:, 0, AN:2 * AN], qk_ps[:, AN:2 * AN], ACT.Identity,
                                     bias=mem.bqk[:, 1:2]).then_inc(qk_hi, 1)
            else:
                nc.scalar.copy(mem.qk[:, 0, :], qk_ps[:]).then_inc(qk_hi, 1)

        def stage_keys(h, n):
            at_least(act, stacked, h.times(4, n + 1))
            p = h + -1
            if n == 0 and not (isinstance(p.k, int) and p.k < 0):
                at_least(act, k_spread[p.u], p.loads(HQ))
            nc.scalar.copy(mem.kstage[:, 2 * n:2 * n + 2, :].rearrange("p j t -> p (j t)"), qk_ps[:]).then_inc(k_staged, 1)

        def exponentials(g, t):
            at_least(act, shifted, g.times(2 * AT, 2 * t + 2))
            nc.scalar.activation(mem.probs[:, t, :], mem.probs[:, t, :], ACT.Exp).then_inc(exp_done, 1)

        def copy_pT(g, t):
            at_least(act, pv_done, g.times(AT, t))
            for half in range(2):
                at_least(act, pT_done, g.times(2 * AT, 2 * t + half + 1))
                nc.scalar.copy(mem.probsT[:, half, :], pT_ps[:, half * 512:(half + 1) * 512]).then_inc(pT_ready, 1)

        def copy_o(g):
            at_least(act, pv_done, g.times(AT, AT))
            at_least(act, oT_back, g.times(1))
            nc.scalar.copy(mem.o_sb[:], o_ps[:]).then_inc(o_ready, 1)

        def copy_oT(g):
            at_least(act, oT_done, g.times(1, 1))
            at_least(act, y_done, g.times(1))
            nc.scalar.copy(mem.oT[:], tail[:, 0:AN]).then_inc(oT_ready, 1)

        act.wait_ge(w_loaded, 16 * WEIGHTS)
        nc.scalar.copy(mem.stack.rearrange("p i c j m -> p (i c j m)"), mem.stage[:, 0:4 * HJ * P]).then_inc(stack_ready, 1)
        def place_queries(h, n):
            at_least(act, stacked, h.times(4, 3 + n))
            at_least(act, scores_done, h.times(2 * AT, -2 * AT))
            src = qk_ps[:].rearrange("p (m b s) -> p m b s", b=2, s=S)
            for b in range(2):
                last = nc.scalar.copy(mem.qst[:, h.u, 2 * AT * n:2 * AT * (n + 1), b, b * S:(b + 1) * S],
                                      src[:, :, b, :])
            last.then_inc(q_placed, 1)

        def step(g):
            if exists(g + 1):
                split_high(g + 1)
            if exists(g + -2):
                copy_oT(g + -2)
            if exists(g + -1):
                copy_pT(g + -1, 1)
            if exists(g + 1):
                stage_keys(g + 1, 0)
                stage_keys(g + 1, 1)
            if exists(g) and layer:
                exponentials(g, 0)
            if exists(g + 1):
                place_queries(g + 1, 0)
            if exists(g) and not layer:
                exponentials(g, 0)
            if exists(g + -1):
                copy_o(g + -1)
            if exists(g + 1):
                place_queries(g + 1, 1)
            if exists(g):
                copy_pT(g, 0)
            if exists(g + 2):
                copy_xcT(g + 2)
            if exists(g):
                exponentials(g, 1)
        run_steps(act, step)

    def vector(dve):
        def layer_norm_stats(h):
            at_least(dve, x_loaded[h.u], h.loads(1))
            at_least(dve, xn_ready, h.times(1))
            for t in range(AT):
                last = nc.vector.bn_stats(mem.st[:, t, :], mem.x[:, h.u, t, :])
            last.then_inc(ln_chain, 1)
            dve.wait_ge(ln_chain, h.times(1, 1))
            stand_alone(dve, mem)
            for t in range(AT):
                last = nc.vector.bn_aggr(mem.mv[:, t, :], mem.st[:, t, :])
            last.then_inc(stats, 1)

        def split_low(h):
            at_least(dve, qk_hi, h.times(1, 1))
            hi = mem.qk[:, 0, :].bitcast(F32)
            if layer:
                for i in range(2):
                    part = slice(i * AN, (i + 1) * AN)
                    last = nc.vector.scalar_tensor_tensor(mem.qk[:, 1, part], qk_ps[:, part], mem.bqk[:, i:i + 1],
                                                          hi[:, part], ALU.add, ALU.subtract)
            else:
                last = nc.vector.tensor_tensor(mem.qk[:, 1, :], qk_ps[:], hi, ALU.subtract)
            last.then_inc(qk_lo, 1)

        def halves(tile, half):
            return tile.rearrange("p (k h s) -> p k h s", k=2, s=S)[:, half]

        def add_bias(g, t, half):
            at_least(dve, scores_done, g.times(2 * AT, 2 * t + half + 1))
            at_least(dve, pT_done, g.times(2 * AT, 2 * t - 2))
            cols = slice(half * 512, (half + 1) * 512)
            nc.vector.tensor_tensor(mem.probs[:, t, cols], scores[:, cols], mem.bias[:, cols], ALU.add)\
                .then_inc(scores_read, 1)

        def row_max(g, t, half):
            n = g.times(2 * AT, 2 * t + half + 1)
            if layer:
                at_least(dve, scores_done, n)
                at_least(dve, pT_done, g.times(2 * AT, 2 * t - 2))
                raw = halves(scores[:, :], half)
            else:
                dve.wait_ge(scores_read, n)
                raw = halves(mem.probs[:, t, :], half)
            nc.vector.tensor_reduce(mem.rowmax[:, t, half * H // 2:(half + 1) * H // 2], raw, AX.X, ALU.max)\
                .then_inc(max_ready, 1)

        def shift(g, t, half):
            dve.wait_ge(max_ready, g.times(2 * AT, 2 * t + half + 1))
            top = mem.rowmax[:, t, half * H // 2:(half + 1) * H // 2]
            nc.vector.tensor_tensor(halves(mem.probs[:, t, :], half), halves(scores[:, :], half),
                                    top.unsqueeze(2).to_broadcast([P, H // 2, S]), ALU.subtract).then_inc(shifted, 1)

        def place_values(h):
            at_least(dve, v_done, h.times(1, 1))
            at_least(dve, pv_done, h.times(AT, -AT))
            for h2 in range(2):
                part = slice(h2 * S, (h2 + 1) * S)
                src = tp_v[part, 0:AN].rearrange("p (b n d) -> p b n d", b=2 * AT, n=HP)
                to = mem.vst[part, h.u, :, h2 * DH:(h2 + 1) * DH].rearrange("p (b n) d -> p b n d", b=2 * AT)
                if layer:
                    bias = mem.bv[part, h2 * 64:(h2 + 1) * 64].rearrange("p (n d) -> p n d", n=HP)
                    last = nc.vector.tensor_tensor(to, src, bias.unsqueeze(1).to_broadcast([S, 2 * AT, HP, DH]), ALU.add)
                else:
                    last = nc.vector.tensor_copy(to, src)
            last.then_inc(v_ready, 1)

        def divide(g):
            at_least(dve, oT_back, g.times(1, 1))
            back = tail[:, :].rearrange("p (n k h d) -> p n k h d", n=AT * HP, k=2, h=2)
            nc.vector.reciprocal(mem.rden[:], back[:, :, 1, :, 0]).then_inc(rden_ready, 1)
            dve.wait_ge(rden_ready, g.times(1, 1))
            at_least(dve, oT_done, g.times(1))
            nc.vector.tensor_tensor(mem.onorm[:].rearrange("p (n h d) -> p n h d", n=AT * HP, h=2),
                                    back[:, :, 0, :, :], mem.rden[:].unsqueeze(3).to_broadcast([P, AT * HP, 2, DH]),
                                    ALU.mult).then_inc(normed, 1)

        def add_residual(g):
            at_least(dve, y_done, g.times(1, 1))
            if layer:
                at_least(dve, res_biased, g.times(1, 1 - AG))
            else:
                at_least(dve, res_loaded[g.u], g.loads(1))
            p = g + -2
            if not (isinstance(p.k, int) and p.k < 0):
                at_least(dve, stored[p.u], p.loads(1))
            nc.vector.tensor_tensor(mem.xnew[:, g.u].rearrange("p t d -> p (t d)"), tail[:, AN:2 * AN],
                                    mem.xres[:, g.u].rearrange("p t d -> p (t d)"), ALU.add).then_inc(added, 1)

        if layer:
            dve.wait_ge(w_loaded, 16 * WEIGHTS)
            nc.vector.tensor_scalar(mem.wq[:], mem.wq[:], float(DH) ** -0.5, None, ALU.mult).then_inc(w_scaled, 1)
            nc.vector.tensor_scalar(mem.bqk[:, 0:1], mem.bqk[:, 0:1], float(DH) ** -0.5, None, ALU.mult)\
                .then_inc(w_scaled, 1)
            dve.wait_ge(w_scaled, 2)
        def soften(g, t):
            for half in range(2):
                if not layer:
                    add_bias(g, t, half)
            for half in range(2):
                row_max(g, t, half)
            for half in range(2):
                if layer:
                    shift(g, t, half)

        def step(g):
            if exists(g + 2):
                layer_norm_stats(g + 2)
            if exists(g + 1):
                split_low(g + 1)
            if exists(g):
                soften(g, 0)
            if exists(g + 1):
                place_values(g + 1)
            if exists(g + -2):
                add_residual(g + -2)
            if exists(g):
                soften(g, 1)
            if exists(g + -1):
                divide(g + -1)
        run_steps(dve, step)

    def gpsimd(pool):
        def ln_scales(h):
            at_least(pool, stats, h.times(1, 1))
            at_least(pool, xn_ready, h.times(1))
            stand_alone(pool, mem)
            nc.gpsimd.tensor_scalar(mem.veps[:, 0:AT], mem.mv[:, 0:AT, 1], EPS, None, ALU.add).then_inc(pool_chain, 1)
            pool.wait_ge(pool_chain, h.times(1, 1))
            nc.gpsimd.tensor_tensor(mem.rstd[:, 0:AT], mem.veps[:, 0:AT], mem.minus_half[:, 0:AT], ALU.pow)\
                .then_inc(ln_scale, 1)

        def normalise(h):
            at_least(pool, ln_scale, h.times(1, 1))
            stand_alone(pool, mem)
            at_least(pool, tr_done, h.times(1, -1))
            stand_alone(pool, mem)
            for t in range(AT):
                last = nc.gpsimd.tensor_scalar(mem.xn[:, h.u, t, :], mem.x[:, h.u, t, :], mem.mv[:, t, 0:1],
                                               mem.rstd[:, t:t + 1], ALU.subtract, ALU.mult)
            last.then_inc(xn_ready, 1)

        def shift(g, t, half):
            at_least(pool, max_ready, g.times(2 * AT, 2 * t + half + 1))
            part = mem.probs[:, t, half * 512:(half + 1) * 512].rearrange("p (h s) -> p h s", s=S)
            top = mem.rowmax[:, t, half * H // 2:(half + 1) * H // 2]
            nc.gpsimd.tensor_tensor(part, part, top.unsqueeze(2).to_broadcast([P, H // 2, S]), ALU.subtract)\
                .then_inc(shifted, 1)

        def bias_residual(g):
            at_least(pool, res_loaded[g.u], g.loads(1))
            nc.gpsimd.tensor_tensor(mem.xres[:, g.u], mem.xres[:, g.u],
                                    mem.bo[:].unsqueeze(1).to_broadcast([P, AT, D]), ALU.add).then_inc(res_biased, 1)

        pool_chain = gp_chain
        if layer:
            pool.wait_ge(w_loaded, 16 * WEIGHTS)
        def step(g):
            if exists(g + 2):
                ln_scales(g + 2)
                normalise(g + 2)
            if exists(g + -1) and layer:
                bias_residual(g + -1)
            if exists(g) and not layer:
                for t in range(AT):
                    shift(g, t, 0)
                    shift(g, t, 1)
        run_steps(pool, step)

    gp_chain = sem("pool_chain")
    done = [(stored[u], 16 * (BASE + AG // 2)) for u in range(2)]
    return dict(sync=sync, tensor=tensor, scalar=scalar, vector=vector, gpsimd=gpsimd), done


def feed_forward(nc, ctx, mem, dram, layer, x_dram, out_dram, x_ready):
    L = f"f{layer}_"

    def sem(name):
        return ctx.enter_context(nc.semaphore(L + name))

    def sb(name, shape, dt=F32):
        return mem_ff(name, shape, dt)

    def mem_ff(name, shape, dt):
        if name not in mem.ff:
            mem.ff[name] = mem.ctx_stack.enter_context(nc.sbuf_tensor("ff_" + name, shape, dt))
        return mem.ff[name]

    nb, ncomb, topk, nlog, nexp = NB[layer], NCOMB[layer], TOPK[layer], LOGITS[layer], EXPERTS[layer]
    act_fn = ACT.Silu if layer else ACT.Gelu
    biased = layer == 0

    w_staged, w_hi, w_lo, w_misc, w_mult, stage_scaled = (sem(n) for n in ("w_staged", "w_hi", "w_lo", "w_misc", "w_mult", "stage_scaled"))
    x_loaded, res_loaded, stored = ([sem(f"{n}{u}") for u in range(2)] for n in ("x_loaded", "res_loaded", "stored"))
    stats, ln_scale, ln_chain, pool_chain, xn_ready = (sem(n) for n in ("stats", "ln_scale", "ln_chain", "pool_chain", "xn_ready"))
    xT_done, xT_ready, x_hi, x_lo = (sem(n) for n in ("xT_done", "xT_ready", "x_hi", "x_lo"))
    logits_done, route, route_exp, route_gate = (sem(n) for n in ("logits_done", "route", "route_exp", "route_gate"))
    comb_ready, combT_done, combT_ready = (sem(n) for n in ("comb_ready", "combT_done", "combT_ready"))
    gate_done, up_done, comb_done, act_done = (sem(n) for n in ("gate_done", "up_done", "comb_done", "act_done"))
    hidden, hidden_scaled, h_hi, h_lo, down_done = (sem(n) for n in ("hidden", "hidden_scaled", "h_hi", "h_lo", "down_done"))
    y_ready, y_back, added = (sem(n) for n in ("y_ready", "y_back", "added"))

    x = sb("x", [P, 2, FT, D])
    xres = sb("xres", [P, 2, FT, D])
    xnew = sb("xnew", [P, 2, FT, D])
    xn = sb("xn", [P, FT, D])
    xT = mem.o_sb
    xTh = sb("xTh", [P, 2, FN], F32R)
    xTl = sb("xTl", [P, 2, FN], F32R)
    combT = sb("combT", [ROWS, 2, FN], F32R)
    activated = mem.probs[:, 0, :].rearrange("p (n t) -> p n t", n=2)
    hid = mem.probs[:, 1, :].rearrange("p (n t) -> p n t", n=2)
    product, yT = (mem.probsT[:, 0, :], mem.xcT[:]), mem.probsT[:, 1, :]
    hh_hl = [sb("hh", [P, 2, FN], F32R), sb("hl", [P, 2, FN], F32R)]
    hh, hl = ([hh_hl[i][:, 0], hh_hl[i][:, 1], mem.kstage[:, 2 * i:2 * i + 2, :].rearrange("p j t -> p (j t)")]
              for i in range(2))
    z17 = sb("z", [P, FT, 32])
    zmax = sb("zmax", [P, FT])
    pexp = sb("pexp", [P, FT, NE])
    psum = sb("psum_z", [P, FT])
    top = sb("top", [P, FT, 8])
    idx = sb("idx", [P, FT, 8], U32)
    idxf = sb("idxf", [P, FT, 8])
    wsum = sb("wsum", [P, FT])
    onehot = sb("onehot", [P, FT, 4, NE])
    comb = sb("comb", [P, FT, 32])
    comb_h = sb("comb_h", [P, FT, 32], F32R)
    comb2 = sb("comb2", [P, FT, ROWS])

    gu01, gu23, misc0, y0, y1, tail = mem.banks
    gate_ps = [gu01[:, 0:512], gu01[:, 512:1024]]
    up_ps = [gu23[:, 0:512], gu23[:, 512:1024]]
    comb_ps = misc0
    y_ps = [y0, y1]

    xt = x_dram.rearrange("(g t p) d -> p g t d", t=FT, p=P)
    ot = out_dram.rearrange("(g t p) d -> p g t d", t=FT, p=P)

    def group_of(ap, turn):
        g = turn.times(1)
        if isinstance(g, int):
            return ap[:, g, :, :]
        return ap[:, bass.ds(g, 1), :, :].rearrange("p a t d -> p (a t) d")

    def has_comb(b):
        return b < ncomb

    def two_ahead(g):
        return not (isinstance(g.k, int) and 2 * g.k + g.u + 2 >= FG)

    def slots(engine, per_slot):
        def step(g, first, last):
            for b in range(nb):
                per_slot(g, b, first, last)
        run_groups(engine, FG, step)

    def before(g, b, n):
        return (g, b - n) if b >= n else (g + -1, b - n + nb)

    def count(g, b, extra=0):
        return g.times(nb, b + extra)

    LAG = 3

    def buffer_free(engine, g, b):
        at_least(engine, down_done, count(g, b, 1 - (LAG if b >= nb % LAG else nb % LAG)))

    last_turn = Turn(FG // 2 - 1, 1)
    SLOT_X, SLOT_LOGITS, SLOT_SHIFT, SLOT_EXP, SLOT_Y, SLOT_WEIGHTS, SLOT_COMB = 0, 1, 2, 3, 6, 5, min(nb - 1, 12)
    SLOT_STATS, SLOT_NORMALISE = ((3, 8), (12, 14))[nb > 12]
    ROUTE = ["largest", "shift", "sum_and_top", "inverse_and_places", "scale", "sum_of_top", "guard", "inverse_of_top",
             "weights", "put_weights", "gather", "gather_third", "high", "parts"]
    if topk == 2:
        ROUTE.remove("guard")
        ROUTE.remove("gather_third")
    STEPS = len(ROUTE) - 1
    SHIFTED = ROUTE.index("shift") + 1

    def sync(sp):
        def load(h):
            at_least(sp, xn_ready, h.times(1, -1))
            stand_alone(sp, mem)
            sp.dma_start(x[:, h.u], group_of(xt, h)).then_inc(x_loaded[h.u], 16)

        def load_res(h):
            at_least(sp, added, h.times(1, -1))
            stand_alone(sp, mem)
            sp.dma_start(xres[:, h.u], group_of(xt, h)).then_inc(res_loaded[h.u], 16)

        def store(h):
            at_least(sp, added, h.times(1, 1))
            stand_alone(sp, mem)
            sp.dma_start(group_of(ot, h), xnew[:, h.u]).then_inc(stored[h.u], 16)

        for s, v in x_ready:
            sp.wait_ge(s, v)
        sp.dma_start(mem.gateT[:, 0:nlog], dram[f"gateT{layer}"]).then_inc(w_misc, 16)
        if biased:
            sp.dma_start(mem.bgu[:], dram["bgu"]).then_inc(w_misc, 16)
            sp.dma_start(mem.mult[:], dram["mult"]).then_inc(w_misc, 16)
        z = Turn(0, 0)
        load(z)
        load(z + 1)
        for i, name in enumerate(("wg", "wu", "wd", "b2")[:4 if biased else 3]):
            at_least(sp, w_hi, i)
            stand_alone(sp, mem)
            at_least(sp, w_lo, i)
            stand_alone(sp, mem)
            if name == "b2":
                sp.dma_start(mem.stage[0:ROWS, 0:D], dram["b2"]).then_inc(w_staged, 16)
            else:
                sp.dma_start(mem.stage[:, 0:nb * P], dram[f"{name}{layer}"]).then_inc(w_staged, 16)
        sp.wait_ge(w_hi, arrays)
        sp.wait_ge(w_lo, arrays)
        sp.dma_start(mem.stage[0:ROWS, 0:ncomb * P], dram[f"sel{layer}"]).then_inc(w_staged, 16)

        def step(g, first, last):
            if two_ahead(g):
                load(g + 2)
            load_res(g)
            if not first:
                store(g + -1)
        run_groups(sp, FG, step)
        store(last_turn)

    arrays = 4 if biased else 3

    def tensor(pe):
        def three(out, w, cols, hi, lo, start, stop):
            nc.tensor.matmul(out, w[0][:, cols, :], hi, start=start, stop=False)
            nc.tensor.matmul(out, w[0][:, cols, :], lo, start=False, stop=False)
            return nc.tensor.matmul(out, w[1][:, cols, :], hi, start=False, stop=stop)

        def gate_up(g, b):
            if b == 0:
                at_least(pe, x_hi, g.times(1, 1))
                at_least(pe, x_lo, g.times(1, 1))
            n = b % 2 if nb % 2 == 0 else (b + g.u) % 2
            at_least(pe, act_done, count(g, b, -1))
            three(gate_ps[n], mem.wg, b, xTh[:, g.u], xTl[:, g.u], True, True).then_inc(gate_done, 1)
            at_least(pe, hidden, count(g, b, -1))
            three(up_ps[n], mem.wu, b, xTh[:, g.u], xTl[:, g.u], True, True).then_inc(up_done, 1)

        def router_weights(g, b):
            if b == 0:
                at_least(pe, combT_ready, g.times(1, 1))
            at_least(pe, hidden, count(g, b))
            nc.tensor.matmul(comb_ps[:, :], mem.sel[:, b, :], combT[:, g.u], start=True, stop=True)\
                .then_inc(comb_done, 1)

        def down(g, b):
            n = b % LAG
            at_least(pe, h_hi, count(g, b, 1))
            at_least(pe, h_lo, count(g, b, 1))
            if b == 0:
                at_least(pe, y_ready, g.times(1, -1))
                if biased:
                    nc.tensor.matmul(y_ps[g.u][:, :], mem.b2[0][:], combT[:, g.u], start=True, stop=False)
                    nc.tensor.matmul(y_ps[g.u][:, :], mem.b2[1][:], combT[:, g.u], start=False, stop=False)
            three(y_ps[g.u][:, :], mem.wd, b, hh[n], hl[n], b == 0 and not biased, b == nb - 1)\
                .then_inc(down_done, 1)

        def back_y(g):
            at_least(pe, y_ready, g.times(1, 1))
            at_least(pe, route, g.times(STEPS, 2 * STEPS + SHIFTED))
            for t in range(FT):
                last = nc.tensor.transpose(tail[:, t * P:(t + 1) * P], yT[:, t * P:(t + 1) * P], mem.ident[:])
            last.then_inc(y_back, 1)

        def back_last_but_one(g):
            at_least(pe, y_ready, g.times(1, 1))
            for t in range(FT):
                last = nc.tensor.transpose(tail[:, t * P:(t + 1) * P], yT[:, t * P:(t + 1) * P], mem.ident[:])
            last.then_inc(y_back, 1)

        def transpose_x(h):
            at_least(pe, xn_ready, h.times(1, 1))
            at_least(pe, combT_ready, h.times(1))
            for t in range(FT):
                last = nc.tensor.transpose(tail[:, t * P:(t + 1) * P], xn[:, t, :], mem.ident[:])
            last.then_inc(xT_done, 1)

        def logits(h):
            at_least(pe, xT_ready, h.times(1, 1))
            for t in range(FT):
                last = nc.tensor.matmul(tail[:, t * 32:t * 32 + nlog], xT[:, t * P:(t + 1) * P],
                                        mem.gateT[:, 0:nlog], start=True, stop=True)
            last.then_inc(logits_done, 1)

        def transpose_comb(h):
            at_least(pe, added, h.times(1, -1))
            at_least(pe, comb_ready, h.times(1, 1))
            stand_alone(pe, mem)
            for t in range(FT):
                last = nc.tensor.transpose(tail[0:ROWS, t * P:(t + 1) * P], comb2[:, t, :], mem.ident[:])
            last.then_inc(combT_done, 1)

        pe.wait_ge(w_misc, 16 * (3 if biased else 1))
        z = Turn(0, 0)
        transpose_x(z)
        logits(z)
        transpose_comb(z)
        pe.wait_ge(w_hi, arrays + 1)
        pe.wait_ge(w_lo, arrays)

        def slot(g, b, first, last):
            gate_up(g, b)
            if not (first and b < LAG):
                down(*before(g, b, LAG))
            if has_comb(b):
                router_weights(g, b)
            if b == SLOT_Y and not first:
                if last:
                    back_last_but_one(g + -1)
                else:
                    back_y(g + -1)
            if not last:
                if b == SLOT_X:
                    transpose_x(g + 1)
                if b == SLOT_LOGITS:
                    logits(g + 1)
                if b == SLOT_COMB:
                    transpose_comb(g + 1)
        slots(pe, slot)
        for n in range(LAG, 0, -1):
            down(last_turn, nb - n)
        at_least(pe, y_ready, last_turn.times(1, 1))
        at_least(pe, added, last_turn.times(1))
        for t in range(FT):
            last = nc.tensor.transpose(tail[:, t * P:(t + 1) * P], yT[:, t * P:(t + 1) * P], mem.ident[:])
        last.then_inc(y_back, 1)

    def scalar(act):
        def activate(g, b):
            n = (b + g.u) % 2
            at_least(act, gate_done, count(g, b, 1))
            at_least(act, hidden, count(g, b, -1))
            if biased:
                nc.scalar.activation(activated[:, n], gate_ps[n], act_fn, bias=mem.bgu[:, 0, b:b + 1])\
                    .then_inc(act_done, 1)
            else:
                nc.scalar.activation(activated[:, n], gate_ps[n], act_fn).then_inc(act_done, 1)

        def high(g, b):
            n = (b + g.u) % 2
            at_least(act, hidden, count(g, b, 1))
            buffer_free(act, g, b)
            nc.scalar.copy(hh[b % LAG], hid[:, n]).then_inc(h_hi, 1)

        def copy_y(g):
            at_least(act, down_done, g.times(nb, nb))
            at_least(act, y_back, g.times(1))
            nc.scalar.copy(yT, y_ps[g.u][:, :]).then_inc(y_ready, 1)

        def copy_xT(h):
            at_least(act, xT_done, h.times(1, 1))
            at_least(act, logits_done, h.times(1))
            at_least(act, x_lo, h.times(1))
            nc.scalar.copy(xT[:], tail[:, :]).then_inc(xT_ready, 1)

        def high_x(h):
            act.wait_ge(xT_ready, h.times(1, 1))
            at_least(act, up_done, h.times(nb, -nb))
            nc.scalar.copy(xTh[:, h.u], xT[:]).then_inc(x_hi, 1)

        def route_exponentials(h):
            at_least(act, route, h.times(STEPS, SHIFTED))
            nc.scalar.activation(pexp[:, :, 0:nexp], z17[:, :, 0:nexp], ACT.Exp).then_inc(route_exp, 1)

        def shared_gate(h):
            at_least(act, route, h.times(STEPS, SHIFTED))
            nc.scalar.activation(comb[:, :, NE:NE + 1], z17[:, :, NE:NE + 1], ACT.Tanh, scale=0.5)\
                .then_inc(route_gate, 1)

        def copy_combT(h):
            at_least(act, combT_done, h.times(1, 1))
            at_least(act, down_done, h.times(nb, 1 - 2 * nb))
            at_least(act, comb_done, h.times(ncomb, -ncomb))
            nc.scalar.copy(combT[:, h.u], tail[0:ROWS, :]).then_inc(combT_ready, 1)

        z = Turn(0, 0)
        copy_xT(z)
        high_x(z)
        route_exponentials(z)
        if layer:
            shared_gate(z)
        copy_combT(z)
        for i in range(arrays):
            act.wait_ge(w_staged, 16 * (i + 1))
            if i == 2 and biased:
                act.wait_ge(stage_scaled, 1)
            if i == 3:
                nc.scalar.copy(mem.b2[0][:], mem.stage[0:ROWS, 0:D]).then_inc(w_hi, 1)
            else:
                w = (mem.wg, mem.wu, mem.wd)[i]
                nc.scalar.copy(w[0][:, 0:nb, :].rearrange("p b f -> p (b f)"), mem.stage[:, 0:nb * P]).then_inc(w_hi, 1)
        act.wait_ge(w_staged, 16 * (arrays + 1))
        nc.scalar.copy(mem.sel[:, 0:ncomb, :].rearrange("r b f -> r (b f)"), mem.stage[0:ROWS, 0:ncomb * P])\
            .then_inc(w_hi, 1)

        def slot(g, b, first, last):
            activate(g, b)
            if not (first and b == 0):
                high(*before(g, b, 1))
            if b == SLOT_Y - 1 and not first:
                copy_y(g + -1)
            if not last:
                if b == SLOT_X:
                    copy_xT(g + 1)
                if b == SLOT_X + 1:
                    high_x(g + 1)
                if b == SLOT_EXP:
                    route_exponentials(g + 1)
                if b == SLOT_EXP + 1 and layer:
                    shared_gate(g + 1)
                if b == SLOT_COMB:
                    copy_combT(g + 1)
        slots(act, slot)
        high(last_turn, nb - 1)
        copy_y(last_turn)

    def vector(dve):
        def layer_norm_stats(h):
            at_least(dve, x_loaded[h.u], h.loads(1))
            at_least(dve, ln_scale, h.times(1))
            for t in range(FT):
                last = nc.vector.bn_stats(mem.st[:, t, :], x[:, h.u, t, :])
            last.then_inc(ln_chain, 1)
            dve.wait_ge(ln_chain, h.times(1, 1))
            stand_alone(dve, mem)
            for t in range(FT):
                last = nc.vector.bn_aggr(mem.mv[:, t, :], mem.st[:, t, :])
            last.then_inc(stats, 1)

        def normalise(h):
            at_least(dve, ln_scale, h.times(1, 1))
            at_least(dve, xT_done, h.times(1))
            for t in range(FT):
                last = nc.vector.tensor_scalar(xn[:, t, :], x[:, h.u, t, :], mem.mv[:, t, 0:1],
                                               mem.rstd[:, t:t + 1], ALU.subtract, ALU.mult)
            last.then_inc(xn_ready, 1)

        def route_step(h, n):
            name = ROUTE[n]

            def rows(column, width):
                return column.to_broadcast([P, FT, width])

            if name == "largest":
                at_least(dve, logits_done, h.times(1, 1))
            if name == "shift":
                at_least(dve, route_exp, h.times(1))
            if name == "sum_and_top":
                at_least(dve, route_exp, h.times(1, 1))
            if name == "gather" and layer:
                at_least(dve, route_gate, h.times(1, 1))
            if name == "parts":
                at_least(dve, combT_done, h.times(1))
            at_least(dve, route, h.times(STEPS, n))
            stand_alone(dve, mem)

            raw = tail[:, 0:FT * 32].rearrange("p (t e) -> p t e", t=FT)
            if name == "largest":
                last = nc.vector.tensor_reduce(zmax[:], raw[:, :, 0:nexp], AX.X, ALU.max)
            elif name == "shift":
                if layer:
                    nc.vector.tensor_copy(z17[:, :, NE:NE + 1], raw[:, :, NE:NE + 1])
                last = nc.vector.tensor_tensor(z17[:, :, 0:nexp], raw[:, :, 0:nexp], rows(zmax[:].unsqueeze(2), nexp),
                                               ALU.subtract)
            elif name == "sum_and_top":
                for t in range(FT):
                    nc.vector.max(top[:, t, :], pexp[:, t, :])
                last = nc.vector.tensor_reduce(psum[:], pexp[:, :, 0:nexp], AX.X, ALU.add)
            elif name == "inverse_and_places":
                for t in range(FT):
                    nc.vector.max_index(idx[:, t, :], top[:, t, :], pexp[:, t, :])
                last = nc.vector.reciprocal(psum[:], psum[:])
            elif name == "scale":
                nc.vector.tensor_copy(idxf[:], idx[:])
                last = nc.vector.tensor_tensor(top[:, :, 0:topk], top[:, :, 0:topk], rows(psum[:].unsqueeze(2), topk), ALU.mult)
            elif name == "sum_of_top":
                for k in range(topk):
                    nc.vector.tensor_tensor(onehot[:, :, k, :], mem.iota[:].unsqueeze(1).to_broadcast([P, FT, NE]),
                                            rows(idxf[:, :, k:k + 1], NE), ALU.is_equal)
                last = nc.vector.tensor_reduce(wsum[:], top[:, :, 0:topk], AX.X, ALU.add)
            elif name == "guard":
                last = nc.vector.tensor_scalar(wsum[:], wsum[:], 1e-20, None, ALU.add)
            elif name == "inverse_of_top":
                last = nc.vector.reciprocal(wsum[:], wsum[:])
            elif name == "weights":
                last = nc.vector.tensor_tensor(top[:, :, 0:topk], top[:, :, 0:topk], rows(wsum[:].unsqueeze(2), topk), ALU.mult)
            elif name == "put_weights":
                for k in range(topk):
                    last = nc.vector.tensor_tensor(onehot[:, :, k, :], onehot[:, :, k, :], rows(top[:, :, k:k + 1], NE),
                                                   ALU.mult)
            elif name == "gather":
                if layer:
                    nc.vector.tensor_scalar(comb[:, :, NE:NE + 1], comb[:, :, NE:NE + 1], 1.0, 0.5, ALU.add, ALU.mult)
                last = nc.vector.tensor_tensor(comb[:, :, 0:nexp], onehot[:, :, 0, 0:nexp], onehot[:, :, 1, 0:nexp], ALU.add)
            elif name == "gather_third":
                last = nc.vector.tensor_tensor(comb[:, :, 0:nexp], comb[:, :, 0:nexp], onehot[:, :, 2, 0:nexp], ALU.add)
            elif name == "high":
                last = nc.vector.tensor_copy(comb_h[:], comb[:])
            elif name == "parts":
                nc.vector.tensor_copy(comb2[:, :, 0:32], comb_h[:].bitcast(F32))
                nc.vector.tensor_tensor(comb2[:, :, 32:64], comb[:], comb_h[:].bitcast(F32), ALU.subtract)\
                    .then_inc(comb_ready, 1)
                return
            last.then_inc(route, 1)

        def multiply(g, b, last):
            n = (b + g.u) % 2
            at_least(dve, up_done, count(g, b, 1))
            at_least(dve, act_done, count(g, b, 1))
            at_least(dve, h_lo, count(g, b, -1))
            if has_comb(b):
                if biased:
                    nc.vector.scalar_tensor_tensor(product[n], up_ps[n], mem.bgu[:, 1, b:b + 1], activated[:, n],
                                                   ALU.add, ALU.mult).then_inc(hidden_scaled, 1)
                else:
                    nc.vector.tensor_tensor(product[n], up_ps[n], activated[:, n], ALU.mult)\
                        .then_inc(hidden_scaled, 1)
                if not last:
                    beside(g, b, 0)
                dve.wait_ge(hidden_scaled, g.times(ncomb, b + 1))
                at_least(dve, comb_done, g.times(ncomb, b + 1))
                nc.vector.tensor_tensor(hid[:, n], product[n], comb_ps[:, :], ALU.mult).then_inc(hidden, 1)
            else:
                nc.vector.scalar_tensor_tensor(hid[:, n], up_ps[n], mem.bgu[:, 1, b:b + 1], activated[:, n],
                                               ALU.add, ALU.mult).then_inc(hidden, 1)

        def beside(g, b, place):
            if b == SLOT_SHIFT:
                route_step(g + 1, place)
            n = 2 * (b - SLOT_WEIGHTS) + place
            if 0 <= n < len(ROUTE) - SHIFTED:
                route_step(g + 1, SHIFTED + n)

        def add_residual(g):
            at_least(dve, y_back, g.times(1, 1))
            at_least(dve, res_loaded[g.u], g.loads(1))
            p = g + -2
            if not (isinstance(p.k, int) and p.k < 0):
                at_least(dve, stored[p.u], p.loads(1))
            nc.vector.tensor_tensor(xnew[:, g.u].rearrange("p t d -> p (t d)"), tail[:, :],
                                    xres[:, g.u].rearrange("p t d -> p (t d)"), ALU.add).then_inc(added, 1)

        nc.vector.memset(comb[:], 0.0).then_inc(w_mult, 1)
        nc.vector.memset(pexp[:], -1.0).then_inc(w_mult, 1)
        dve.wait_ge(w_mult, 2)
        if layer == 0:
            nc.vector.memset(comb[:, :, NE - 1:NE], 1.0).then_inc(w_mult, 1)
            dve.wait_ge(w_mult, 3)
        dve.wait_ge(w_misc, 16 * (3 if biased else 1))
        z = Turn(0, 0)
        layer_norm_stats(z)
        normalise(z)
        layer_norm_stats(z + 1)
        for n in range(len(ROUTE)):
            route_step(z, n)
        normalise(z + 1)
        for i in range(arrays):
            dve.wait_ge(w_staged, 16 * (i + 1))
            if i == 2 and biased:
                staged = mem.stage[:, 0:nb * P].rearrange("p (b f) -> p b f", b=nb)
                nc.vector.tensor_tensor(staged, staged, mem.mult[:].unsqueeze(2).to_broadcast([P, nb, P]), ALU.mult)\
                    .then_inc(stage_scaled, 1)
            dve.wait_ge(w_hi, i + 1)
            if i == 3:
                nc.vector.tensor_tensor(mem.b2[1][:], mem.stage[0:ROWS, 0:D], mem.b2[0].bitcast(F32)[:], ALU.subtract)\
                    .then_inc(w_lo, 1)
            else:
                w = (mem.wg, mem.wu, mem.wd)[i]
                nc.vector.tensor_tensor(w[1][:, 0:nb, :].rearrange("p b f -> p (b f)"), mem.stage[:, 0:nb * P],
                                        w[0].bitcast(F32)[:, 0:nb, :].rearrange("p b f -> p (b f)"), ALU.subtract)\
                    .then_inc(w_lo, 1)

        def slot(g, b, first, last):
            multiply(g, b, last)
            if not last:
                beside(g, b, 1)
            if b == SLOT_Y and not first:
                add_residual(g + -1)
            if two_ahead(g):
                if b == SLOT_STATS:
                    layer_norm_stats(g + 2)
                if b == SLOT_NORMALISE:
                    normalise(g + 2)
        slots(dve, slot)
        add_residual(last_turn)

    def gpsimd(pool):
        def ln_scales(h):
            at_least(pool, stats, h.times(1, 1))
            at_least(pool, xn_ready, h.times(1))
            stand_alone(pool, mem)
            nc.gpsimd.tensor_scalar(mem.veps[:], mem.mv[:, :, 1], EPS, None, ALU.add).then_inc(pool_chain, 1)
            pool.wait_ge(pool_chain, h.times(1, 1))
            nc.gpsimd.tensor_tensor(mem.rstd[:], mem.veps[:], mem.minus_half[:], ALU.pow).then_inc(ln_scale, 1)

        def low_x(h):
            at_least(pool, x_hi, h.times(1, 1))
            nc.gpsimd.tensor_tensor(xTl[:, h.u], xT[:], xTh.bitcast(F32)[:, h.u], ALU.subtract).then_inc(x_lo, 1)

        def low(g, b):
            n = (b + g.u) % 2
            at_least(pool, h_hi, count(g, b, 1))
            buffer_free(pool, g, b)
            nc.gpsimd.tensor_tensor(hl[b % LAG], hid[:, n], hh[b % LAG].bitcast(F32), ALU.subtract).then_inc(h_lo, 1)

        z = Turn(0, 0)
        ln_scales(z)
        ln_scales(z + 1)
        low_x(z)

        def slot(g, b, first, last):
            low(g, b)
            if not last:
                if b == SLOT_X + 1:
                    low_x(g + 1)
            if b == SLOT_STATS and two_ahead(g):
                ln_scales(g + 2)
        slots(pool, slot)

    done = [(stored[u], 16 * (FG // 2)) for u in range(2)]
    return dict(sync=sync, tensor=tensor, scalar=scalar, vector=vector, gpsimd=gpsimd), done


def decoder_kernel(nc, dram, out):
    with ExitStack() as ctx:
        mem = Memory(nc, ctx)
        mem.ff, mem.ctx_stack = {}, ctx
        mem.tick = ctx.enter_context(nc.semaphore("tick"))
        ready = ctx.enter_context(nc.semaphore("ready"))
        vzero = ctx.enter_context(nc.semaphore("vzero"))
        x1, x2, x3 = (dram[n] for n in ("x1", "x2", "x3"))
        setup = constants(nc, ctx, mem, dram, {"ready": ready, "vzero": vzero})
        named = {}

        def shared(name):
            if name not in named:
                named[name] = ctx.enter_context(nc.semaphore("attn_" + name))
            return named[name]

        a0, x1_ready = attention(nc, shared, mem, dram, 0, dram["x"], x1, None)
        f0, x2_ready = feed_forward(nc, ctx, mem, dram, 0, x1, x2, x1_ready)
        a1, x3_ready = attention(nc, shared, mem, dram, 1, x2, x3, x2_ready)
        f1, out_ready = feed_forward(nc, ctx, mem, dram, 1, x3, out, x3_ready)
        block = ctx.enter_context(nc.Block())

        def phases(engine, name):
            setup[name](engine)
            engine.wait_ge(ready, 3)
            for part in (a0, f0, a1, f1):
                part[name](engine)

        @block.sync
        def _(sp):
            phases(sp, "sync")
            for s, v in out_ready:
                sp.wait_ge(s, v)

        @block.tensor
        def _(pe):
            phases(pe, "tensor")

        @block.scalar
        def _(act):
            phases(act, "scalar")

        @block.vector
        def _(dve):
            phases(dve, "vector")

        @block.gpsimd
        def _(pool):
            phases(pool, "gpsimd")


def bucket_table():
    rel = np.arange(S)[None, :] - np.arange(S)[:, None]
    half, exact, far = NBUCKET // 2, NBUCKET // 4, 128
    dist = np.abs(rel)
    log = np.log((np.maximum(dist, 1) / exact).astype(np.float32)) / np.float32(math.log(far / exact))
    large = np.minimum(exact + (log * (half - exact)).astype(np.int32), half - 1)
    bucket = (rel > 0) * half + np.where(dist < exact, dist, large)
    return (np.arange(NBUCKET)[:, None] == bucket.reshape(1, -1)).astype(np.float32)


def stacking():
    m = np.zeros((P, 2, 2, HJ, P), np.float32)
    for h4 in range(HQ):
        for c in range(NC):
            for d in range(DH):
                for j in range(HJ):
                    row, col = h4 * 32 + d * HJ + j, h4 * 32 + c * DH + d
                    m[row, 0, c % 2, j, col] = 1.0
                    m[row, 1, c // 2, j, col] = 1.0
    return m.reshape(P, -1)


def selection(layer):
    sel = np.zeros((ROWS, NCOMB[layer], P), np.float32)
    for b in range(NCOMB[layer]):
        for f in range(P):
            e = b if layer == 0 else (2 * b + f // 64 if b < 8 else NE)
            sel[e, b, f] = sel[32 + e, b, f] = 1.0
    return sel


def layout(inp):
    a = {k: np.asarray(v) for k, v in inp.items()}
    c = np.ascontiguousarray

    def qk_order(w):
        return c(w.reshape(-1, HJ, HQ, DH).transpose(0, 2, 3, 1).reshape(-1, D))

    def heads_last(w):
        return w.transpose(1, 0, 2).reshape(D, H * DH)

    def pairs_apart(w):
        return c(w.reshape(-1, HP, 2, DH).transpose(0, 2, 1, 3).reshape(-1, D))

    t = {"x": a["x"].reshape(TOK, D), "ctx": a["ctx_1024"].reshape(TOK, D)}
    t["wq0"], t["wk0"] = qk_order(a["L0_xattn_wq"]), qk_order(a["L0_xattn_wk"])
    t["wv0"], t["wo0"] = pairs_apart(a["L0_xattn_wv"]), a["L0_xattn_wo"]
    t["rel_bias"] = a["L0_xattn_rel_bias"]
    t["wq1"], t["wk1"] = qk_order(heads_last(a["L1_xattn_wq"])), qk_order(heads_last(a["L1_xattn_wk"]))
    t["wv1"], t["wo1"] = pairs_apart(heads_last(a["L1_xattn_wv"])), a["L1_xattn_wo"]
    t["bqk"] = np.stack([qk_order(a[n].reshape(1, D))[0] for n in ("L1_xattn_bq", "L1_xattn_bk")], 1)
    t["bv"], t["bo"] = pairs_apart(a["L1_xattn_bv"].reshape(1, D)), a["L1_xattn_bo"].reshape(1, D)
    F = 128
    fc1, sfc1 = a["L0_ffn_fc1_w"], a["L0_ffn_s_fc1_w"].reshape(2, 2, F, D)
    up = np.concatenate([fc1[:, :F], sfc1[0]])
    gate = np.concatenate([fc1[:, F:], sfc1[1]])
    t["wu0"], t["wg0"] = (w.transpose(2, 0, 1).reshape(D, -1) for w in (up, gate))
    down = np.concatenate([a["L0_ffn_fc2_w"], a["L0_ffn_s_fc2_w"].reshape(D, 2, F).transpose(1, 0, 2)])
    t["wd0"] = down.transpose(2, 0, 1).reshape(F, -1)
    b1, sb1 = a["L0_ffn_fc1_b"], a["L0_ffn_s_fc1_b"].reshape(2, 2, F)
    bias_gate, bias_up = np.concatenate([b1[:, F:], sb1[1]]), np.concatenate([b1[:, :F], sb1[0]])
    t["bgu"] = np.stack([bias_gate.T, bias_up.T], 1)
    t["mult"] = np.concatenate([a["L0_ffn_geglu_mult"], a["L0_ffn_s_geglu_mult"].reshape(2, F)]).T
    b2 = np.zeros((2, 32, D), np.float32)
    b2[:, :15], b2[:, 15] = a["L0_ffn_fc2_b"], a["L0_ffn_s_fc2_b"]
    t["b2"] = b2.reshape(ROWS, D)
    t["gateT0"] = a["L0_ffn_gate_w"].T
    gu = a["L1_ffn_w_gate_up"].reshape(8, 2, D, 2, 64).transpose(3, 2, 0, 1, 4).reshape(2, D, 8 * P)
    def filled(w):
        return np.concatenate([w, np.zeros((3 * P - w.shape[0], D), np.float32)])
    t["wg1"] = np.concatenate([gu[0], filled(a["L1_ffn_shared_w_gate"]).T], 1)
    t["wu1"] = np.concatenate([gu[1], filled(a["L1_ffn_shared_w_up"]).T], 1)
    d1 = a["L1_ffn_w_down"].reshape(8, P, D).transpose(1, 0, 2).reshape(P, -1)
    sd = filled(a["L1_ffn_shared_w_down"].T).reshape(3, P, D).transpose(1, 0, 2).reshape(P, -1)
    t["wd1"] = np.concatenate([d1, sd], 1)
    t["gateT1"] = np.concatenate([a["L1_ffn_gate_w"], a["L1_ffn_shared_gate_w"]]).T
    t["ident"] = np.eye(P, dtype=np.float32)
    t["iota"] = np.tile(np.arange(NE, dtype=np.float32), (P, 1))
    t["buckets"] = bucket_table()
    t["stack"] = stacking()
    t["sel0"], t["sel1"] = selection(0).reshape(ROWS, -1), selection(1).reshape(ROWS, -1)
    return {k: c(v) for k, v in t.items()}


def kernel(**inputs):
    import concourse.bacc as bacc
    from concourse.bass_utils import run_bass_kernel_spmd

    nc = bacc.Bacc("TRN2", target_bir_lowering=False, num_devices=1)
    arrays, dram = {}, {}
    for name, a in layout(inputs).items():
        arrays[f"in_{name}"] = a
        dram[name] = nc.dram_tensor(f"in_{name}", a.shape, mybir.dt.from_np(a.dtype), kind="ExternalInput").ap()
    for name, shape in (("x1", (TOK, D)), ("x2", (TOK, D)), ("x3", (TOK, D)), ("bias_rows", (H, S * S))):
        dram[name] = nc.dram_tensor(name, shape, F32, kind="Internal").ap()
    out = nc.dram_tensor("out", (TOK, D), F32, kind="ExternalOutput").ap()
    decoder_kernel(nc, dram, out)
    result = run_bass_kernel_spmd(nc, [arrays], core_ids=[0])
    return result.results[0]["out"].reshape(B, S, D)
```

```python
import math
from contextlib import ExitStack

import numpy as np

import concourse.bass as bass
from concourse import mybir

ALU = mybir.AluOpType
ACT = mybir.ActivationFunctionType
AX = mybir.AxisListType
F32 = mybir.dt.float32
F32R = mybir.dt.float32r
U32 = mybir.dt.uint32

P = 128
B, S, D = 128, 64, 128
H, DH = 16, 8
HQ, HJ = 4, 4
NC = 4
TOK = B * S
TILES = TOK // P
HP = H // 2
AT = 2
AN = AT * P
AG = TILES // AT
FT = 4
FN = FT * P
FG = TILES // FT
NE = 16
ROWS = 64
EPS = 1e-5
NB = (17, 11)
NCOMB = (15, 11)
TOPK = (3, 2)
LOGITS = (15, 17)
EXPERTS = (15, 16)
NBUCKET = 32


def add(k, n):
    return k + n if n else k


def at_least(engine, sem, value):
    if isinstance(value, int) and value <= 0:
        return
    engine.wait_ge(sem, value)


def stand_alone(engine, mem):
    engine.sem_inc(mem.tick, 1)


class Turn:

    def __init__(self, k, u):
        self.k, self.u = k, u

    def __add__(self, n):
        v = self.u + n
        return Turn(add(self.k, v // 2), v % 2)

    def times(self, per, extra=0):
        return add(self.k * (2 * per), per * self.u + extra)

    def loads(self, per):
        return add(self.k * (16 * per), 16 * per)


def run_groups(engine, groups, emit):
    for k in range(2):
        emit(Turn(k, 0), k == 0, False)
        emit(Turn(k, 1), False, False)
    with engine.Fori(2, groups // 2 - 1) as k:
        emit(Turn(k, 0), False, False)
        emit(Turn(k, 1), False, False)
    k = groups // 2 - 1
    emit(Turn(k, 0), False, False)
    emit(Turn(k, 1), False, True)


class Memory:

    def __init__(self, nc, ctx):
        def sb(name, shape, dt=F32):
            return ctx.enter_context(nc.sbuf_tensor(name, shape, dt))

        self.ident = sb("ident", [P, P])
        self.iota = sb("iota", [P, NE])
        self.minus_half = sb("minus_half", [P, FT])
        self.bias = sb("bias", [P, H * S])
        self.rel = sb("rel", [NBUCKET, H])
        self.buckets = sb("buckets", [NBUCKET, 2 * S - 1])
        self.stage = sb("stage", [P, max(NB) * P])
        self.wq, self.wk, self.wv, self.wo = (sb(n, [P, D]) for n in ("wq", "wk", "wv", "wo"))
        self.bqk = sb("bqk", [P, 2])
        self.bv, self.bo = sb("bv", [P, D]), sb("bo", [P, D])
        self.x = sb("x", [P, 2, AT, D])
        self.ctx = sb("ctx", [P, 2, AT, D])
        self.xn = sb("xn", [P, 2, AT, D])
        self.xres = sb("xres", [P, 2, AT, D])
        self.xnew = sb("xnew", [P, 2, AT, D])
        self.st = sb("st", [P, FT, 6])
        self.mv = sb("mv", [P, FT, 2])
        self.veps = sb("veps", [P, FT])
        self.rstd = sb("rstd", [P, FT])
        self.xcT = sb("xcT", [P, 2 * AN])
        self.qk = sb("qk", [P, 2, 2 * AN], F32R)
        self.kstage = sb("kstage", [P, HJ, AN], F32R)
        self.qst = sb("qst", [P, 2, HJ * AT, 2, P], F32R)
        self.kst = sb("kst", [P, 2, HQ, HJ, AN], F32R)
        self.vst = sb("vst", [P, 2, 2 * AT * HP, 32])
        self.probs = sb("probs", [P, 2, H * S])
        self.rowmax = sb("rowmax", [P, 2, H])
        self.probsT = sb("probsT", [P, 2, 4 * P])
        self.o_sb = sb("o_sb", [P, 2 * AN])
        self.rden = sb("rden", [P, AT * HP, 2])
        self.onorm = sb("onorm", [P, AN])
        self.oT = sb("oT", [P, AN])
        nb = max(NB)
        self.wg = [sb(f"wg{i}", [P, nb, P], F32R) for i in range(2)]
        self.wu = [sb(f"wu{i}", [P, nb, P], F32R) for i in range(2)]
        self.wd = [sb(f"wd{i}", [P, nb, P], F32R) for i in range(2)]
        self.b2 = [sb(f"b2{i}", [ROWS, D], F32R) for i in range(2)]
        self.stack = self.wd[1][:, 0:4 * HJ, :].rearrange("p (i c j) m -> p i c j m", i=2, c=2)
        self.sel = sb("sel", [ROWS, max(NCOMB), P], F32R)
        self.bgu = sb("bgu", [P, 2, nb])
        self.mult = sb("mult", [P, nb])
        self.gateT = sb("gateT", [P, max(LOGITS)])

        def ps(name, banks):
            return ctx.enter_context(nc.psum_tensor(name, [P, banks * 512], F32))

        self.banks = [ps(f"bank{i}", n) for i, n in enumerate((2, 2, 1, 1, 1, 1))]


def constants(nc, mem, dram, sem):
    loaded, bias_summed, bias_ready, zeroed, values_set = (
        sem[n] for n in ("const_loaded", "bias_summed", "bias_ready", "zeroed", "values_set"))

    BIAS_FIRST = 40

    def sync(sp):
        sp.dma_start(mem.rel[:], dram["rel_bias"]).then_inc(loaded, 16)
        sp.dma_start(mem.buckets[:], dram["buckets"]).then_inc(loaded, 16)
        sp.dma_start(mem.ident[:], dram["ident"]).then_inc(loaded, 16)
        sp.dma_start(mem.iota[:], dram["iota"]).then_inc(loaded, 16)

    def tensor(pe, part):
        pe.wait_ge(loaded, 64)
        keys = range(BIAS_FIRST) if part == 0 else range(BIAS_FIRST, S)
        for s in keys:
            for b in range(2):
                last = nc.tensor.matmul(mem.banks[0][b * S:(b + 1) * S, s * H:(s + 1) * H],
                                        mem.buckets[:, S - 1 - s:2 * S - 1 - s], mem.rel[:], start=True, stop=True)
        last.then_inc(bias_summed, 1)

    def scalar(act):
        act.wait_ge(bias_summed, 2)
        nc.scalar.copy(mem.bias[:].rearrange("p (h s) -> p h s", h=H),
                       mem.banks[0][:, :].rearrange("p (s h) -> p h s", h=H)).then_inc(bias_ready, 1)

    def gpsimd(pool):
        nc.gpsimd.memset(mem.minus_half[:], -0.5).then_inc(zeroed, 1)
        nc.gpsimd.memset(mem.kst[:].bitcast(F32), 0.0).then_inc(zeroed, 1)
        nc.gpsimd.memset(mem.qst[:].bitcast(F32), 0.0).then_inc(zeroed, 1)
        pool.wait_ge(zeroed, 1)

    def vector(dve):
        nc.vector.memset(mem.vst[:], 0.0).then_inc(values_set, 1)
        dve.wait_ge(values_set, 1)
        for h2 in range(2):
            nc.vector.memset(mem.vst[h2 * S:(h2 + 1) * S, :, :, 16 + 8 * h2:24 + 8 * h2], 1.0)\
                .then_inc(values_set, 1)
        dve.wait_ge(values_set, 3)

    return dict(sync=sync, tensor=tensor, scalar=scalar, gpsimd=gpsimd, vector=vector)


def attention(nc, sem, once, mem, dram, layer, x_dram, out_dram, x_ready, beside):
    BASE = layer * (AG // 2)
    w_loaded, w_scaled = sem("w_loaded"), sem("w_scaled")
    x_loaded, ctx_loaded, res_loaded, stored = ([sem(f"{n}{u}") for u in range(2)] for n in
                                                ("x_loaded", "ctx_loaded", "res_loaded", "stored"))
    k_spread = [sem(f"k_spread{u}") for u in range(2)]
    stack_ready, stacked, k_staged, q_placed = sem("stack_ready"), sem("stacked"), sem("k_staged"), sem("q_placed")
    stats, ln_scale, ln_chain, xn_ready = sem("stats"), sem("ln_scale"), sem("ln_chain"), sem("xn_ready")
    tr_done, xcT_ready = sem("tr_done"), sem("xcT_ready")
    qk_done, qk_hi, qk_lo = sem("qk_done"), sem("qk_hi"), sem("qk_lo")
    v_done, v_ready = sem("v_done"), sem("v_ready")
    scores_done, scores_read, max_ready, shifted = sem("scores_done"), sem("scores_read"), sem("max_ready"), sem("shifted")
    exp_done, shifted_beside = sem("exp_done"), sem("shifted_beside")
    pT_done, pT_ready, pv_done, o_ready = sem("pT_done"), sem("pT_ready"), sem("pv_done"), sem("o_ready")
    oT_back, rden_ready, normed, oT_done, oT_ready = sem("o_back"), sem("rden"), sem("normed"), sem("oT_done"), sem("oT_ready")
    y_done, res_biased, added = sem("y_done"), sem("res_biased"), sem("added")

    scores, pT_ps, o_ps, tp_v, qk_ps, tail = mem.banks
    WEIGHTS = (5, 5 + 8)[layer]
    xt = x_dram.rearrange("(g t p) d -> p g t d", t=AT, p=P)
    ct = dram["ctx"].rearrange("(g t p) d -> p g t d", t=AT, p=P)
    ot = out_dram.rearrange("(g t p) d -> p g t d", t=AT, p=P)

    def group_of(ap, turn):
        g = turn.times(1, -layer * AG)
        if isinstance(g, int):
            return ap[:, g, :, :]
        return ap[:, bass.ds(g, 1), :, :].rearrange("p a t d -> p (a t) d")

    def exists(turn):
        return not isinstance(turn.k, int) or 0 <= turn.times(1, -2 * BASE) < AG

    def run_steps(engine, step, name, part):
        if part == 0:
            step(Turn(BASE, 0) + -3)
            step(Turn(BASE, 0) + -2)
            beside(name, engine, -2)
            return
        for n in range(-1, 4):
            step(Turn(BASE, 0) + n)
            beside(name, engine, n)
        with engine.Fori(BASE + 2, BASE + AG // 2 - 2) as k:
            step(Turn(k, 0))
            step(Turn(k, 1))
        for n in range(AG - 4, AG + 2):
            step(Turn(BASE, 0) + n)
            beside(name, engine, n)

    def opening(turn):
        return layer == 0 and isinstance(turn.k, int) and turn.times(1) == 0

    def sync(sp, part):
        def load_x(h):
            at_least(sp, xn_ready, h.times(1, -1))
            stand_alone(sp, mem)
            sp.dma_start(mem.x[:, h.u], group_of(xt, h)).then_inc(x_loaded[h.u], 16)

        def load_ctx(h):
            at_least(sp, tr_done, h.times(1, -1))
            stand_alone(sp, mem)
            sp.dma_start(mem.ctx[:, h.u], group_of(ct, h)).then_inc(ctx_loaded[h.u], 16)

        def load_res(h):
            at_least(sp, added, h.times(1, -1))
            stand_alone(sp, mem)
            sp.dma_start(mem.xres[:, h.u], group_of(xt, h)).then_inc(res_loaded[h.u], 16)

        def spread_keys(h):
            if opening(h):
                sp.wait_ge(once["zeroed"], 2)
            at_least(sp, k_staged, h.times(2, 2))
            stand_alone(sp, mem)
            at_least(sp, scores_done, h.times(2 * AT, -2 * AT))
            stand_alone(sp, mem)
            for h4 in range(HQ):
                rows = slice(32 * h4, 32 * h4 + 32)
                sp.dma_start(mem.kst[rows, h.u, h4, :, :].bitcast(F32), mem.kstage[rows, :, :].bitcast(F32))\
                    .then_inc(k_spread[h.u], 16)

        def store(h):
            at_least(sp, added, h.times(1, 1))
            stand_alone(sp, mem)
            sp.dma_start(group_of(ot, h), mem.xnew[:, h.u]).then_inc(stored[h.u], 16)

        def load_weights():
            for n, t in (("wq", mem.wq), ("wk", mem.wk), ("wv", mem.wv), ("wo", mem.wo)):
                sp.dma_start(t[:], dram[f"{n}{layer}"]).then_inc(w_loaded, 16)
            if layer:
                sp.dma_start(mem.bqk[:], dram["bqk"]).then_inc(w_loaded, 16)
                sp.dma_start(mem.bv[:], dram["bv"].to_broadcast([P, D])).then_inc(w_loaded, 16)
                sp.dma_start(mem.bo[:], dram["bo"].to_broadcast([P, D])).then_inc(w_loaded, 16)
            sp.dma_start(mem.stage[:, 0:4 * HJ * P], dram["stack"]).then_inc(w_loaded, 16)

        if part == 0 and layer:
            for s, v in x_ready["first"]:
                sp.wait_ge(s, v)
        if part == 1 and layer:
            for s, v in x_ready["all"]:
                sp.wait_ge(s, v)

        def step(g):
            if exists(g + 3):
                load_x(g + 3)
                load_ctx(g + 3)
            if exists(g + 1):
                spread_keys(g + 1)
            if exists(g + -2):
                store(g + -2)
            if exists(g):
                load_res(g)
        run_steps(sp, step, "sync", part)
        if part == 0:
            load_weights()

    def tensor(pe, part):
        def transposes(h):
            at_least(pe, xn_ready, h.times(1, 1))
            at_least(pe, ctx_loaded[h.u], h.loads(1))
            at_least(pe, v_ready, h.times(1))
            for t in range(AT):
                nc.tensor.transpose(tp_v[:, t * P:(t + 1) * P], mem.xn[:, h.u, t, :], mem.ident[:])
            for t in range(AT):
                last = nc.tensor.transpose(tp_v[:, AN + t * P:AN + (t + 1) * P], mem.ctx[:, h.u, t, :], mem.ident[:])
            last.then_inc(tr_done, 1)

        def project_qk(h):
            at_least(pe, xcT_ready, h.times(1, 1))
            at_least(pe, q_placed, h.times(2))
            nc.tensor.matmul(qk_ps[:, 0:AN], mem.wq[:], mem.xcT[:, 0:AN], start=True, stop=True)
            nc.tensor.matmul(qk_ps[:, AN:2 * AN], mem.wk[:], mem.xcT[:, AN:2 * AN], start=True, stop=True)\
                .then_inc(qk_done, 1)

        def stack(h, n):
            if n == 0:
                at_least(pe, qk_hi, h.times(1, 1))
                at_least(pe, qk_lo, h.times(1, 1))
            elif n < 3:
                at_least(pe, k_staged, h.times(2, n))
            else:
                at_least(pe, q_placed, h.times(2, 1))
            i = 1 - n // 2
            for jj in range(2):
                out = qk_ps[:, jj * AN:(jj + 1) * AN]
                for part in range(2):
                    last = nc.tensor.matmul(out, mem.stack[:, i, part, 2 * (n % 2) + jj, :],
                                            mem.qk[:, part, i * AN:(i + 1) * AN], start=(part == 0), stop=(part == 1))
            last.then_inc(stacked, 1)

        def project_v(h):
            at_least(pe, xcT_ready, h.times(1, 1))
            for b in range(2 * AT):
                for h2 in range(2):
                    last = nc.tensor.matmul(tp_v[h2 * S:(h2 + 1) * S, b * 64:(b + 1) * 64],
                                            mem.xcT[:, AN + b * S:AN + (b + 1) * S],
                                            mem.wv[:, h2 * 64:(h2 + 1) * 64], start=True, stop=True)
            last.then_inc(v_done, 1)

        def score(g, t):
            if opening(g):
                pe.wait_ge(once["bias_ready"], 1)
            at_least(pe, q_placed, g.times(2, 2))
            at_least(pe, k_spread[g.u], g.loads(HQ))
            for half in range(2):
                at_least(pe, shifted if layer else scores_read, g.times(2 * AT, 2 * t - 1 + half - layer * AT * AG))
                for j in range(half * HJ // 2, (half + 1) * HJ // 2):
                    for b in range(2):
                        last = nc.tensor.matmul(scores[:, j * 256:(j + 1) * 256], mem.qst[:, g.u, j * AT + t, b, :],
                                                mem.kst[:, g.u, :, j, t * P + b * S:t * P + (b + 1) * S],
                                                start=(b == 0), stop=(b == 1))
                last.then_inc(scores_done, 1)

        def transpose_probs(g, t):
            at_least(pe, exp_done, g.times(AT, t + 1))
            for half in range(2):
                at_least(pe, pT_ready, g.times(2 * AT, 2 * t - 1 + half))
                for i in range(4):
                    hp = 4 * half + i
                    last = nc.tensor.transpose(pT_ps[:, hp * P:(hp + 1) * P],
                                               mem.probs[:, t, hp * P:(hp + 1) * P], mem.ident[:])
                last.then_inc(pT_done, 1)

        def values(g, t):
            at_least(pe, pT_ready, g.times(2 * AT, 2 * t + 2))
            at_least(pe, v_ready, g.times(1, 1))
            if t == 0:
                at_least(pe, o_ready, g.times(1))
            for hp in range(HP):
                col = t * 256 + (hp // 4) * P
                for b in range(2):
                    last = nc.tensor.matmul(o_ps[32 * (hp % 4):32 * (hp % 4) + 32, col + b * S:col + (b + 1) * S],
                                            mem.vst[:, g.u, (2 * t + b) * HP + hp, :],
                                            mem.probsT[:, hp // 4, (hp % 4) * P + b * S:(hp % 4) * P + (b + 1) * S],
                                            start=True, stop=True)
            last.then_inc(pv_done, 1)

        def back_o(g):
            at_least(pe, o_ready, g.times(1, 1))
            at_least(pe, added, g.times(1))
            for i in range(2 * AT):
                last = nc.tensor.transpose(tail[:, i * P:(i + 1) * P], mem.o_sb[:, i * P:(i + 1) * P], mem.ident[:])
            last.then_inc(oT_back, 1)

        def transpose_o(g):
            at_least(pe, normed, g.times(1, 1))
            for t in range(AT):
                last = nc.tensor.transpose(tail[:, t * P:(t + 1) * P], mem.onorm[:, t * P:(t + 1) * P], mem.ident[:])
            last.then_inc(oT_done, 1)

        def project_o(g):
            at_least(pe, oT_ready, g.times(1, 1))
            for t in range(AT):
                last = nc.tensor.matmul(tail[:, AN + t * P:AN + (t + 1) * P], mem.oT[:, t * P:(t + 1) * P],
                                        mem.wo[:], start=True, stop=True)
            last.then_inc(y_done, 1)

        if part:
            pe.wait_ge(w_loaded, 16 * WEIGHTS)
            pe.wait_ge(stack_ready, layer + 1)
            if layer:
                pe.wait_ge(w_scaled, 2)

        def step(g):
            if exists(g + 1):
                project_qk(g + 1)
            if exists(g):
                score(g, 0)
            if exists(g + -2):
                transpose_o(g + -2)
            if exists(g + -1):
                transpose_probs(g + -1, 1)
            if exists(g + 1):
                stack(g + 1, 0)
            if exists(g + -2):
                project_o(g + -2)
            if exists(g + 1):
                project_v(g + 1)
                stack(g + 1, 1)
            if exists(g + -1):
                values(g + -1, 1)
            if exists(g + 1):
                stack(g + 1, 2)
            if exists(g):
                score(g, 1)
            if exists(g):
                transpose_probs(g, 0)
            if exists(g + 1):
                stack(g + 1, 3)
            if exists(g + 2):
                transposes(g + 2)
            if exists(g + -1):
                back_o(g + -1)
            if exists(g):
                values(g, 0)
        run_steps(pe, step, "tensor", part)

    def scalar(act, part):
        def copy_xcT(h):
            at_least(act, tr_done, h.times(1, 1))
            at_least(act, v_done, h.times(1))
            nc.scalar.copy(mem.xcT[:], tp_v[:]).then_inc(xcT_ready, 1)

        def split_high(h):
            at_least(act, qk_done, h.times(1, 1))
            at_least(act, stacked, h.times(4))
            if layer:
                nc.scalar.activation(mem.qk[:, 0, 0:AN], qk_ps[:, 0:AN], ACT.Identity, bias=mem.bqk[:, 0:1])
                nc.scalar.activation(mem.qk[:, 0, AN:2 * AN], qk_ps[:, AN:2 * AN], ACT.Identity,
                                     bias=mem.bqk[:, 1:2]).then_inc(qk_hi, 1)
            else:
                nc.scalar.copy(mem.qk[:, 0, :], qk_ps[:]).then_inc(qk_hi, 1)

        def stage_keys(h, n):
            at_least(act, stacked, h.times(4, n + 1))
            p = h + -1
            if n == 0 and not (isinstance(p.k, int) and p.k < 0):
                at_least(act, k_spread[p.u], p.loads(HQ))
            nc.scalar.copy(mem.kstage[:, 2 * n:2 * n + 2, :].rearrange("p j t -> p (j t)"), qk_ps[:]).then_inc(k_staged, 1)

        def exponentials(g, t):
            if layer:
                at_least(act, shifted, g.times(2 * AT, 2 * t + 2 - AT * AG))
            else:
                at_least(act, shifted, g.times(AT, t + 1))
                at_least(act, shifted_beside, g.times(AT, t + 1))
            nc.scalar.activation(mem.probs[:, t, :], mem.probs[:, t, :], ACT.Exp).then_inc(exp_done, 1)

        def copy_pT(g, t):
            at_least(act, pv_done, g.times(AT, t))
            for half in range(2):
                at_least(act, pT_done, g.times(2 * AT, 2 * t + half + 1))
                nc.scalar.copy(mem.probsT[:, half, :], pT_ps[:, half * 512:(half + 1) * 512]).then_inc(pT_ready, 1)

        def copy_o(g):
            at_least(act, pv_done, g.times(AT, AT))
            at_least(act, oT_back, g.times(1))
            nc.scalar.copy(mem.o_sb[:], o_ps[:]).then_inc(o_ready, 1)

        def copy_oT(g):
            at_least(act, oT_done, g.times(1, 1))
            at_least(act, y_done, g.times(1))
            nc.scalar.copy(mem.oT[:], tail[:, 0:AN]).then_inc(oT_ready, 1)

        if part:
            act.wait_ge(w_loaded, 16 * WEIGHTS)
            nc.scalar.copy(mem.stack.rearrange("p i c j m -> p (i c j m)"), mem.stage[:, 0:4 * HJ * P])\
                .then_inc(stack_ready, 1)

        def place_queries(h, n):
            if opening(h):
                act.wait_ge(once["zeroed"], 3)
            at_least(act, stacked, h.times(4, 3 + n))
            at_least(act, scores_done, h.times(2 * AT, -2 * AT))
            src = qk_ps[:].rearrange("p (m b s) -> p m b s", b=2, s=S)
            for b in range(2):
                last = nc.scalar.copy(mem.qst[:, h.u, 2 * AT * n:2 * AT * (n + 1), b, b * S:(b + 1) * S],
                                      src[:, :, b, :])
            last.then_inc(q_placed, 1)

        def step(g):
            if exists(g + 1):
                split_high(g + 1)
            if exists(g + -2):
                copy_oT(g + -2)
            if exists(g + -1):
                copy_pT(g + -1, 1)
            if exists(g + 1):
                stage_keys(g + 1, 0)
                stage_keys(g + 1, 1)
            if exists(g):
                exponentials(g, 0)
            if exists(g + 1):
                place_queries(g + 1, 0)
            if exists(g + -1):
                copy_o(g + -1)
            if exists(g):
                copy_pT(g, 0)
            if exists(g + 1):
                place_queries(g + 1, 1)
            if exists(g + 2):
                copy_xcT(g + 2)
            if exists(g):
                exponentials(g, 1)
        run_steps(act, step, "scalar", part)

    def vector(dve, part):
        def layer_norm_stats(h):
            at_least(dve, x_loaded[h.u], h.loads(1))
            at_least(dve, xn_ready, h.times(1))
            for t in range(AT):
                last = nc.vector.bn_stats(mem.st[:, t, :], mem.x[:, h.u, t, :])
            last.then_inc(ln_chain, 1)
            dve.wait_ge(ln_chain, h.times(1, 1))
            stand_alone(dve, mem)
            for t in range(AT):
                last = nc.vector.bn_aggr(mem.mv[:, t, :], mem.st[:, t, :])
            last.then_inc(stats, 1)

        def split_low(h):
            at_least(dve, qk_hi, h.times(1, 1))
            hi = mem.qk[:, 0, :].bitcast(F32)
            if layer:
                for i in range(2):
                    part = slice(i * AN, (i + 1) * AN)
                    last = nc.vector.scalar_tensor_tensor(mem.qk[:, 1, part], qk_ps[:, part], mem.bqk[:, i:i + 1],
                                                          hi[:, part], ALU.add, ALU.subtract)
            else:
                last = nc.vector.tensor_tensor(mem.qk[:, 1, :], qk_ps[:], hi, ALU.subtract)
            last.then_inc(qk_lo, 1)

        def halves(tile, half):
            return tile.rearrange("p (k h s) -> p k h s", k=2, s=S)[:, half]

        def add_bias(g, t, half):
            if opening(g):
                dve.wait_ge(once["bias_ready"], 1)
            at_least(dve, scores_done, g.times(2 * AT, 2 * t + half + 1))
            at_least(dve, pT_done, g.times(2 * AT, 2 * t - 2))
            cols = slice(half * 512, (half + 1) * 512)
            nc.vector.tensor_tensor(mem.probs[:, t, cols], scores[:, cols], mem.bias[:, cols], ALU.add)\
                .then_inc(scores_read, 1)

        def row_max(g, t, half):
            n = g.times(2 * AT, 2 * t + half + 1)
            if layer:
                at_least(dve, scores_done, n)
                at_least(dve, pT_done, g.times(2 * AT, 2 * t - 2))
                raw = halves(scores[:, :], half)
            else:
                dve.wait_ge(scores_read, n)
                raw = halves(mem.probs[:, t, :], half)
            nc.vector.tensor_reduce(mem.rowmax[:, t, half * H // 2:(half + 1) * H // 2], raw, AX.X, ALU.max)\
                .then_inc(max_ready, 1)

        def shift(g, t, half):
            dve.wait_ge(max_ready, g.times(2 * AT, 2 * t + half + 1))
            top = mem.rowmax[:, t, half * H // 2:(half + 1) * H // 2]
            raw = halves(scores[:, :] if layer else mem.probs[:, t, :], half)
            nc.vector.tensor_tensor(halves(mem.probs[:, t, :], half), raw, top.unsqueeze(2).to_broadcast([P, H // 2, S]),
                                    ALU.subtract).then_inc(shifted if layer else shifted_beside, 1)

        def place_values(h):
            at_least(dve, v_done, h.times(1, 1))
            at_least(dve, pv_done, h.times(AT, -AT))
            for h2 in range(2):
                part = slice(h2 * S, (h2 + 1) * S)
                src = tp_v[part, 0:AN].rearrange("p (b n d) -> p b n d", b=2 * AT, n=HP)
                to = mem.vst[part, h.u, :, h2 * DH:(h2 + 1) * DH].rearrange("p (b n) d -> p b n d", b=2 * AT)
                if layer:
                    bias = mem.bv[part, h2 * 64:(h2 + 1) * 64].rearrange("p (n d) -> p n d", n=HP)
                    last = nc.vector.tensor_tensor(to, src, bias.unsqueeze(1).to_broadcast([S, 2 * AT, HP, DH]), ALU.add)
                else:
                    last = nc.vector.tensor_copy(to, src)
            last.then_inc(v_ready, 1)

        def divide(g):
            at_least(dve, oT_back, g.times(1, 1))
            back = tail[:, :].rearrange("p (n k h d) -> p n k h d", n=AT * HP, k=2, h=2)
            nc.vector.reciprocal(mem.rden[:], back[:, :, 1, :, 0]).then_inc(rden_ready, 1)
            dve.wait_ge(rden_ready, g.times(1, 1))
            at_least(dve, oT_done, g.times(1))
            nc.vector.tensor_tensor(mem.onorm[:].rearrange("p (n h d) -> p n h d", n=AT * HP, h=2),
                                    back[:, :, 0, :, :], mem.rden[:].unsqueeze(3).to_broadcast([P, AT * HP, 2, DH]),
                                    ALU.mult).then_inc(normed, 1)

        def add_residual(g):
            at_least(dve, y_done, g.times(1, 1))
            if layer:
                at_least(dve, res_biased, g.times(1, 1 - AG))
            else:
                at_least(dve, res_loaded[g.u], g.loads(1))
            p = g + -2
            if not (isinstance(p.k, int) and p.k < 0):
                at_least(dve, stored[p.u], p.loads(1))
            nc.vector.tensor_tensor(mem.xnew[:, g.u].rearrange("p t d -> p (t d)"), tail[:, AN:2 * AN],
                                    mem.xres[:, g.u].rearrange("p t d -> p (t d)"), ALU.add).then_inc(added, 1)

        if layer and part == 0:
            dve.wait_ge(w_loaded, 16 * WEIGHTS)
            nc.vector.tensor_scalar(mem.wq[:], mem.wq[:], float(DH) ** -0.5, None, ALU.mult).then_inc(w_scaled, 1)
            nc.vector.tensor_scalar(mem.bqk[:, 0:1], mem.bqk[:, 0:1], float(DH) ** -0.5, None, ALU.mult)\
                .then_inc(w_scaled, 1)
            dve.wait_ge(w_scaled, 2)
        def soften(g, t):
            for half in range(2):
                if not layer:
                    add_bias(g, t, half)
            for half in range(2):
                row_max(g, t, half)
            for half in range(2):
                if layer or half == 1:
                    shift(g, t, half)

        def step(g):
            if exists(g + 2):
                layer_norm_stats(g + 2)
            if exists(g + 1):
                split_low(g + 1)
            if exists(g):
                soften(g, 0)
            if exists(g + 1):
                place_values(g + 1)
            if exists(g + -2):
                add_residual(g + -2)
            if exists(g):
                soften(g, 1)
            if exists(g + -1):
                divide(g + -1)
        run_steps(dve, step, "vector", part)

    def gpsimd(pool, part):
        def ln_scales(h):
            at_least(pool, stats, h.times(1, 1))
            at_least(pool, xn_ready, h.times(1))
            stand_alone(pool, mem)
            nc.gpsimd.tensor_scalar(mem.veps[:, 0:AT], mem.mv[:, 0:AT, 1], EPS, None, ALU.add).then_inc(pool_chain, 1)
            pool.wait_ge(pool_chain, h.times(1, 1))
            nc.gpsimd.tensor_tensor(mem.rstd[:, 0:AT], mem.veps[:, 0:AT], mem.minus_half[:, 0:AT], ALU.pow)\
                .then_inc(ln_scale, 1)

        def normalise(h):
            at_least(pool, ln_scale, h.times(1, 1))
            stand_alone(pool, mem)
            at_least(pool, tr_done, h.times(1, -1))
            stand_alone(pool, mem)
            for t in range(AT):
                last = nc.gpsimd.tensor_scalar(mem.xn[:, h.u, t, :], mem.x[:, h.u, t, :], mem.mv[:, t, 0:1],
                                               mem.rstd[:, t:t + 1], ALU.subtract, ALU.mult)
            last.then_inc(xn_ready, 1)

        def shift(g, t, half):
            at_least(pool, max_ready, g.times(2 * AT, 2 * t + half + 1))
            part = mem.probs[:, t, half * 512:(half + 1) * 512].rearrange("p (h s) -> p h s", s=S)
            top = mem.rowmax[:, t, half * H // 2:(half + 1) * H // 2]
            nc.gpsimd.tensor_tensor(part, part, top.unsqueeze(2).to_broadcast([P, H // 2, S]), ALU.subtract)\
                .then_inc(shifted, 1)

        def bias_residual(g):
            at_least(pool, res_loaded[g.u], g.loads(1))
            nc.gpsimd.tensor_tensor(mem.xres[:, g.u], mem.xres[:, g.u],
                                    mem.bo[:].unsqueeze(1).to_broadcast([P, AT, D]), ALU.add).then_inc(res_biased, 1)

        pool_chain = gp_chain
        if layer and part == 0:
            pool.wait_ge(w_loaded, 16 * WEIGHTS)

        def step(g):
            if exists(g + 2):
                ln_scales(g + 2)
                normalise(g + 2)
            if exists(g + -1) and layer:
                bias_residual(g + -1)
            if exists(g) and not layer:
                shift(g, 0, 0)
                shift(g, 1, 0)
        run_steps(pool, step, "gpsimd", part)

    gp_chain = sem("pool_chain")
    done = {"all": [(stored[u], 16 * (BASE + AG // 2)) for u in range(2)],
            "first": [(stored[u], 16 * (BASE + 2)) for u in range(2)],
            "normalised": (xn_ready, 2 * BASE + AG)}
    return dict(sync=sync, tensor=tensor, scalar=scalar, vector=vector, gpsimd=gpsimd), done


def feed_forward(nc, ctx, mem, dram, layer, x_dram, out_dram, x_ready, beside):
    L = f"f{layer}_"

    def sem(name):
        return ctx.enter_context(nc.semaphore(L + name))

    def sb(name, shape, dt=F32):
        if name not in mem.ff:
            mem.ff[name] = mem.ctx_stack.enter_context(nc.sbuf_tensor("ff_" + name, shape, dt))
        return mem.ff[name]

    nb, ncomb, topk, nlog, nexp = NB[layer], NCOMB[layer], TOPK[layer], LOGITS[layer], EXPERTS[layer]
    act_fn = ACT.Silu if layer else ACT.Gelu
    biased = layer == 0

    w_staged, w_hi, w_lo, w_misc, w_mult, stage_scaled = (
        sem(n) for n in ("w_staged", "w_hi", "w_lo", "w_misc", "w_mult", "stage_scaled"))
    x_loaded, res_loaded, stored = ([sem(f"{n}{u}") for u in range(2)] for n in ("x_loaded", "res_loaded", "stored"))
    stats, ln_scale, ln_chain, pool_chain, xn_ready = (sem(n) for n in ("stats", "ln_scale", "ln_chain", "pool_chain", "xn_ready"))
    xT_done, xT_ready, x_hi, x_lo = (sem(n) for n in ("xT_done", "xT_ready", "x_hi", "x_lo"))
    logits_done, route, route_exp, route_gate = (sem(n) for n in ("logits_done", "route", "route_exp", "route_gate"))
    comb_ready, combT_done, combT_ready = (sem(n) for n in ("comb_ready", "combT_done", "combT_ready"))
    gate_done, up_done, comb_done, act_done = (sem(n) for n in ("gate_done", "up_done", "comb_done", "act_done"))
    hidden, hidden_scaled, h_hi, h_lo, down_done = (sem(n) for n in ("hidden", "hidden_scaled", "h_hi", "h_lo", "down_done"))
    y_ready, y_back, added = (sem(n) for n in ("y_ready", "y_back", "added"))

    x = sb("x", [P, 2, FT, D])
    xres = sb("xres", [P, 2, FT, D])
    xnew = sb("xnew", [P, 2, FT, D])
    xn = sb("xn", [P, FT, D])

    def xT_of(h):
        return mem.xcT if isinstance(h.k, int) and h.times(1) == 0 else mem.o_sb

    def router_bank(h):
        return y1 if isinstance(h.k, int) and h.times(1) == 0 else tail

    xTh = sb("xTh", [P, 2, FN], F32R)
    xTl = sb("xTl", [P, 2, FN], F32R)
    combT = sb("combT", [ROWS, 2, FN], F32R)
    activated = mem.probs[:, 0, :].rearrange("p (n t) -> p n t", n=2)
    hid = mem.probs[:, 1, :].rearrange("p (n t) -> p n t", n=2)
    product, yT = (mem.probsT[:, 0, :], mem.xcT[:]), mem.probsT[:, 1, :]
    hh_hl = [sb("hh", [P, 2, FN], F32R), sb("hl", [P, 2, FN], F32R)]
    hh, hl = ([hh_hl[i][:, 0], hh_hl[i][:, 1], mem.kstage[:, 2 * i:2 * i + 2, :].rearrange("p j t -> p (j t)")]
              for i in range(2))
    z17 = sb("z", [P, FT, 32])
    zmax = sb("zmax", [P, FT])
    pexp = sb("pexp", [P, FT, NE])
    psum = sb("psum_z", [P, FT])
    top = sb("top", [P, FT, 8])
    idx = sb("idx", [P, FT, 8], U32)
    idxf = sb("idxf", [P, FT, 8])
    wsum = sb("wsum", [P, FT])
    onehot = sb("onehot", [P, FT, 4, NE])
    comb = sb("comb", [P, FT, 32])
    comb_h = sb("comb_h", [P, FT, 32], F32R)
    comb2 = sb("comb2", [P, FT, ROWS])

    gu01, gu23, misc0, y0, y1, tail = mem.banks
    gate_ps = [gu01[:, 0:512], gu01[:, 512:1024]]
    up_ps = [gu23[:, 0:512], gu23[:, 512:1024]]
    comb_ps = misc0
    y_ps = [y0, y1]

    xt = x_dram.rearrange("(g t p) d -> p g t d", t=FT, p=P)
    ot = out_dram.rearrange("(g t p) d -> p g t d", t=FT, p=P)

    def group_of(ap, turn):
        g = turn.times(1)
        if isinstance(g, int):
            return ap[:, g, :, :]
        return ap[:, bass.ds(g, 1), :, :].rearrange("p a t d -> p (a t) d")

    def has_comb(b):
        return b < ncomb

    def two_ahead(g):
        return not (isinstance(g.k, int) and 2 * g.k + g.u + 2 >= FG)

    def slots(engine, per_slot):
        def step(g, first, last):
            for b in range(nb):
                per_slot(g, b, first, last)
        run_groups(engine, FG, step)

    def before(g, b, n):
        return (g, b - n) if b >= n else (g + -1, b - n + nb)

    def count(g, b, extra=0):
        return g.times(nb, b + extra)

    LAG = 3

    def buffer_free(engine, g, b):
        at_least(engine, down_done, count(g, b, 1 - (LAG if b >= nb % LAG else nb % LAG)))

    last_turn = Turn(FG // 2 - 1, 1)
    z = Turn(0, 0)
    SLOT_X, SLOT_LOGITS, SLOT_SHIFT, SLOT_EXP, SLOT_Y, SLOT_WEIGHTS, SLOT_COMB = 0, 1, 2, 3, 6, 5, min(nb - 1, 12)
    SLOT_STATS, SLOT_NORMALISE = ((3, 8), (12, 14))[nb > 12]
    ROUTE = ["largest", "shift", "sum_and_top", "inverse_and_places", "scale", "sum_of_top", "guard", "inverse_of_top",
             "weights", "put_weights", "gather", "gather_third", "high", "parts"]
    if topk == 2:
        ROUTE.remove("guard")
        ROUTE.remove("gather_third")
    STEPS = len(ROUTE) - 1
    SHIFTED = ROUTE.index("shift") + 1

    def sync(sp, at=None):
        def load(h):
            at_least(sp, xn_ready, h.times(1, -1))
            stand_alone(sp, mem)
            sp.dma_start(x[:, h.u], group_of(xt, h)).then_inc(x_loaded[h.u], 16)

        def load_res(h):
            at_least(sp, added, h.times(1, -1))
            stand_alone(sp, mem)
            sp.dma_start(xres[:, h.u], group_of(xt, h)).then_inc(res_loaded[h.u], 16)

        def store(h):
            at_least(sp, added, h.times(1, 1))
            stand_alone(sp, mem)
            sp.dma_start(group_of(ot, h), xnew[:, h.u]).then_inc(stored[h.u], 16)

        def load_weights(i):
            at_least(sp, w_hi, i)
            stand_alone(sp, mem)
            at_least(sp, w_lo, i)
            stand_alone(sp, mem)
            if i == 0:
                sp.dma_start(mem.gateT[:, 0:nlog], dram[f"gateT{layer}"]).then_inc(w_misc, 16)
                if biased:
                    sp.dma_start(mem.bgu[:], dram["bgu"]).then_inc(w_misc, 16)
                    sp.dma_start(mem.mult[:], dram["mult"]).then_inc(w_misc, 16)
            if i < 3:
                sp.dma_start(mem.stage[:, 0:nb * P], dram[f"{('wg', 'wu', 'wd')[i]}{layer}"]).then_inc(w_staged, 16)
            else:
                if biased:
                    sp.dma_start(mem.stage[0:ROWS, 0:D], dram["b2"]).then_inc(w_staged, 16)
                sp.dma_start(mem.stage[0:ROWS, D:D + ncomb * P], dram[f"sel{layer}"]).then_inc(w_staged, 16)

        if at is not None:
            if at == AG - 4:
                for s, v in x_ready["first"]:
                    sp.wait_ge(s, v)
                load(z)
                load(z + 1)
            if AG - 4 <= at < AG:
                load_weights(at - (AG - 4))
            return
        for s, v in x_ready["all"]:
            sp.wait_ge(s, v)

        def step(g, first, last):
            if last:
                beside("sync", sp)
            if two_ahead(g):
                load(g + 2)
            load_res(g)
            if not first:
                store(g + -1)
        run_groups(sp, FG, step)
        store(last_turn)


    def tensor(pe, at=None):
        def three(out, w, cols, hi, lo, start, stop):
            nc.tensor.matmul(out, w[0][:, cols, :], hi, start=start, stop=False)
            nc.tensor.matmul(out, w[0][:, cols, :], lo, start=False, stop=False)
            return nc.tensor.matmul(out, w[1][:, cols, :], hi, start=False, stop=stop)

        def gate_up(g, b):
            if b == 0:
                at_least(pe, x_hi, g.times(1, 1))
                at_least(pe, x_lo, g.times(1, 1))
            n = b % 2 if nb % 2 == 0 else (b + g.u) % 2
            at_least(pe, act_done, count(g, b, -1))
            three(gate_ps[n], mem.wg, b, xTh[:, g.u], xTl[:, g.u], True, True).then_inc(gate_done, 1)
            at_least(pe, hidden, count(g, b, -1))
            three(up_ps[n], mem.wu, b, xTh[:, g.u], xTl[:, g.u], True, True).then_inc(up_done, 1)

        def router_weights(g, b):
            if b == 0:
                at_least(pe, combT_ready, g.times(1, 1))
            at_least(pe, hidden, count(g, b))
            nc.tensor.matmul(comb_ps[:, :], mem.sel[:, b, :], combT[:, g.u], start=True, stop=True)\
                .then_inc(comb_done, 1)

        def down(g, b):
            n = b % LAG
            at_least(pe, h_hi, count(g, b, 1))
            at_least(pe, h_lo, count(g, b, 1))
            if b == 0:
                at_least(pe, y_ready, g.times(1, -1))
                if biased:
                    nc.tensor.matmul(y_ps[g.u][:, :], mem.b2[0][:], combT[:, g.u], start=True, stop=False)
                    nc.tensor.matmul(y_ps[g.u][:, :], mem.b2[1][:], combT[:, g.u], start=False, stop=False)
            three(y_ps[g.u][:, :], mem.wd, b, hh[n], hl[n], b == 0 and not biased, b == nb - 1)\
                .then_inc(down_done, 1)

        def back_y(g):
            at_least(pe, y_ready, g.times(1, 1))
            at_least(pe, route, g.times(STEPS, 2 * STEPS + SHIFTED))
            for t in range(FT):
                last = nc.tensor.transpose(tail[:, t * P:(t + 1) * P], yT[:, t * P:(t + 1) * P], mem.ident[:])
            last.then_inc(y_back, 1)

        def back_last_but_one(g):
            at_least(pe, y_ready, g.times(1, 1))
            for t in range(FT):
                last = nc.tensor.transpose(tail[:, t * P:(t + 1) * P], yT[:, t * P:(t + 1) * P], mem.ident[:])
            last.then_inc(y_back, 1)

        def transpose_x(h):
            bank = router_bank(h)
            at_least(pe, xn_ready, h.times(1, 1))
            at_least(pe, combT_ready, h.times(1))
            for t in range(FT):
                last = nc.tensor.transpose(bank[:, t * P:(t + 1) * P], xn[:, t, :], mem.ident[:])
            last.then_inc(xT_done, 1)

        def logits(h):
            bank = router_bank(h)
            at_least(pe, xT_ready, h.times(1, 1))
            for t in range(FT):
                last = nc.tensor.matmul(bank[:, t * 32:t * 32 + nlog], xT_of(h)[:, t * P:(t + 1) * P],
                                        mem.gateT[:, 0:nlog], start=True, stop=True)
            last.then_inc(logits_done, 1)

        def transpose_comb(h):
            at_least(pe, added, h.times(1, -1))
            at_least(pe, comb_ready, h.times(1, 1))
            stand_alone(pe, mem)
            bank = router_bank(h)
            for t in range(FT):
                last = nc.tensor.transpose(bank[0:ROWS, t * P:(t + 1) * P], comb2[:, t, :], mem.ident[:])
            last.then_inc(combT_done, 1)

        if at is not None:
            if at == AG - 1:
                transpose_x(z)
            if at == AG:
                pe.wait_ge(w_misc, 16 * (3 if biased else 1))
                logits(z)
            return
        transpose_comb(z)
        pe.wait_ge(w_hi, 4)
        pe.wait_ge(w_lo, 4)

        def slot(g, b, first, last):
            gate_up(g, b)
            if not (first and b < LAG):
                down(*before(g, b, LAG))
            if has_comb(b):
                router_weights(g, b)
            if b == SLOT_Y and not first:
                if last:
                    back_last_but_one(g + -1)
                else:
                    back_y(g + -1)
            if not last:
                if b == SLOT_X:
                    transpose_x(g + 1)
                if b == SLOT_LOGITS:
                    logits(g + 1)
                if b == SLOT_COMB:
                    transpose_comb(g + 1)
        slots(pe, slot)
        beside("tensor", pe)
        for n in range(LAG, 0, -1):
            down(last_turn, nb - n)
        at_least(pe, y_ready, last_turn.times(1, 1))
        at_least(pe, added, last_turn.times(1))
        for t in range(FT):
            last = nc.tensor.transpose(tail[:, t * P:(t + 1) * P], yT[:, t * P:(t + 1) * P], mem.ident[:])
        last.then_inc(y_back, 1)

    def scalar(act, at=None):
        def activate(g, b):
            n = (b + g.u) % 2
            at_least(act, gate_done, count(g, b, 1))
            at_least(act, hidden, count(g, b, -1))
            if biased:
                nc.scalar.activation(activated[:, n], gate_ps[n], act_fn, bias=mem.bgu[:, 0, b:b + 1])\
                    .then_inc(act_done, 1)
            else:
                nc.scalar.activation(activated[:, n], gate_ps[n], act_fn).then_inc(act_done, 1)

        def high(g, b):
            n = (b + g.u) % 2
            at_least(act, hidden, count(g, b, 1))
            buffer_free(act, g, b)
            nc.scalar.copy(hh[b % LAG], hid[:, n]).then_inc(h_hi, 1)

        def copy_y(g):
            at_least(act, down_done, g.times(nb, nb))
            at_least(act, y_back, g.times(1))
            nc.scalar.copy(yT, y_ps[g.u][:, :]).then_inc(y_ready, 1)

        def copy_xT(h):
            at_least(act, xT_done, h.times(1, 1))
            at_least(act, logits_done, h.times(1))
            at_least(act, x_lo, h.times(1))
            nc.scalar.copy(xT_of(h)[:], router_bank(h)[:, :]).then_inc(xT_ready, 1)

        def high_x(h):
            act.wait_ge(xT_ready, h.times(1, 1))
            at_least(act, up_done, h.times(nb, -nb))
            nc.scalar.copy(xTh[:, h.u], xT_of(h)[:]).then_inc(x_hi, 1)

        def route_exponentials(h):
            at_least(act, route, h.times(STEPS, SHIFTED))
            nc.scalar.activation(pexp[:, :, 0:nexp], z17[:, :, 0:nexp], ACT.Exp).then_inc(route_exp, 1)

        def shared_gate(h):
            at_least(act, route, h.times(STEPS, SHIFTED))
            nc.scalar.activation(comb[:, :, NE:NE + 1], z17[:, :, NE:NE + 1], ACT.Tanh, scale=0.5)\
                .then_inc(route_gate, 1)

        def copy_combT(h):
            at_least(act, combT_done, h.times(1, 1))
            at_least(act, down_done, h.times(nb, 1 - 2 * nb))
            at_least(act, comb_done, h.times(ncomb, -ncomb))
            nc.scalar.copy(combT[:, h.u], router_bank(h)[0:ROWS, :]).then_inc(combT_ready, 1)

        def high_weights(i):
            act.wait_ge(w_staged, 16 * (i + 1 + (i == 3 and biased)))
            if i == 2 and biased:
                act.wait_ge(stage_scaled, 1)
            if i < 3:
                w = (mem.wg, mem.wu, mem.wd)[i]
                nc.scalar.copy(w[0][:, 0:nb, :].rearrange("p b f -> p (b f)"), mem.stage[:, 0:nb * P]).then_inc(w_hi, 1)
                return
            if biased:
                nc.scalar.copy(mem.b2[0][:], mem.stage[0:ROWS, 0:D])
            nc.scalar.copy(mem.sel[:, 0:ncomb, :].rearrange("r b f -> r (b f)"), mem.stage[0:ROWS, D:D + ncomb * P])\
                .then_inc(w_hi, 1)

        if at is not None:
            if AG - 3 <= at <= AG:
                high_weights(at - (AG - 3))
            if at == AG - 1:
                copy_xT(z)
                high_x(z)
            if at == AG:
                route_exponentials(z)
                if layer:
                    shared_gate(z)
            return
        copy_combT(z)

        def slot(g, b, first, last):
            activate(g, b)
            if not (first and b == 0):
                high(*before(g, b, 1))
            if b == SLOT_Y - 1 and not first:
                copy_y(g + -1)
            if not last:
                if b == SLOT_X:
                    copy_xT(g + 1)
                if b == SLOT_X + 1:
                    high_x(g + 1)
                if b == SLOT_EXP:
                    route_exponentials(g + 1)
                if b == SLOT_EXP + 1 and layer:
                    shared_gate(g + 1)
                if b == SLOT_COMB:
                    copy_combT(g + 1)
        slots(act, slot)
        high(last_turn, nb - 1)
        beside("scalar", act)
        copy_y(last_turn)

    def vector(dve, at=None):
        def layer_norm_stats(h):
            if isinstance(h.k, int) and h.times(1) == 0:
                dve.wait_ge(*x_ready["normalised"])
            at_least(dve, x_loaded[h.u], h.loads(1))
            at_least(dve, ln_scale, h.times(1))
            for t in range(FT):
                last = nc.vector.bn_stats(mem.st[:, t, :], x[:, h.u, t, :])
            last.then_inc(ln_chain, 1)
            dve.wait_ge(ln_chain, h.times(1, 1))
            stand_alone(dve, mem)
            for t in range(FT):
                last = nc.vector.bn_aggr(mem.mv[:, t, :], mem.st[:, t, :])
            last.then_inc(stats, 1)

        def normalise(h):
            at_least(dve, ln_scale, h.times(1, 1))
            at_least(dve, xT_done, h.times(1))
            for t in range(FT):
                last = nc.vector.tensor_scalar(xn[:, t, :], x[:, h.u, t, :], mem.mv[:, t, 0:1],
                                               mem.rstd[:, t:t + 1], ALU.subtract, ALU.mult)
            last.then_inc(xn_ready, 1)

        def route_step(h, n):
            name = ROUTE[n]

            def rows(column, width):
                return column.to_broadcast([P, FT, width])

            if name == "largest":
                at_least(dve, logits_done, h.times(1, 1))
            if name == "shift":
                at_least(dve, route_exp, h.times(1))
            if name == "sum_and_top":
                at_least(dve, route_exp, h.times(1, 1))
            if name == "gather" and layer:
                at_least(dve, route_gate, h.times(1, 1))
            if name == "parts":
                at_least(dve, combT_done, h.times(1))
            at_least(dve, route, h.times(STEPS, n))
            stand_alone(dve, mem)

            raw = router_bank(h)[:, 0:FT * 32].rearrange("p (t e) -> p t e", t=FT)
            if name == "largest":
                last = nc.vector.tensor_reduce(zmax[:], raw[:, :, 0:nexp], AX.X, ALU.max)
            elif name == "shift":
                if layer:
                    nc.vector.tensor_copy(z17[:, :, NE:NE + 1], raw[:, :, NE:NE + 1])
                last = nc.vector.tensor_tensor(z17[:, :, 0:nexp], raw[:, :, 0:nexp], rows(zmax[:].unsqueeze(2), nexp),
                                               ALU.subtract)
            elif name == "sum_and_top":
                for t in range(FT):
                    nc.vector.max(top[:, t, :], pexp[:, t, :])
                last = nc.vector.tensor_reduce(psum[:], pexp[:, :, 0:nexp], AX.X, ALU.add)
            elif name == "inverse_and_places":
                for t in range(FT):
                    nc.vector.max_index(idx[:, t, :], top[:, t, :], pexp[:, t, :])
                last = nc.vector.reciprocal(psum[:], psum[:])
            elif name == "scale":
                nc.vector.tensor_copy(idxf[:], idx[:])
                last = nc.vector.tensor_tensor(top[:, :, 0:topk], top[:, :, 0:topk], rows(psum[:].unsqueeze(2), topk), ALU.mult)
            elif name == "sum_of_top":
                for k in range(topk):
                    nc.vector.tensor_tensor(onehot[:, :, k, :], mem.iota[:].unsqueeze(1).to_broadcast([P, FT, NE]),
                                            rows(idxf[:, :, k:k + 1], NE), ALU.is_equal)
                last = nc.vector.tensor_reduce(wsum[:], top[:, :, 0:topk], AX.X, ALU.add)
            elif name == "guard":
                last = nc.vector.tensor_scalar(wsum[:], wsum[:], 1e-20, None, ALU.add)
            elif name == "inverse_of_top":
                last = nc.vector.reciprocal(wsum[:], wsum[:])
            elif name == "weights":
                last = nc.vector.tensor_tensor(top[:, :, 0:topk], top[:, :, 0:topk], rows(wsum[:].unsqueeze(2), topk), ALU.mult)
            elif name == "put_weights":
                for k in range(topk):
                    last = nc.vector.tensor_tensor(onehot[:, :, k, :], onehot[:, :, k, :], rows(top[:, :, k:k + 1], NE),
                                                   ALU.mult)
            elif name == "gather":
                if layer:
                    nc.vector.tensor_scalar(comb[:, :, NE:NE + 1], comb[:, :, NE:NE + 1], 1.0, 0.5, ALU.add, ALU.mult)
                last = nc.vector.tensor_tensor(comb[:, :, 0:nexp], onehot[:, :, 0, 0:nexp], onehot[:, :, 1, 0:nexp], ALU.add)
            elif name == "gather_third":
                last = nc.vector.tensor_tensor(comb[:, :, 0:nexp], comb[:, :, 0:nexp], onehot[:, :, 2, 0:nexp], ALU.add)
            elif name == "high":
                last = nc.vector.tensor_copy(comb_h[:], comb[:])
            elif name == "parts":
                nc.vector.tensor_copy(comb2[:, :, 0:32], comb_h[:].bitcast(F32))
                nc.vector.tensor_tensor(comb2[:, :, 32:64], comb[:], comb_h[:].bitcast(F32), ALU.subtract)\
                    .then_inc(comb_ready, 1)
                return
            last.then_inc(route, 1)

        def multiply(g, b, last):
            n = (b + g.u) % 2
            at_least(dve, up_done, count(g, b, 1))
            at_least(dve, act_done, count(g, b, 1))
            at_least(dve, h_lo, count(g, b, -1))
            if has_comb(b):
                if biased:
                    nc.vector.scalar_tensor_tensor(product[n], up_ps[n], mem.bgu[:, 1, b:b + 1], activated[:, n],
                                                   ALU.add, ALU.mult).then_inc(hidden_scaled, 1)
                else:
                    nc.vector.tensor_tensor(product[n], up_ps[n], activated[:, n], ALU.mult)\
                        .then_inc(hidden_scaled, 1)
                if not last:
                    router_steps(g, b, 0)
                dve.wait_ge(hidden_scaled, g.times(ncomb, b + 1))
                at_least(dve, comb_done, g.times(ncomb, b + 1))
                nc.vector.tensor_tensor(hid[:, n], product[n], comb_ps[:, :], ALU.mult).then_inc(hidden, 1)
            else:
                nc.vector.scalar_tensor_tensor(hid[:, n], up_ps[n], mem.bgu[:, 1, b:b + 1], activated[:, n],
                                               ALU.add, ALU.mult).then_inc(hidden, 1)

        def router_steps(g, b, place):
            if b == SLOT_SHIFT:
                route_step(g + 1, place)
            n = 2 * (b - SLOT_WEIGHTS) + place
            if 0 <= n < len(ROUTE) - SHIFTED:
                route_step(g + 1, SHIFTED + n)

        def add_residual(g):
            at_least(dve, y_back, g.times(1, 1))
            at_least(dve, res_loaded[g.u], g.loads(1))
            p = g + -2
            if not (isinstance(p.k, int) and p.k < 0):
                at_least(dve, stored[p.u], p.loads(1))
            nc.vector.tensor_tensor(xnew[:, g.u].rearrange("p t d -> p (t d)"), tail[:, :],
                                    xres[:, g.u].rearrange("p t d -> p (t d)"), ALU.add).then_inc(added, 1)

        def constant_columns():
            nc.vector.memset(comb[:], 0.0).then_inc(w_mult, 1)
            nc.vector.memset(pexp[:], -1.0).then_inc(w_mult, 1)
            dve.wait_ge(w_mult, 2)
            if layer == 0:
                nc.vector.memset(comb[:, :, NE - 1:NE], 1.0).then_inc(w_mult, 1)
                dve.wait_ge(w_mult, 3)

        def low_weights(i):
            dve.wait_ge(w_staged, 16 * (i + 1 + (i == 3 and biased)))
            if i == 2 and biased:
                dve.wait_ge(w_misc, 16 * 3)
                staged = mem.stage[:, 0:nb * P].rearrange("p (b f) -> p b f", b=nb)
                nc.vector.tensor_tensor(staged, staged, mem.mult[:].unsqueeze(2).to_broadcast([P, nb, P]), ALU.mult)\
                    .then_inc(stage_scaled, 1)
            dve.wait_ge(w_hi, i + 1)
            if i < 3:
                w = (mem.wg, mem.wu, mem.wd)[i]
                nc.vector.tensor_tensor(w[1][:, 0:nb, :].rearrange("p b f -> p (b f)"), mem.stage[:, 0:nb * P],
                                        w[0].bitcast(F32)[:, 0:nb, :].rearrange("p b f -> p (b f)"), ALU.subtract)\
                    .then_inc(w_lo, 1)
            elif biased:
                nc.vector.tensor_tensor(mem.b2[1][:], mem.stage[0:ROWS, 0:D], mem.b2[0].bitcast(F32)[:], ALU.subtract)\
                    .then_inc(w_lo, 1)
            else:
                dve.sem_inc(w_lo, 1)

        if at is not None:
            if AG - 3 <= at <= AG:
                low_weights(at - (AG - 3))
            if at == AG - 3:
                layer_norm_stats(z)
                constant_columns()
            if at == AG - 2:
                normalise(z)
                layer_norm_stats(z + 1)
            if at == AG:
                for n in range(len(ROUTE)):
                    route_step(z, n)
            if at == AG + 1:
                normalise(z + 1)
            return

        def slot(g, b, first, last):
            multiply(g, b, last)
            if not last:
                router_steps(g, b, 1)
            if b == SLOT_Y and not first:
                add_residual(g + -1)
            if two_ahead(g):
                if b == SLOT_STATS:
                    layer_norm_stats(g + 2)
                if b == SLOT_NORMALISE:
                    normalise(g + 2)
            if last and b == nb - 2:
                beside("vector", dve)
        slots(dve, slot)
        add_residual(last_turn)

    def gpsimd(pool, at=None):
        def ln_scales(h):
            at_least(pool, stats, h.times(1, 1))
            at_least(pool, xn_ready, h.times(1))
            stand_alone(pool, mem)
            nc.gpsimd.tensor_scalar(mem.veps[:], mem.mv[:, :, 1], EPS, None, ALU.add).then_inc(pool_chain, 1)
            pool.wait_ge(pool_chain, h.times(1, 1))
            nc.gpsimd.tensor_tensor(mem.rstd[:], mem.veps[:], mem.minus_half[:], ALU.pow).then_inc(ln_scale, 1)

        def low_x(h):
            at_least(pool, x_hi, h.times(1, 1))
            nc.gpsimd.tensor_tensor(xTl[:, h.u], xT_of(h)[:], xTh.bitcast(F32)[:, h.u], ALU.subtract).then_inc(x_lo, 1)

        def low(g, b):
            n = (b + g.u) % 2
            at_least(pool, h_hi, count(g, b, 1))
            buffer_free(pool, g, b)
            nc.gpsimd.tensor_tensor(hl[b % LAG], hid[:, n], hh[b % LAG].bitcast(F32), ALU.subtract).then_inc(h_lo, 1)

        if at is not None:
            if at == AG - 3:
                ln_scales(z)
            if at == AG - 2:
                ln_scales(z + 1)
            if at == AG - 1:
                low_x(z)
            return

        def slot(g, b, first, last):
            low(g, b)
            if not last:
                if b == SLOT_X + 1:
                    low_x(g + 1)
            if b == SLOT_STATS and two_ahead(g):
                ln_scales(g + 2)
            if last and b == nb - 2:
                beside("gpsimd", pool)
        slots(pool, slot)

    done = {"all": [(stored[u], 16 * (FG // 2)) for u in range(2)], "first": [(stored[0], 16)]}
    return dict(sync=sync, tensor=tensor, scalar=scalar, vector=vector, gpsimd=gpsimd), done


def decoder_kernel(nc, dram, out):
    with ExitStack() as ctx:
        mem = Memory(nc, ctx)
        mem.ff, mem.ctx_stack = {}, ctx
        mem.tick = ctx.enter_context(nc.semaphore("tick"))
        once = {n: ctx.enter_context(nc.semaphore(n))
                for n in ("const_loaded", "bias_summed", "bias_ready", "zeroed", "values_set")}
        x1, x2, x3 = (dram[n] for n in ("x1", "x2", "x3"))
        setup = constants(nc, mem, dram, once)
        named = {}

        def shared(name):
            if name not in named:
                named[name] = ctx.enter_context(nc.semaphore("attn_" + name))
            return named[name]

        def beside_first(name, engine, n):
            if n == -2 and name == "tensor":
                setup[name](engine, 1)
            if n == -1 and name == "scalar":
                setup[name](engine)
            if n >= AG - 4:
                f0[name](engine, n)

        def beside_second(name, engine, n):
            if n >= AG - 4:
                f1[name](engine, n)

        def before_second(name, engine):
            a1[name](engine, 0)

        a0, x1_ready = attention(nc, shared, once, mem, dram, 0, dram["x"], x1, None, beside_first)
        f0, x2_ready = feed_forward(nc, ctx, mem, dram, 0, x1, x2, x1_ready, before_second)
        a1, x3_ready = attention(nc, shared, once, mem, dram, 1, x2, x3, x2_ready, beside_second)
        f1, out_ready = feed_forward(nc, ctx, mem, dram, 1, x3, out, x3_ready, lambda name, engine: None)
        block = ctx.enter_context(nc.Block())

        def phases(engine, name):
            if name == "tensor":
                setup[name](engine, 0)
            elif name != "scalar":
                setup[name](engine)
            a0[name](engine, 0)
            a0[name](engine, 1)
            f0[name](engine)
            a1[name](engine, 1)
            f1[name](engine)

        @block.sync
        def _(sp):
            phases(sp, "sync")
            for s, v in out_ready["all"]:
                sp.wait_ge(s, v)

        @block.tensor
        def _(pe):
            phases(pe, "tensor")

        @block.scalar
        def _(act):
            phases(act, "scalar")

        @block.vector
        def _(dve):
            phases(dve, "vector")

        @block.gpsimd
        def _(pool):
            phases(pool, "gpsimd")


def bucket_table():
    rel = S - 1 - np.arange(2 * S - 1)
    half, exact, far = NBUCKET // 2, NBUCKET // 4, 128
    dist = np.abs(rel)
    log = np.log((np.maximum(dist, 1) / exact).astype(np.float32)) / np.float32(math.log(far / exact))
    large = np.minimum(exact + (log * (half - exact)).astype(np.int32), half - 1)
    bucket = (rel > 0) * half + np.where(dist < exact, dist, large)
    return (np.arange(NBUCKET)[:, None] == bucket[None, :]).astype(np.float32)


def stacking():
    m = np.zeros((P, 2, 2, HJ, P), np.float32)
    for h4 in range(HQ):
        for c in range(NC):
            for d in range(DH):
                for j in range(HJ):
                    row, col = h4 * 32 + d * HJ + j, h4 * 32 + c * DH + d
                    m[row, 0, c % 2, j, col] = 1.0
                    m[row, 1, c // 2, j, col] = 1.0
    return m.reshape(P, -1)


def selection(layer):
    sel = np.zeros((ROWS, NCOMB[layer], P), np.float32)
    for b in range(NCOMB[layer]):
        for f in range(P):
            e = b if layer == 0 else (2 * b + f // 64 if b < 8 else NE)
            sel[e, b, f] = sel[32 + e, b, f] = 1.0
    return sel


def layout(inp):
    a = {k: np.asarray(v) for k, v in inp.items()}
    c = np.ascontiguousarray

    def qk_order(w):
        return c(w.reshape(-1, HJ, HQ, DH).transpose(0, 2, 3, 1).reshape(-1, D))

    def heads_last(w):
        return w.transpose(1, 0, 2).reshape(D, H * DH)

    def pairs_apart(w):
        return c(w.reshape(-1, HP, 2, DH).transpose(0, 2, 1, 3).reshape(-1, D))

    t = {"x": a["x"].reshape(TOK, D), "ctx": a["ctx_1024"].reshape(TOK, D)}
    t["wq0"], t["wk0"] = qk_order(a["L0_xattn_wq"]), qk_order(a["L0_xattn_wk"])
    t["wv0"], t["wo0"] = pairs_apart(a["L0_xattn_wv"]), a["L0_xattn_wo"]
    t["rel_bias"] = a["L0_xattn_rel_bias"]
    t["wq1"], t["wk1"] = qk_order(heads_last(a["L1_xattn_wq"])), qk_order(heads_last(a["L1_xattn_wk"]))
    t["wv1"], t["wo1"] = pairs_apart(heads_last(a["L1_xattn_wv"])), a["L1_xattn_wo"]
    t["bqk"] = np.stack([qk_order(a[n].reshape(1, D))[0] for n in ("L1_xattn_bq", "L1_xattn_bk")], 1)
    t["bv"], t["bo"] = pairs_apart(a["L1_xattn_bv"].reshape(1, D)), a["L1_xattn_bo"].reshape(1, D)
    F = 128
    fc1, sfc1 = a["L0_ffn_fc1_w"], a["L0_ffn_s_fc1_w"].reshape(2, 2, F, D)
    up = np.concatenate([fc1[:, :F], sfc1[0]])
    gate = np.concatenate([fc1[:, F:], sfc1[1]])
    t["wu0"], t["wg0"] = (w.transpose(2, 0, 1).reshape(D, -1) for w in (up, gate))
    down = np.concatenate([a["L0_ffn_fc2_w"], a["L0_ffn_s_fc2_w"].reshape(D, 2, F).transpose(1, 0, 2)])
    t["wd0"] = down.transpose(2, 0, 1).reshape(F, -1)
    b1, sb1 = a["L0_ffn_fc1_b"], a["L0_ffn_s_fc1_b"].reshape(2, 2, F)
    bias_gate, bias_up = np.concatenate([b1[:, F:], sb1[1]]), np.concatenate([b1[:, :F], sb1[0]])
    t["bgu"] = np.stack([bias_gate.T, bias_up.T], 1)
    t["mult"] = np.concatenate([a["L0_ffn_geglu_mult"], a["L0_ffn_s_geglu_mult"].reshape(2, F)]).T
    b2 = np.zeros((2, 32, D), np.float32)
    b2[:, :15], b2[:, 15] = a["L0_ffn_fc2_b"], a["L0_ffn_s_fc2_b"]
    t["b2"] = b2.reshape(ROWS, D)
    t["gateT0"] = a["L0_ffn_gate_w"].T
    gu = a["L1_ffn_w_gate_up"].reshape(8, 2, D, 2, 64).transpose(3, 2, 0, 1, 4).reshape(2, D, 8 * P)
    def filled(w):
        return np.concatenate([w, np.zeros((3 * P - w.shape[0], D), np.float32)])
    t["wg1"] = np.concatenate([gu[0], filled(a["L1_ffn_shared_w_gate"]).T], 1)
    t["wu1"] = np.concatenate([gu[1], filled(a["L1_ffn_shared_w_up"]).T], 1)
    d1 = a["L1_ffn_w_down"].reshape(8, P, D).transpose(1, 0, 2).reshape(P, -1)
    sd = filled(a["L1_ffn_shared_w_down"].T).reshape(3, P, D).transpose(1, 0, 2).reshape(P, -1)
    t["wd1"] = np.concatenate([d1, sd], 1)
    t["gateT1"] = np.concatenate([a["L1_ffn_gate_w"], a["L1_ffn_shared_gate_w"]]).T
    t["ident"] = np.eye(P, dtype=np.float32)
    t["iota"] = np.tile(np.arange(NE, dtype=np.float32), (P, 1))
    t["buckets"] = bucket_table()
    t["stack"] = stacking()
    t["sel0"], t["sel1"] = selection(0).reshape(ROWS, -1), selection(1).reshape(ROWS, -1)
    return {k: c(v) for k, v in t.items()}


def kernel(**inputs):
    import concourse.bacc as bacc
    from concourse.bass_utils import run_bass_kernel_spmd

    nc = bacc.Bacc("TRN2", target_bir_lowering=False, num_devices=1)
    arrays, dram = {}, {}
    for name, a in layout(inputs).items():
        arrays[f"in_{name}"] = a
        dram[name] = nc.dram_tensor(f"in_{name}", a.shape, mybir.dt.from_np(a.dtype), kind="ExternalInput").ap()
    for name, shape in (("x1", (TOK, D)), ("x2", (TOK, D)), ("x3", (TOK, D))):
        dram[name] = nc.dram_tensor(name, shape, F32, kind="Internal").ap()
    out = nc.dram_tensor("out", (TOK, D), F32, kind="ExternalOutput").ap()
    decoder_kernel(nc, dram, out)
    result = run_bass_kernel_spmd(nc, [arrays], core_ids=[0])
    return result.results[0]["out"].reshape(B, S, D)
```
